# Optimizing a Trainium2 kernel written in Bass

```python
import numpy as np
import jax
import jax.numpy as jnp

def _softmax(x, axis=-1):
    return jax.nn.softmax(x, axis=axis)

def _gelu(x):
    return jax.nn.gelu(x, approximate=True)

def _silu(x):
    return jax.nn.silu(x)

def _sigmoid(x):
    return jax.nn.sigmoid(x)

def _layernorm(x, axis=-1, eps=1e-05):
    m = jnp.mean(x, axis=axis, keepdims=True)
    v = jnp.var(x, axis=axis, keepdims=True)
    return (x - m) / jnp.sqrt(v + eps)

def _scatter_add(tgt, idx, src, axis=0):
    return tgt.at[idx].add(src)

def _segment_sum(src, seg, n):
    return jax.ops.segment_sum(src, seg, n)
kernel_name = 'mk_adaln_d2_jaxref_r8_6b6791'

def setup_inputs(seed: int=0):
    np.random.seed(seed)
    _w = jnp.asarray

    def _L0_attn_setup():
        import jax, jax.numpy as jnp
        import numpy as np
        import math
        B, T, E = (2, 256, 256)
        G, QPG, D = (4, 4, 128)

        def sinusoidal_pe(t, d, dtype):
            pos = jnp.arange(t, dtype=jnp.float32)[:, None]
            i = jnp.arange(0, d, 2, dtype=jnp.float32)
            inv_freq = jnp.exp(-(jnp.log(10000.0) * i / d))
            ang = pos * inv_freq
            pe = jnp.zeros((t, d), dtype=jnp.float32)
            pe = pe.at[:, 0::2].set(jnp.sin(ang)).at[:, 1::2].set(jnp.cos(ang))
            return pe.astype(dtype)
        key = jax.random.key(seed)
        ks = jax.random.split(key, 6)
        s = lambda fan_in: 1.0 / math.sqrt(fan_in)
        return {'x': jax.random.normal(ks[0], (B, T, E), dtype=jnp.float32), 'wq': jax.random.uniform(ks[1], (E, G * QPG * D), jnp.float32, -s(E), s(E)), 'bq': jax.random.uniform(ks[2], (G * QPG * D,), jnp.float32, -s(E), s(E)), 'wkv': jax.random.uniform(ks[3], (E, 2 * G * D), jnp.float32, -s(E), s(E)), 'bkv': jax.random.uniform(ks[4], (2 * G * D,), jnp.float32, -s(E), s(E)), 'wo': jax.random.uniform(ks[5], (G * QPG * D, E), jnp.float32, -s(G * QPG * D), s(G * QPG * D))}
    _L0_attn_in = _L0_attn_setup()

    def _L0_ffn_setup():
        import jax, jax.numpy as jnp
        import numpy as np
        H = 256
        I = 128
        K = 8
        E = 128
        TOPK = 4
        EPS = 1e-08
        key = jax.random.key(seed)
        ks = jax.random.split(key, 10)
        s = 0.02
        return {'x': jax.random.normal(ks[0], (4, 256, H), jnp.float32), 'w_router': jax.random.normal(ks[1], (H, E), jnp.float32) * s, 'w_gate': jax.random.normal(ks[2], (H, K * I), jnp.float32) * s, 'w_up': jax.random.normal(ks[3], (H, K * I), jnp.float32) * s, 'w_down': jax.random.normal(ks[4], (I, H), jnp.float32) * s, 'amplitudes': jax.random.normal(ks[5], (E, K, 2), jnp.float32) * 0.1, 'expert_scale': jnp.ones((E,), jnp.float32), 'shared_w_gate': jax.random.normal(ks[6], (H, 2 * I), jnp.float32) * s, 'shared_w_up': jax.random.normal(ks[7], (H, 2 * I), jnp.float32) * s, 'shared_w_down': jax.random.normal(ks[8], (2 * I, H), jnp.float32) * s}
    _L0_ffn_in = _L0_ffn_setup()
    _L0_c = _w((lambda *s: np.random.randn(*s).astype(np.float32) * 0.05)(1, 256))
    _L0_wmod = _w((lambda *s: np.random.randn(*s).astype(np.float32) * 0.05)(256, 6 * 256) * 256 ** (-0.5))

    def _L1_attn_setup():
        import jax, jax.numpy as jnp
        import numpy as np
        N_EMBD = 256
        N_HEADS = 16
        HEAD_DIM = N_EMBD // N_HEADS
        THETA = 10000.0

        def _rope_tables(seq_len, head_dim):
            inv = 1.0 / THETA ** (jnp.arange(0, head_dim, 2, dtype=jnp.float32) / head_dim)
            pos = jnp.arange(seq_len, dtype=jnp.float32)
            freqs = jnp.outer(pos, inv)
            return (jnp.cos(freqs)[None, :, None, :], jnp.sin(freqs)[None, :, None, :])

        def _apply_rope(t, cos, sin):
            B, S, H, D = t.shape
            tr = t.reshape(B, S, H, D // 2, 2)
            x0, x1 = (tr[..., 0], tr[..., 1])
            r0 = x0 * cos - x1 * sin
            r1 = x0 * sin + x1 * cos
            return jnp.stack([r0, r1], axis=-1).reshape(B, S, H, D)
        key = jax.random.key(seed)
        ks = jax.random.split(key, 9)
        B, S, E = (4, 256, N_EMBD)
        scale = 1.0 / np.sqrt(E)
        inp = {'x': jax.random.normal(ks[0], (B, S, E), dtype=jnp.float32), 'Wq': jax.random.normal(ks[1], (E, E), dtype=jnp.float32) * scale, 'bq': jnp.zeros((E,), dtype=jnp.float32), 'Wk': jax.random.normal(ks[2], (E, E), dtype=jnp.float32) * scale, 'bk': jnp.zeros((E,), dtype=jnp.float32), 'Wv': jax.random.normal(ks[3], (E, E), dtype=jnp.float32) * scale, 'bv': jnp.zeros((E,), dtype=jnp.float32), 'Wo': jax.random.normal(ks[4], (E, E), dtype=jnp.float32) * scale, 'bo': jnp.zeros((E,), dtype=jnp.float32)}
        return inp
    _L1_attn_in = _L1_attn_setup()

    def _L1_ffn_setup():
        import jax, jax.numpy as jnp
        import numpy as np
        B, S, DIM = (2, 256, 256)
        INTER = 176
        E = 8
        K = 2
        SHARED = 1
        ROUTE_SCALE = 1.0

        def _expert(xt, w1, w2, w3, cw=None):
            h = jax.nn.silu((xt @ w1.T).astype(jnp.float32)) * (xt @ w3.T).astype(jnp.float32)
            if cw is not None:
                h = cw[:, None] * h
            return h.astype(xt.dtype) @ w2.T
        key = jax.random.key(seed)
        ks = jax.random.split(key, 9)
        bf = lambda k, shape: (jax.random.normal(k, shape, dtype=jnp.float32) * 0.02).astype(jnp.bfloat16)
        return {'x': jax.random.normal(ks[0], (B, S, DIM), dtype=jnp.float32).astype(jnp.bfloat16), 'gate_w': jax.random.normal(ks[1], (E, DIM), dtype=jnp.float32) * 0.02, 'gate_b': jax.random.normal(ks[2], (E,), dtype=jnp.float32) * 0.01, 'w1': bf(ks[3], (E, INTER, DIM)), 'w2': bf(ks[4], (E, DIM, INTER)), 'w3': bf(ks[5], (E, INTER, DIM)), 'sw1': bf(ks[6], (SHARED * INTER, DIM)), 'sw2': bf(ks[7], (DIM, SHARED * INTER)), 'sw3': bf(ks[8], (SHARED * INTER, DIM))}
    _L1_ffn_in = _L1_ffn_setup()
    _L1_c = _w((lambda *s: np.random.randn(*s).astype(np.float32) * 0.05)(1, 256))
    _L1_wmod = _w((lambda *s: np.random.randn(*s).astype(np.float32) * 0.05)(256, 6 * 256) * 256 ** (-0.5))
    _d = {'L0_attn_x': _L0_attn_in['x'], 'L0_attn_wq': _L0_attn_in['wq'], 'L0_attn_bq': _L0_attn_in['bq'], 'L0_attn_wkv': _L0_attn_in['wkv'], 'L0_attn_bkv': _L0_attn_in['bkv'], 'L0_attn_wo': _L0_attn_in['wo'], 'L0_ffn_w_router': _L0_ffn_in['w_router'], 'L0_ffn_w_gate': _L0_ffn_in['w_gate'], 'L0_ffn_w_up': _L0_ffn_in['w_up'], 'L0_ffn_w_down': _L0_ffn_in['w_down'], 'L0_ffn_amplitudes': _L0_ffn_in['amplitudes'], 'L0_ffn_expert_scale': _L0_ffn_in['expert_scale'], 'L0_ffn_shared_w_gate': _L0_ffn_in['shared_w_gate'], 'L0_ffn_shared_w_up': _L0_ffn_in['shared_w_up'], 'L0_ffn_shared_w_down': _L0_ffn_in['shared_w_down'], 'L0_c': _L0_c, 'L0_wmod': _L0_wmod, 'L1_attn_Wq': _L1_attn_in['Wq'], 'L1_attn_bq': _L1_attn_in['bq'], 'L1_attn_Wk': _L1_attn_in['Wk'], 'L1_attn_bk': _L1_attn_in['bk'], 'L1_attn_Wv': _L1_attn_in['Wv'], 'L1_attn_bv': _L1_attn_in['bv'], 'L1_attn_Wo': _L1_attn_in['Wo'], 'L1_attn_bo': _L1_attn_in['bo'], 'L1_ffn_gate_w': _L1_ffn_in['gate_w'], 'L1_ffn_gate_b': _L1_ffn_in['gate_b'], 'L1_ffn_w1': _L1_ffn_in['w1'], 'L1_ffn_w2': _L1_ffn_in['w2'], 'L1_ffn_w3': _L1_ffn_in['w3'], 'L1_ffn_sw1': _L1_ffn_in['sw1'], 'L1_ffn_sw2': _L1_ffn_in['sw2'], 'L1_ffn_sw3': _L1_ffn_in['sw3'], 'L1_c': _L1_c, 'L1_wmod': _L1_wmod}
    _x0 = _d['L0_attn_x']
    _d['L0_attn_x'] = jax.random.normal(jax.random.fold_in(jax.random.key(seed), 1), (1, 1024, 256), dtype=_x0.dtype)
    del _x0
    return _d

def reference(L0_attn_x, L0_attn_wq, L0_attn_bq, L0_attn_wkv, L0_attn_bkv, L0_attn_wo, L0_ffn_w_router, L0_ffn_w_gate, L0_ffn_w_up, L0_ffn_w_down, L0_ffn_amplitudes, L0_ffn_expert_scale, L0_ffn_shared_w_gate, L0_ffn_shared_w_up, L0_ffn_shared_w_down, L0_c, L0_wmod, L1_attn_Wq, L1_attn_bq, L1_attn_Wk, L1_attn_bk, L1_attn_Wv, L1_attn_bv, L1_attn_Wo, L1_attn_bo, L1_ffn_gate_w, L1_ffn_gate_b, L1_ffn_w1, L1_ffn_w2, L1_ffn_w3, L1_ffn_sw1, L1_ffn_sw2, L1_ffn_sw3, L1_c, L1_wmod):

    def _L0_attn_ref(x, wq, bq, wkv, bkv, wo):
        import jax, jax.numpy as jnp
        import numpy as np
        import math
        B, T, E = (2, 256, 256)
        G, QPG, D = (4, 4, 128)

        def sinusoidal_pe(t, d, dtype):
            pos = jnp.arange(t, dtype=jnp.float32)[:, None]
            i = jnp.arange(0, d, 2, dtype=jnp.float32)
            inv_freq = jnp.exp(-(jnp.log(10000.0) * i / d))
            ang = pos * inv_freq
            pe = jnp.zeros((t, d), dtype=jnp.float32)
            pe = pe.at[:, 0::2].set(jnp.sin(ang)).at[:, 1::2].set(jnp.cos(ang))
            return pe.astype(dtype)
        b, t, e = x.shape
        q = (x @ wq + bq).reshape(b, t, G, QPG, D).transpose(0, 2, 3, 1, 4)
        kv = (x @ wkv + bkv).reshape(b, t, G, 1, 2 * D).transpose(0, 2, 3, 1, 4)
        k, v = (kv[..., :D], kv[..., D:])
        pe = sinusoidal_pe(t, D, x.dtype)
        q = q + pe
        k = k + pe
        scores = jnp.einsum('bgqtd,bgksd->bgqts', q, k) / math.sqrt(D)
        causal = jnp.tril(jnp.ones((t, t), dtype=bool))
        scores = jnp.where(causal, scores, -jnp.inf)
        probs = jax.nn.softmax(scores, axis=-1)
        out = jnp.einsum('bgqts,bgksd->btgqd', probs, v).reshape(b, t, G * QPG * D)
        return out @ wo

    def _L0_ffn_ref(x, w_router, w_gate, w_up, w_down, amplitudes, expert_scale, shared_w_gate, shared_w_up, shared_w_down):
        import jax, jax.numpy as jnp
        import numpy as np
        H = 256
        I = 128
        K = 8
        E = 128
        TOPK = 4
        EPS = 1e-08
        B, S, _ = x.shape
        T = B * S
        xt = x.reshape(T, H)
        probs = jax.nn.softmax(xt @ w_router, axis=-1)
        topk_p, topk_idx = jax.lax.top_k(probs, TOPK)
        topk_w = topk_p / (jnp.sum(topk_p, axis=-1, keepdims=True) + EPS)
        gate = (xt @ w_gate).reshape(T, K, I)
        up = (xt @ w_up).reshape(T, K, I)
        basis = jax.nn.silu(gate) * up
        p = amplitudes[..., 0] ** 2 + amplitudes[..., 1] ** 2
        mix = p / (jnp.sum(p, axis=-1, keepdims=True) + EPS)
        mix_sel = mix[topk_idx]
        mixed = jnp.einsum('tek,tki->tei', mix_sel, basis)
        down = jnp.einsum('tei,ih->teh', mixed, w_down)
        coeff = topk_w * expert_scale[topk_idx]
        out = jnp.einsum('teh,te->th', down, coeff)
        shared = jax.nn.silu(xt @ shared_w_gate) * (xt @ shared_w_up) @ shared_w_down
        out = out + shared
        return out.reshape(B, S, H)

    def _L1_attn_ref(x, Wq, bq, Wk, bk, Wv, bv, Wo, bo):
        import jax, jax.numpy as jnp
        import numpy as np
        N_EMBD = 256
        N_HEADS = 16
        HEAD_DIM = N_EMBD // N_HEADS
        THETA = 10000.0

        def _rope_tables(seq_len, head_dim):
            inv = 1.0 / THETA ** (jnp.arange(0, head_dim, 2, dtype=jnp.float32) / head_dim)
            pos = jnp.arange(seq_len, dtype=jnp.float32)
            freqs = jnp.outer(pos, inv)
            return (jnp.cos(freqs)[None, :, None, :], jnp.sin(freqs)[None, :, None, :])

        def _apply_rope(t, cos, sin):
            B, S, H, D = t.shape
            tr = t.reshape(B, S, H, D // 2, 2)
            x0, x1 = (tr[..., 0], tr[..., 1])
            r0 = x0 * cos - x1 * sin
            r1 = x0 * sin + x1 * cos
            return jnp.stack([r0, r1], axis=-1).reshape(B, S, H, D)
        B, S, E = x.shape
        H, D = (N_HEADS, HEAD_DIM)
        q = (x @ Wq.T + bq).reshape(B, S, H, D)
        k = (x @ Wk.T + bk).reshape(B, S, H, D)
        v = (x @ Wv.T + bv).reshape(B, S, H, D)
        cos, sin = _rope_tables(S, D)
        q = _apply_rope(q, cos, sin)
        k = _apply_rope(k, cos, sin)
        qk = jnp.einsum('bshd,bstd->bsht', q, k) / jnp.sqrt(jnp.float32(D))
        att = jax.nn.softmax(qk, axis=-1)
        out = jnp.einsum('bsht,bstd->bshd', att, v)
        out = jnp.swapaxes(out, 1, 2).reshape(B, S, E)
        return out @ Wo.T + bo

    def _L1_ffn_ref(x, gate_w, gate_b, w1, w2, w3, sw1, sw2, sw3):
        import jax, jax.numpy as jnp
        import numpy as np
        B, S, DIM = (2, 256, 256)
        INTER = 176
        E = 8
        K = 2
        SHARED = 1
        ROUTE_SCALE = 1.0

        def _expert(xt, w1, w2, w3, cw=None):
            h = jax.nn.silu((xt @ w1.T).astype(jnp.float32)) * (xt @ w3.T).astype(jnp.float32)
            if cw is not None:
                h = cw[:, None] * h
            return h.astype(xt.dtype) @ w2.T
        Bx, Sx, D = x.shape
        xt = x.reshape(-1, D)
        T = xt.shape[0]
        scores = xt.astype(jnp.float32) @ gate_w.T
        scores = jnp.sqrt(jax.nn.softplus(scores))
        biased = scores + gate_b
        _, idx = jax.lax.top_k(biased, K)
        weights = jnp.take_along_axis(scores, idx, axis=1) * ROUTE_SCALE
        cw = jnp.einsum('tk,tke->te', weights, jax.nn.one_hot(idx, E, dtype=jnp.float32))
        y = jnp.zeros((T, D), dtype=xt.dtype)
        for e in range(E):
            y = y + _expert(xt, w1[e], w2[e], w3[e], cw[:, e])
        z = _expert(xt, sw1, sw2, sw3)
        return (y + z).reshape(Bx, Sx, D)
    x = L0_attn_x
    mod = (_silu(L0_c) @ L0_wmod).reshape(L0_c.shape[0], 6, 1, -1)
    sa, ca, ga, sb, cb, gb = (mod[:, 0], mod[:, 1], mod[:, 2], mod[:, 3], mod[:, 4], mod[:, 5])
    ga = (2 * (ga >= 0) - 1) * jnp.maximum(jnp.abs(ga), 0.25)
    gb = (2 * (gb >= 0) - 1) * jnp.maximum(jnp.abs(gb), 0.25)
    h = _layernorm(x, axis=-1) * (1 + ca) + sa
    x = x + ga * _L0_attn_ref(h, L0_attn_wq, L0_attn_bq, L0_attn_wkv, L0_attn_bkv, L0_attn_wo)
    h = _layernorm(x, axis=-1) * (1 + cb) + sb
    x = x + gb * _L0_ffn_ref(h, L0_ffn_w_router, L0_ffn_w_gate, L0_ffn_w_up, L0_ffn_w_down, L0_ffn_amplitudes, L0_ffn_expert_scale, L0_ffn_shared_w_gate, L0_ffn_shared_w_up, L0_ffn_shared_w_down)
    mod = (_silu(L1_c) @ L1_wmod).reshape(L1_c.shape[0], 6, 1, -1)
    sa, ca, ga, sb, cb, gb = (mod[:, 0], mod[:, 1], mod[:, 2], mod[:, 3], mod[:, 4], mod[:, 5])
    ga = (2 * (ga >= 0) - 1) * jnp.maximum(jnp.abs(ga), 0.25)
    gb = (2 * (gb >= 0) - 1) * jnp.maximum(jnp.abs(gb), 0.25)
    h = _layernorm(x, axis=-1) * (1 + ca) + sa
    x = x + ga * _L1_attn_ref(h, L1_attn_Wq, L1_attn_bq, L1_attn_Wk, L1_attn_bk, L1_attn_Wv, L1_attn_bv, L1_attn_Wo, L1_attn_bo)
    h = _layernorm(x, axis=-1) * (1 + cb) + sb
    x = x + gb * _L1_ffn_ref(h, L1_ffn_gate_w, L1_ffn_gate_b, L1_ffn_w1, L1_ffn_w2, L1_ffn_w3, L1_ffn_sw1, L1_ffn_sw2, L1_ffn_sw3)
    return x

_drawn_inputs = setup_inputs


def setup_inputs(seed=0):
    import zlib

    import numpy as np

    out = dict(_drawn_inputs(seed))
    spreads = {'L0_ffn_expert_scale': (1.0, 0.6),
     'L1_attn_bq': (0.0, 0.8),
     'L1_attn_bk': (0.0, 0.8),
     'L1_attn_bv': (0.0, 0.696),
     'L1_attn_bo': (0.0, 0.333)}
    factors = {'L0_attn_wq': 8.0,
     'L0_attn_bq': 8.0,
     'L0_attn_wkv': 4.619,
     'L0_attn_bkv': 8.0,
     'L0_attn_wo': 4.227,
     'L0_ffn_w_router': 8.0,
     'L0_ffn_w_gate': 8.0,
     'L0_ffn_w_up': 8.0,
     'L0_ffn_w_down': 8.0,
     'L0_ffn_amplitudes': 8.0,
     'L0_ffn_shared_w_gate': 8.0,
     'L0_ffn_shared_w_up': 8.0,
     'L0_ffn_shared_w_down': 8.0,
     'L0_c': 3.87,
     'L0_wmod': 3.853,
     'L1_ffn_gate_w': 8.0,
     'L1_ffn_gate_b': 8.0,
     'L1_ffn_w1': 8.0,
     'L1_ffn_w2': 8.0,
     'L1_ffn_w3': 8.0,
     'L1_ffn_sw1': 8.0,
     'L1_ffn_sw2': 8.0,
     'L1_ffn_sw3': 8.0}
    for name, (base, spread) in spreads.items():
        noise = np.random.default_rng([zlib.crc32(name.encode()), seed]).standard_normal(out[name].shape)
        drawn = base * np.exp(spread * noise) if base else spread * noise
        out[name] = jnp.asarray(drawn.astype(out[name].dtype))
    for name, factor in factors.items():
        out[name] = (out[name] * factor).astype(out[name].dtype)
    return out
```

```python
from contextlib import ExitStack

import concourse.bass as bass
from concourse import mybir

P = 128
F32 = mybir.dt.float32
BF16 = mybir.dt.bfloat16
U32 = mybir.dt.uint32
ALU = mybir.AluOpType
ACT = mybir.ActivationFunctionType
AX = mybir.AxisListType

LN_EPS = 1e-5
TOP_EPS = 1e-8
GATE_FLOOR = 0.25


def build_program(nc, d, out):
    S, E = d["x"].shape
    NT = S // P
    KE = E // P
    HQ = d["wq"].shape[1] // P
    NG = d["wkv"].shape[1] // (2 * P)
    QPG = HQ // NG
    NU = NT * HQ
    NGR = NT * NG
    NB = 8
    NX = d["wr"].shape[1]
    H1, D1 = 16, E // 16
    INTER, NE = 176, 8
    HID = INTER * (NE + 1)
    KH = -(-HID // P)
    SCALE0 = float(P) ** -0.5
    SCALE1 = float(D1) ** -0.5
    LAG = 3

    with ExitStack() as ctx:
        def sb(name, shape, dt=F32):
            return ctx.enter_context(nc.sbuf_tensor(name, shape, dt))

        def sem(name):
            return ctx.enter_context(nc.semaphore(name))

        x = sb("x", [P, NT, E])
        hT = sb("hT", [P, KE, S])
        wq_region = sb("wq_region", [P, KE * HQ * P])
        wkv_region = sb("wkv_region", [P, KE * 2 * NG * P])
        q_region = sb("q_region", [P, NT * HQ * P])
        k_region = sb("k_region", [P, NG * S])
        v_region = sb("v_region", [P, NT * NG * P])
        pt_region = sb("pt_region", [P, 8192])
        wo_region = sb("wo_region", [P, HQ * E])
        peT = sb("peT", [P, S])
        bvB = sb("bvB", [P, NG * P])
        xn = sb("xn", [P, 2, E])
        tmp = sb("tmp", [P, 2, 512])
        gates = sb("gates", [P, 2, 2, E])
        modcol = sb("modcol", [P, 2, 8])
        ident = sb("ident", [P, P])
        ident_b = sb("ident_b", [P, P], BF16)
        mask_b = sb("mask_b", [P, P], BF16)
        mask_f = sb("mask_f", [P, P])
        csB = sb("csB", [P, 4, P])
        half = sb("half", [P, NT * NE])
        cs = sb("cs", [P, 4])
        cth = sb("cth", [P, 4])
        bq = sb("bq", [P, HQ])
        bk = sb("bk", [P, NG])
        mhalf = sb("mhalf", [P, NT])
        mv = sb("mv", [P, NT, 2])
        st = sb("st", [P, 2, 6])
        mv2 = sb("mv2", [P, 2, 2])
        ve = sb("ve", [P, 2])
        rstd = sb("rstd", [P, 2])
        ve0 = sb("ve0", [P, NT])
        rstd0 = sb("rstd0", [P, NT])
        negmax = sb("negmax", [P, 4])
        rowsum = sb("rowsum", [P, 4])
        rinv = sb("rinv", [P, 4])
        mixs = sb("mixs", [P, NB])
        small = sb("small", [P, 64])

        wq = wq_region[:, :].rearrange("p (k n) -> p k n", k=KE)
        wkv = wkv_region[:, :].rearrange("p (k n) -> p k n", k=KE)
        probs = wq_region[:, :].rearrange("p (r n) -> p r n", r=4)
        oT = wkv_region[:, :].bitcast(BF16).rearrange("p (w h n) -> p w h n", w=2, h=HQ)
        qT = q_region[:, :].rearrange("p (t h n) -> p t h n", t=NT, h=HQ)
        kT = k_region[:, :].rearrange("p (g n) -> p g n", g=NG)
        v_hl = v_region[:, :].bitcast(BF16).rearrange("p (w t n) -> p w t n", w=2, t=NT)
        pT = pt_region[:, :].bitcast(BF16).rearrange("p (b w j h n) -> p b w j h n", b=2, w=2, j=NT, h=QPG)
        wo_hl = wo_region[:, :].bitcast(BF16).rearrange("p (w h n) -> p w h n", w=2, h=HQ)
        wmod = pt_region[:, 0:2 * KE * 6 * E].rearrange("p (l k n) -> p l k n", l=2, k=KE)
        wo_stage = pt_region[:, 2 * KE * 6 * E:8192].rearrange("p (b h n) -> p b h n", b=2, h=4)
        modrow = xn[:, :, :].rearrange("p a n -> p (a n)")

        def slot(a, b):
            w = HQ * P
            return q_region[:, a * w:b * w]

        h_hl = slot(0, 1).bitcast(BF16).rearrange("p (w k n) -> p w k n", w=2, k=KE)
        wgu_f = slot(1, 3).rearrange("p (m k n) -> p m k n", m=2, k=KE)
        wr = slot(3, 4)[:, 0:KE * NX].rearrange("p (k n) -> p k n", k=KE)
        wsh_f = slot(3, 4)[:, 256:256 + 1024].rearrange("p (k n) -> p k n", k=KE)
        wdn_f = slot(3, 4)[:, 1280:1280 + 768].rearrange("p (k n) -> p k n", k=3)
        wgu = slot(4, 6).bitcast(BF16).rearrange("p (w m k n) -> p w m k n", w=2, m=2, k=KE)
        wsh = slot(6, 7)[:, 0:1024].bitcast(BF16).rearrange("p (w k n) -> p w k n", w=2, k=KE)
        wdn = slot(6, 7)[:, 1024:1792].bitcast(BF16).rearrange("p (w k n) -> p w k n", w=2, k=3)
        sc = pt_region
        th0 = sc[:, 0:1024].rearrange("p (b n) -> p b n", b=2)
        act0 = sc[:, 1024:2048].rearrange("p (b n) -> p b n", b=2)
        basis = sc[:, 2048:4096].rearrange("p (b k n) -> p b k n", b=2, k=NB)
        tree = sc[:, 4096:4096 + 768]
        mcat = sc[:, 4864:4864 + 768].rearrange("p (b n) -> p b n", b=2)
        mcT = sc[:, 5632:5632 + 768].bitcast(BF16).rearrange("p (b w n) -> p b w n", b=2, w=2)
        logit = sc[:, 6400:6528]
        eexp = sc[:, 6528:6656]
        onehot = sc[:, 6656:6784]
        coeff = sc[:, 6784:6912]
        coeffT = sc[:, 6912:7040]
        iota = wq_region[:, 0:128]
        c_tok = wq_region[:, 128:128 + 2 * NB].rearrange("p (b n) -> p b n", b=2)
        w1b = k_region[:, 0:HID].bitcast(BF16).rearrange("p (k n) -> p k n", k=KE)
        w3b = k_region[:, HID:2 * HID].bitcast(BF16).rearrange("p (k n) -> p k n", k=KE)
        w2b = v_region[:, 0:KH * E // 2].bitcast(BF16).rearrange("p (k n) -> p k n", k=KH)
        w1a_f = v_region[:, 1664:1664 + KE * 4 * E].rearrange("p (k n) -> p k n", k=KE)
        w1a = wo_region[:, 0:KE * 4 * E].bitcast(BF16).rearrange("p (w k n) -> p w k n", w=2, k=KE)
        b1a = wo_region[:, 2048:2048 + 4 * E]
        ropeC = wo_region[:, 3072:3072 + NT * D1].rearrange("p (t n) -> p t n", t=NT)
        ropeS = wo_region[:, 3200:3200 + NT * D1].rearrange("p (t n) -> p t n", t=NT)
        gwf = wo_region[:, 3328:3328 + KE * NE].rearrange("p (k n) -> p k n", k=KE)
        gbB = wo_region[:, 3344:3344 + NE]
        iota1 = wo_region[:, 3352:3352 + NE]
        prod1 = slot(1, 5).rearrange("p (b n) -> p b n", b=2)
        prod2 = wq_region[:, :]
        qkb = slot(5, 6)[:, 0:1024].rearrange("p (b n) -> p b n", b=2)
        vb = slot(5, 6)[:, 1024:1536].rearrange("p (b n) -> p b n", b=2)
        ropeA = slot(6, 7)[:, 0:512]
        ropeB = slot(6, 7)[:, 512:1024]
        qkr = slot(6, 7)[:, 1024:2048].rearrange("p (b n) -> p b n", b=2)
        ssub = slot(7, 8)[:, 0:256]
        e1 = slot(7, 8)[:, 256:768].rearrange("p (b n) -> p b n", b=2)
        av = slot(7, 8)[:, 768:1280].rearrange("p (b n) -> p b n", b=2)
        avr = slot(7, 8)[:, 1280:1536]
        m1 = slot(7, 8)[:, 1536:1568].rearrange("p (b n) -> p b n", b=2)
        s1 = slot(7, 8)[:, 1568:1584]
        r1 = slot(7, 8)[:, 1584:1600]
        mixed_rows = pt_region[:, 0:NT * E].rearrange("p (t n) -> p t n", t=NT)
        aT = pt_region[:, 2048:2048 + 512].bitcast(BF16).rearrange("p (b w n) -> p b w n", b=2, w=2)
        ytmp = pt_region[:, 2560:2816]
        hc = slot(1, 3)[:, 0:2 * HID].rearrange("p (b n) -> p b n", b=2)
        hcT = slot(3, 5)[:, 0:2 * KH * P].bitcast(BF16).rearrange("p (b w n) -> p b w n", b=2, w=2)
        th1 = slot(5, 6)[:, 0:704].rearrange("p (b n) -> p b n", b=2)
        a1 = slot(5, 6)[:, 704:1408].rearrange("p (b n) -> p b n", b=2)
        cw = slot(6, 7)[:, 0:NT * NE].rearrange("p (t n) -> p t n", t=NT)
        g_s = slot(6, 7)[:, 256:320]
        g_a = slot(6, 7)[:, 320:384]
        g_b = slot(6, 7)[:, 384:448]
        g_c = slot(6, 7)[:, 448:512]
        g_m = slot(6, 7)[:, 512:576]
        g_x = slot(6, 7)[:, 576:640]
        g_i = slot(6, 7)[:, 640:704]
        g_u = slot(6, 7)[:, 704:768].bitcast(U32)
        g_r = slot(6, 7)[:, 768:832]

        psS = ctx.enter_context(nc.psum_tensor("psS", [P, 4, 512], F32))
        psT = ctx.enter_context(nc.psum_tensor("psT", [P, 2, 512], F32))
        psO = ctx.enter_context(nc.psum_tensor("psO", [P, 512], F32))
        psM = ctx.enter_context(nc.psum_tensor("psM", [P, 512], F32))
        scratch = nc.dram_tensor("head_shuffle", [H1, S, D1], F32, kind="Internal").ap()

        names_loaded = ["cs", "xa", "xb", "wmod0a", "wmod0b", "wmod1", "wkv", "wq", "peT", "bvB", "ident", "mask",
                        "bq", "bk", "wgu", "wr", "wsh", "wdn", "iota", "amp", "w1", "w3", "w2", "w1a", "b1a",
                        "rope", "gw", "mixed", "escale"]
        loaded = {n: sem("loaded_" + n) for n in names_loaded}
        wo_loaded = [sem(f"wo_loaded{c}") for c in range(4)]
        ve_chain = sem("vector_chain")
        ac_chain = sem("scalar_chain")
        po_chain = sem("pool_chain")
        cond_tanh = sem("cond_tanh")
        cond_rows = sem("cond_rows")
        mod_ps = sem("mod_ps")
        mod_rows = sem("mod_rows")
        mod_T = sem("mod_T")
        mod_done = sem("mod_done")
        var_ready = sem("var_ready")
        rstd_ready = sem("rstd_ready")
        xn_ready = sem("xn_ready")
        xn_T = sem("xn_T")
        hT_ready = sem("hT_ready")
        hlo_ready = sem("hlo_ready")
        proj_done = sem("proj_done")
        tmp_ready = sem("tmp_ready")
        tmp_used = sem("tmp_used")
        q_ready = sem("q_ready")
        vlo_ready = sem("vlo_ready")
        wo_hi = sem("wo_hi")
        wo_lo = sem("wo_lo")
        masks_ready = sem("masks_ready")
        scores = sem("scores")
        negmax_ready = sem("negmax_ready")
        exp_done = sem("exp_done")
        rinv_ready = sem("rinv_ready")
        normed = sem("normed")
        pT_ps = sem("pT_ps")
        pT_hi = sem("pT_hi")
        pT_lo = sem("pT_lo")
        pv = sem("pv")
        oT_hi = sem("oT_hi")
        oT_lo = sem("oT_lo")
        wo_done = sem("wo_done")
        res_read = sem("res_read")
        w_hi = sem("w_hi")
        w_lo = sem("w_lo")
        logit_ps = sem("logit_ps")
        neg_ready = sem("neg_ready")
        e_ready = sem("e_ready")
        coeff_ready = sem("coeff_ready")
        coT_ps = sem("coT_ps")
        coT_ready = sem("coT_ready")
        c_ps = sem("c_ps")
        c_ready = sem("c_ready")
        pair_ps = sem("pair_ps")
        tanh_ready = sem("tanh_ready")
        pair_used = sem("pair_used")
        basis_sum = sem("basis_sum")
        mix_T = sem("mix_T")
        mix_hi = sem("mix_hi")
        mix_lo = sem("mix_lo")
        down_ps = sem("down_ps")
        qkv_ps = sem("qkv_ps")
        qkv_read = sem("qkv_read")
        prod1_ready = sem("prod1_ready")
        s_sum = sem("s_sum")
        sub_ready = sem("sub_ready")
        e1_ready = sem("e1_ready")
        prod2_ready = sem("prod2_ready")
        prod2_used = sem("prod2_used")
        qkr_ready = sem("qkr_ready")
        av_ready = sem("av_ready")
        shuffled = [sem(f"shuffled{t}") for t in range(NT)]
        a_T = sem("a_T")
        a_hi = sem("a_hi")
        a_lo = sem("a_lo")
        o_ps = sem("o_ps")
        gate_ps = sem("gate_ps")
        gate_read = sem("gate_read")
        gexp = sem("gexp")
        gabs = sem("gabs")
        sp_ready = sem("sp_ready")
        sq_ready = sem("sq_ready")
        chunk_ps = sem("chunk_ps")
        chunk_tanh = sem("chunk_tanh")
        chunk_used = sem("chunk_used")
        hc_T = sem("hc_T")
        hc_hi = sem("hc_hi")
        hc_lo = sem("hc_lo")
        moe_ps = sem("moe_ps")
        x_out = sem("x_out")
        stored = sem("stored")

        def unit(u):
            return u // HQ, u % HQ

        def chunks(i):
            return [(c, min(4, i + 1 - c)) for c in range(0, i + 1, 4)]

        chunk_end = []
        for u in range(NU):
            chunk_end.append((chunk_end[-1] if u else 0) + len(chunks(unit(u)[0])))

        proj = [("k", g, n) for n in (0,) for g in range(NG)] + [("v", i, 0) for i in range(NT // 2)]
        proj += [("k", g, 1) for g in range(NG)] + [("v", i, 0) for i in range(NT // 2, NT)]
        NKV = len(proj)
        proj += [("q", h, n) for n in range(2) for h in range(HQ)]

        MOD = [(0, 0), (0, 1), (0, 2), (1, 0), (1, 1), (1, 2)]

        WSPLIT = [(NT - 1) * HQ + 1 + 2 * n_ for n_ in range(6)]
        NCH = NE // 2 + 1

        block = ctx.enter_context(nc.Block())

        @block.sync
        def _(sp):
            sp.dma_start(cs[:, :], d["cs"]).then_inc(loaded["cs"], 16)
            xv = d["x"].rearrange("(t p) n -> p t n", p=P)
            wm = [d[f"wmod{n}"].rearrange("(k p) n -> p k n", p=P) for n in range(2)]
            sp.dma_start(wmod[:, 0, :, 0:2 * E], wm[0][:, :, 0:2 * E]).then_inc(loaded["wmod0a"], 16)
            sp.dma_start(x[:, 0:4, :], xv[:, 0:4, :]).then_inc(loaded["xa"], 16)
            sp.dma_start(ident[:, :], d["ident"]).then_inc(loaded["ident"], 16)
            sp.dma_start(x[:, 4:8, :], xv[:, 4:8, :]).then_inc(loaded["xb"], 16)
            sp.dma_start(wkv, d["wkv"].rearrange("(k p) n -> p k n", p=P)).then_inc(loaded["wkv"], 16)
            sp.dma_start(peT[:, :], d["peT"]).then_inc(loaded["peT"], 16)
            sp.dma_start(bk[:, :], d["bk"]).then_inc(loaded["bk"], 16)
            sp.dma_start(bvB[:, :], d["bv"].partition_broadcast(P)).then_inc(loaded["bvB"], 16)
            sp.dma_start(mask_f[:, :], d["mask"]).then_inc(loaded["mask"], 16)
            sp.dma_start(bq[:, :], d["bq"]).then_inc(loaded["bq"], 16)
            sp.dma_start(wq, d["wq"].rearrange("(k p) n -> p k n", p=P)).then_inc(loaded["wq"], 16)
            sp.dma_start(small[:, 0:16], d["amp"]).then_inc(loaded["amp"], 16)
            sp.dma_start(small[:, 16:17], d["escale"]).then_inc(loaded["escale"], 16)
            sp.dma_start(wmod[:, 0, :, 2 * E:6 * E], wm[0][:, :, 2 * E:6 * E]).then_inc(loaded["wmod0b"], 16)
            sp.dma_start(wmod[:, 1, :, :], wm[1]).then_inc(loaded["wmod1"], 16)
            wov = d["wo"].rearrange("(h p) n -> p h n", p=P)
            for c in range(4):
                if c >= 2:
                    sp.wait_ge(wo_lo, c - 1)
                sp.dma_start(wo_stage[:, c % 2, :, :], wov[:, 4 * c:4 * c + 4, :]).then_inc(wo_loaded[c], 16)
            sp.wait_ge(scores, 3 * HQ)
            for m, n in enumerate(("wg", "wu")):
                sp.dma_start(wgu_f[:, m, :, :], d[n].rearrange("(k p) n -> p k n", p=P)).then_inc(loaded["wgu"], 16)
            sp.wait_ge(scores, 4 * HQ)
            sp.dma_start(wr, d["wr"].rearrange("(k p) n -> p k n", p=P)).then_inc(loaded["wr"], 16)
            for m, n in enumerate(("swg", "swu")):
                sp.dma_start(wsh_f[:, :, m * E:(m + 1) * E],
                             d[n].rearrange("(k p) n -> p k n", p=P)).then_inc(loaded["wsh"], 16)
            sp.dma_start(wdn_f[:, 0:1, :], d["wd"].rearrange("(k p) n -> p k n", p=P)).then_inc(loaded["wdn"], 16)
            sp.dma_start(wdn_f[:, 1:3, :], d["swd"].rearrange("(k p) n -> p k n", p=P)).then_inc(loaded["wdn"], 16)
            sp.wait_ge(wo_done, NT)
            sp.dma_start(iota, d["iota"].partition_broadcast(P)).then_inc(loaded["iota"], 16)
            sp.dma_start(w1a_f, d["w1a"].rearrange("(k p) n -> p k n", p=P)).then_inc(loaded["w1a"], 16)
            sp.dma_start(b1a, d["b1a"].partition_broadcast(P)).then_inc(loaded["b1a"], 16)
            sp.dma_start(ropeC, d["ropeC"].rearrange("p (t n) -> p t n", t=NT)).then_inc(loaded["rope"], 16)
            sp.dma_start(ropeS, d["ropeS"].rearrange("p (t n) -> p t n", t=NT)).then_inc(loaded["rope"], 16)
            sp.dma_start(gwf, d["gw"].rearrange("(k p) n -> p k n", p=P)).then_inc(loaded["gw"], 16)
            sp.dma_start(gbB, d["gb"].partition_broadcast(P)).then_inc(loaded["gw"], 16)
            sp.dma_start(iota1, d["iota"][:, 0:NE].partition_broadcast(P)).then_inc(loaded["gw"], 16)
            sp.dma_start(w1b, d["w1"].rearrange("(k p) n -> p k n", p=P)).then_inc(loaded["w1"], 16)
            sp.dma_start(w3b, d["w3"].rearrange("(k p) n -> p k n", p=P)).then_inc(loaded["w3"], 16)
            full = HID // P
            sp.dma_start(w2b[:, 0:full, :], d["w2"][0:full * P, :].rearrange("(k p) n -> p k n", p=P)) \
                .then_inc(loaded["w2"], 16)
            sp.dma_start(w2b[0:HID - full * P, full, :], d["w2"][full * P:HID, :]).then_inc(loaded["w2"], 16)
            for t in range(NT):
                sp.wait_ge(av_ready, t + 1)
                sp.dma_start(scratch[:, t * P:(t + 1) * P, :].rearrange("h p n -> p h n"),
                             av[:, t % 2, :].rearrange("p (h n) -> p h n", h=H1)).then_inc(shuffled[t], 16)
            for t in range(NT):
                sp.wait_ge(shuffled[t], 16)
            rows = scratch.rearrange("h s n -> (h s n)").rearrange("(t p n) -> p t n", p=P, n=E)
            for j in range(2):
                sp.dma_start(mixed_rows[:, 4 * j:4 * j + 4, :], rows[:, 4 * j:4 * j + 4, :]) \
                    .then_inc(loaded["mixed"], 16)
            ov = out.rearrange("(t p) n -> p t n", p=P)
            for t in range(NT):
                sp.wait_ge(x_out, t + 1)
                sp.dma_start(ov[:, t, :], x[:, t, :]).then_inc(stored, 16)
            sp.wait_ge(stored, 16 * NT)

        @block.gpsimd
        def _(pool):
            g = nc.gpsimd
            n = [0]

            def link(ins):
                n[0] += 1
                ins.then_inc(po_chain, 1)
                pool.wait_ge(po_chain, n[0])

            link(g.memset(mhalf[:, :], -0.5))
            link(g.memset(half[:, :], 0.5))
            pool.wait_ge(var_ready, 1)
            g.tensor_tensor(rstd0[:, :], ve0[:, :], mhalf[:, :], ALU.pow).then_inc(rstd_ready, 1)

            def rstd_of(q):
                pool.wait_ge(var_ready, q - NT + 2)
                g.tensor_tensor(rstd[:, q % 2:q % 2 + 1], ve[:, q % 2:q % 2 + 1], mhalf[:, 0:1], ALU.pow) \
                    .then_inc(rstd_ready, 1)

            for u in range(NU):
                i, h = unit(u)
                w = (i + 1) * P
                pool.wait_ge(rinv_ready, u + 1)
                g.tensor_tensor(probs[:, u % 4, 0:w], probs[:, u % 4, 0:w],
                                rinv[:, u % 4:u % 4 + 1].to_broadcast([P, w]), ALU.mult).then_inc(normed, 1)
                if u >= 24 and (u - 24) % HQ == 0:
                    rstd_of(NT + (u - 24) // HQ)
            rstd_of(2 * NT - 1)
            for t in range(NT):
                b = t % 2
                pool.wait_ge(pair_used, 3 * t + 2)
                link(g.tensor_tensor(tree[:, 0:512], basis[:, b, 0:4, :], basis[:, b, 4:8, :], ALU.add))
                link(g.tensor_tensor(tree[:, 512:768], tree[:, 0:256], tree[:, 256:512], ALU.add))
                if t >= 2:
                    pool.wait_ge(mix_T, t - 1)
                g.tensor_tensor(mcat[:, b, 0:P], tree[:, 512:640], tree[:, 640:768], ALU.add).then_inc(basis_sum, 1)
                if t >= 1:
                    rstd_of(2 * NT + t - 1)
            rstd_of(3 * NT - 1)
            for t in range(NT):
                pool.wait_ge(e1_ready, t + 1)
                pool.wait_ge(qkr_ready, t + 1)
                if t >= 1:
                    pool.wait_ge(prod2_used, t)
                g.tensor_tensor(prod2.rearrange("p (h d t) -> p h d t", h=H1, d=D1),
                                e1[:, t % 2, :].rearrange("p (h t) -> p h t", h=H1).unsqueeze(2)
                                .to_broadcast([P, H1, D1, H1]),
                                vb[:, t % 2, :].rearrange("p (t d) -> p d t", t=H1).unsqueeze(1)
                                .to_broadcast([P, H1, D1, H1]), ALU.mult).then_inc(prod2_ready, 1)
            for t in range(NT):
                rstd_of(3 * NT + t)
            pool.wait_ge(sp_ready, 1)
            g.tensor_tensor(g_r, g_c, half[:, :], ALU.pow).then_inc(sq_ready, 1)

        @block.scalar
        def _(act):
            s = nc.scalar
            act.wait_ge(loaded["cs"], 16)
            s.activation(cth[:, :], cs[:, :], ACT.Tanh, scale=0.5).then_inc(cond_tanh, 1)

            def norm_out(q, ps, layer, which, halves):
                i = q % NT
                act.wait_ge(xn_T, q + 1)
                for k in range(KE):
                    o = which * 4
                    sh = modcol[:, layer, o + k:o + k + 1]
                    sc_ = modcol[:, layer, o + 2 + k:o + 3 + k]
                    src = ps[:, k * P:(k + 1) * P]
                    s.activation(hT[:, k, i * P:(i + 1) * P], src, ACT.Identity, bias=sh, scale=sc_) \
                        .then_inc(hT_ready, 1)
                    if halves:
                        s.activation(h_hl[:, 0, k, i * P:(i + 1) * P], src, ACT.Identity, bias=sh, scale=sc_) \
                            .then_inc(hT_ready, 1)

            act.wait_ge(mod_done, 1)
            for i in range(NT):
                norm_out(i, psT[:, i % 2, :], 0, 0, False)
            for m in range(NKV):
                kind, a, b = proj[m]
                act.wait_ge(tmp_ready, m + 1)
                if kind == "k":
                    s.activation(kT[:, a, b * 512:(b + 1) * 512], tmp[:, m % 2, :], ACT.Copy, scale=SCALE0) \
                        .then_inc(tmp_used, 1)
                else:
                    s.activation(v_hl[:, 0, a, :], tmp[:, m % 2, :], ACT.Copy).then_inc(tmp_used, 1)
            for c in range(4):
                act.wait_ge(wo_loaded[c], 16)
                s.activation(wo_hl[:, 0, 4 * c:4 * c + 4, :], wo_stage[:, c % 2, :, :], ACT.Copy).then_inc(wo_hi, 1)

            def weights_high(n_):
                if n_ < 4:
                    m, k = n_ // 2, n_ % 2
                    act.wait_ge(loaded["wgu"], 32)
                    s.activation(wgu[:, 0, m, k, :], wgu_f[:, m, k, :], ACT.Copy).then_inc(w_hi, 1)
                elif n_ == 4:
                    act.wait_ge(loaded["wsh"], 32)
                    s.activation(wsh[:, 0, :, :], wsh_f, ACT.Copy).then_inc(w_hi, 1)
                else:
                    act.wait_ge(loaded["wdn"], 32)
                    s.activation(wdn[:, 0, 0, :], wdn_f[:, 0, :], ACT.Copy).then_inc(w_hi, 1)
                    s.activation(wdn[:, 0, 1:3, :], wdn_f[:, 1:3, :], ACT.Copy, scale=0.5).then_inc(w_hi, 1)

            nh = [0]
            for st_ in range(NU + 13):
                if st_ >= 11 and (st_ - 11) % QPG == 0 and (st_ - 11) // QPG < NGR:
                    G = (st_ - 11) // QPG
                    act.wait_ge(pv, G + 1)
                    if G >= NG:
                        act.wait_ge(wo_done, G // NG)
                    s.activation(oT[:, 0, (G % NG) * QPG:(G % NG + 1) * QPG, :],
                                 psO[:, :].rearrange("p (h n) -> p h n", h=QPG), ACT.Copy).then_inc(oT_hi, 1)
                if LAG <= st_ < NU + LAG:
                    u = st_ - LAG
                    i, h = unit(u)
                    G = u // QPG
                    if G >= 2:
                        act.wait_ge(pv, G - 1)
                    for c, k in chunks(i):
                        act.wait_ge(pT_ps, nh[0] + 1)
                        s.activation(pT[:, G % 2, 0, c:c + k, h % QPG, :],
                                     psT[:, nh[0] % 2, 0:k * P].rearrange("p (k n) -> p k n", k=k),
                                     ACT.Copy).then_inc(pT_hi, 1)
                        nh[0] += 1
                if st_ < NU:
                    u = st_
                    i, h = unit(u)
                    w = (i + 1) * P
                    act.wait_ge(negmax_ready, u + 1)
                    if u >= 4:
                        act.wait_ge(pT_ps, chunk_end[u - 4])
                    s.activation(probs[:, u % 4, 0:w], psS[:, 2 * (u % 2):2 * (u % 2) + 2, :]
                                 .rearrange("p a n -> p (a n)")[:, 0:w], ACT.Exp,
                                 bias=negmax[:, u % 4:u % 4 + 1], accum_out=rowsum[:, u % 4:u % 4 + 1]) \
                        .then_inc(exp_done, 1)
                if st_ >= 27 and (st_ - 27) % HQ == 0:
                    norm_out(NT + (st_ - 27) // HQ, psM[:, 256:512], 0, 1, True)
                if st_ in WSPLIT:
                    weights_high(WSPLIT.index(st_))
            def router_exps(t):
                act.wait_ge(neg_ready, t + 1)
                s.activation(eexp, logit, ACT.Exp, bias=small[:, 28:29], accum_out=small[:, 29:30]) \
                    .then_inc(e_ready, 1)
                s.activation(small[:, 30:34], small[:, 20:24], ACT.Exp, bias=small[:, 28:29],
                             accum_out=small[:, 34:35]).then_inc(e_ready, 1)
                act.wait_ge(coT_ps, t + 1)
                s.activation(coeffT, psO[:, P:2 * P], ACT.Copy).then_inc(coT_ready, 1)

            router_exps(0)
            for t in range(NT + 1):
                if t < NT:
                    for j in range(3):
                        p = 3 * t + j
                        w = 512 if j < 2 else 256
                        act.wait_ge(pair_ps, p + 1)
                        if p >= 2:
                            act.wait_ge(pair_used, p - 1)
                        s.activation(th0[:, p % 2, 0:w], psS[:, 2 * (p % 2), 0:w], ACT.Tanh, scale=0.5) \
                            .then_inc(tanh_ready, 1)
                if t >= 1:
                    b = (t - 1) % 2
                    act.wait_ge(mix_T, t)
                    s.activation(mcT[:, b, 0, :], psT[:, b, 0:384], ACT.Copy).then_inc(mix_hi, 1)
                if t + 1 < NT:
                    router_exps(t + 1)
                if t >= 2:
                    norm_out(2 * NT + t - 2, psM[:, 256:512], 1, 0, True)
            norm_out(3 * NT - 1, psM[:, 256:512], 1, 0, True)
            act.wait_ge(loaded["w1a"], 16)
            for k in range(KE):
                s.activation(w1a[:, 0, k, :], w1a_f[:, k, :], ACT.Copy).then_inc(w_hi, 1)
            for t in range(NT):
                act.wait_ge(sub_ready, t + 1)
                if t >= 2:
                    act.wait_ge(prod2_ready, t - 1)
                s.activation(e1[:, t % 2, :], ssub, ACT.Exp, scale=SCALE1).then_inc(e1_ready, 1)
            for t in range(NT + 1):
                if t < NT:
                    act.wait_ge(a_T, t + 1)
                    s.activation(aT[:, t % 2, 0, :], psT[:, t % 2, 0:E], ACT.Copy).then_inc(a_hi, 1)
                if t >= 1:
                    norm_out(3 * NT + t - 1, psM[:, 256:512], 1, 1, True)
            act.wait_ge(gabs, 1)
            s.activation(g_b, g_a, ACT.Exp, scale=-1.0).then_inc(gexp, 1)
            act.wait_ge(gabs, 2)
            s.activation(g_c, g_a, ACT.Ln).then_inc(gexp, 1)
            nchunk = NCH
            for t in range(NT + 1):
                if t < NT:
                    for j in range(nchunk):
                        p = nchunk * t + j
                        w = 2 * INTER if j < 4 else INTER
                        act.wait_ge(chunk_ps, p + 1)
                        if p >= 2:
                            act.wait_ge(chunk_used, p - 1)
                        s.activation(th1[:, p % 2, 0:w], psS[:, 2 * (p % 2), 0:w], ACT.Tanh, scale=0.5) \
                            .then_inc(chunk_tanh, 1)
                if t >= 1:
                    for c in range(4):
                        m = 4 * (t - 1) + c
                        w = 4 if c < 3 else 1
                        act.wait_ge(hc_T, m + 1)
                        if t >= 3 and c == 0:
                            act.wait_ge(moe_ps, t - 2)
                        rows_ = P if c < 3 else HID - 12 * P
                        s.activation(hcT[0:rows_, (t - 1) % 2, 0, c * 512:c * 512 + w * P],
                                     psT[0:rows_, m % 2, 0:w * P], ACT.Copy).then_inc(hc_hi, 1)

        @block.vector
        def _(dve):
            v = nc.vector
            n = [0]

            def link(ins):
                n[0] += 1
                ins.then_inc(ve_chain, 1)
                dve.wait_ge(ve_chain, n[0])

            def xn_of(q, mean, rs):
                dve.wait_ge(xn_T, q - 1) if q >= 2 else None
                v.tensor_scalar(xn[:, q % 2, :], x[:, q % NT, :], mean, rs, ALU.subtract, ALU.mult) \
                    .then_inc(xn_ready, 1)

            dve.wait_ge(cond_tanh, 1)
            link(v.scalar_tensor_tensor(out=cth[:, :], in0=cth[:, :], scalar=1.0, in1=cs[:, :],
                                        op0=ALU.add, op1=ALU.mult))
            link(v.tensor_scalar(cth[:, :], cth[:, :], 0.5, None, ALU.mult))
            v.tensor_copy(csB[:, :, :], cth[:, :].unsqueeze(2).to_broadcast([P, 4, P])).then_inc(cond_rows, 1)

            for i in range(NT):
                dve.wait_ge(loaded["xa" if i < 4 else "xb"], 16)
                link(v.bn_stats(st[:, i % 2, :], x[:, i, :]))
                link(v.bn_aggr(mv[:, i, :], st[:, i % 2, :]))
            v.tensor_scalar(ve0[:, :], mv[:, :, 1], LN_EPS, None, ALU.add).then_inc(var_ready, 1)

            def modulation(j):
                layer, third = MOD[j]
                dve.wait_ge(mod_ps, j + 1)
                if third == 0:
                    v.tensor_copy(modrow, psO[:, :]).then_inc(mod_rows, 1)
                else:
                    a = 256 if third == 1 else 0
                    gt = 256 - a
                    v.tensor_copy(modrow[:, 0:256], psO[:, a:a + 256]).then_inc(mod_rows, 1)
                    gdst = gates[:, layer, third - 1, :]
                    gps = psO[:, gt:gt + 256]
                    link(v.tensor_scalar(tmp[:, 0, 0:256], gps, 0.0, 2.0, ALU.is_ge, ALU.mult))
                    link(v.tensor_scalar(tmp[:, 0, 0:256], tmp[:, 0, 0:256], -1.0, None, ALU.add))
                    link(v.tensor_tensor(tmp[:, 0, 256:512], gps, tmp[:, 0, 0:256], ALU.mult))
                    link(v.scalar_tensor_tensor(out=gdst, in0=tmp[:, 0, 256:512], scalar=GATE_FLOOR,
                                                in1=tmp[:, 0, 0:256], op0=ALU.max, op1=ALU.mult))
                dve.wait_ge(mod_T, j + 1)
                cols = psM[:, :].rearrange("p (b n) -> p b n", n=P)[:, :, 0]
                if third == 0:
                    link(v.tensor_copy(modcol[:, layer, 0:2], cols[:, 0:2]))
                    v.tensor_scalar(modcol[:, layer, 2:4], cols[:, 2:4], 1.0, None, ALU.add).then_inc(mod_done, 1)
                elif third == 1:
                    v.tensor_copy(modcol[:, layer, 4:6], cols[:, 0:2]).then_inc(mod_done, 1)
                else:
                    v.tensor_scalar(modcol[:, layer, 6:8], cols[:, 0:2], 1.0, None, ALU.add).then_inc(mod_done, 1)

            modulation(0)
            dve.wait_ge(rstd_ready, 1)
            dve.wait_ge(mod_T, 1)
            for i in range(NT):
                xn_of(i, mv[:, i, 0:1], rstd0[:, i:i + 1])
            dve.wait_ge(loaded["ident"], 16)
            link(v.tensor_copy(ident_b[:, :], ident[:, :]))
            dve.wait_ge(loaded["mask"], 16)
            v.tensor_copy(mask_b[:, :], mask_f[:, :]).then_inc(masks_ready, 1)
            dve.wait_ge(loaded["peT"], 16)
            dve.wait_ge(loaded["bk"], 16)
            dve.wait_ge(loaded["bvB"], 16)
            dve.wait_ge(mod_ps, 1)

            def v_low(m):
                kind, a, b = proj[m]
                if kind == "v":
                    dve.wait_ge(tmp_used, m + 1)
                    link(v.tensor_tensor(v_hl[:, 1, a, :], tmp[:, m % 2, :], v_hl[:, 0, a, :], ALU.subtract))

            for m in range(NKV):
                kind, a, b = proj[m]
                if m >= 1:
                    v_low(m - 1)
                dve.wait_ge(proj_done, m + 1)
                if m >= 2:
                    dve.wait_ge(tmp_used, m - 1)
                bank = psS[:, m % 4, :]
                if kind == "k":
                    v.scalar_tensor_tensor(out=tmp[:, m % 2, :], in0=bank, scalar=bk[:, a:a + 1],
                                           in1=peT[:, b * 512:(b + 1) * 512], op0=ALU.add, op1=ALU.add) \
                        .then_inc(tmp_ready, 1)
                else:
                    v.tensor_tensor(tmp[:, m % 2, :], bank, bvB[:, :], ALU.add).then_inc(tmp_ready, 1)
            v_low(NKV - 1)
            dve.wait_ge(loaded["amp"], 16)
            dve.wait_ge(loaded["escale"], 16)
            link(v.tensor_tensor(small[:, 36:52], small[:, 0:16], small[:, 0:16], ALU.mult))
            link(v.tensor_reduce(mixs[:, :], small[:, 36:52].rearrange("p (k c) -> p k c", c=2), AX.X, ALU.add))
            link(v.tensor_reduce(small[:, 17:18], mixs[:, :], AX.X, ALU.add))
            link(v.tensor_scalar(small[:, 17:18], small[:, 17:18], TOP_EPS, None, ALU.add))
            link(v.reciprocal(small[:, 18:19], small[:, 17:18]))
            link(v.tensor_scalar(mixs[:, :], mixs[:, :], small[:, 18:19], small[:, 16:17], ALU.mult, ALU.mult))
            link(v.tensor_scalar(mixs[:, :], mixs[:, :], 0.5, None, ALU.mult))
            dve.wait_ge(loaded["bq"], 16)
            for m in range(NKV, len(proj)):
                kind, h, nn = proj[m]
                dve.wait_ge(proj_done, m + 1)
                v.scalar_tensor_tensor(out=qT[:, 4 * nn:4 * nn + 4, h, :],
                                       in0=psS[:, m % 4, :].rearrange("p (t n) -> p t n", t=4),
                                       scalar=bq[:, h:h + 1],
                                       in1=peT[:, nn * 512:(nn + 1) * 512].rearrange("p (t n) -> p t n", t=4),
                                       op0=ALU.add, op1=ALU.add).then_inc(q_ready, 1)
                if h % 8 == 7:
                    c = (m - NKV) // 8
                    dve.wait_ge(wo_hi, c + 1)
                    v.tensor_tensor(wo_hl[:, 1, 4 * c:4 * c + 4, :], wo_stage[:, c % 2, :, :],
                                    wo_hl[:, 0, 4 * c:4 * c + 4, :], ALU.subtract).then_inc(wo_lo, 1)
            for j in range(1, 6):
                modulation(j)

            def residual(q, ps, layer, which, ready, value, last=False):
                i = q % NT
                dve.wait_ge(ready, value)
                link(v.tensor_tensor(tmp[:, 0, 0:E], ps, gates[:, layer, which, :], ALU.mult))
                if last:
                    v.tensor_tensor(x[:, i, :], x[:, i, :], tmp[:, 0, 0:E], ALU.add).then_inc(x_out, 1)
                    return
                link(v.tensor_tensor(x[:, i, :], x[:, i, :], tmp[:, 0, 0:E], ALU.add))
                link(v.bn_stats(st[:, q % 2, :], x[:, i, :]))
                link(v.bn_aggr(mv2[:, q % 2, :], st[:, q % 2, :]))
                v.tensor_scalar(ve[:, q % 2:q % 2 + 1], mv2[:, q % 2, 1:2], LN_EPS, None, ALU.add) \
                    .then_inc(var_ready, 1)

            def xn_later(q):
                dve.wait_ge(rstd_ready, q - NT + 2)
                xn_of(q, mv2[:, q % 2, 0:1], rstd[:, q % 2:q % 2 + 1])

            def h_low(q):
                i = q % NT
                dve.wait_ge(hT_ready, 2 * NT + 4 * (q - NT + 1))
                v.tensor_tensor(h_hl[:, 1, :, i * P:(i + 1) * P], hT[:, :, i * P:(i + 1) * P],
                                h_hl[:, 0, :, i * P:(i + 1) * P], ALU.subtract).then_inc(hlo_ready, 1)

            def weights_low(n_):
                if n_ < 4:
                    m, k = n_ // 2, n_ % 2
                    dve.wait_ge(w_hi, n_ + 1)
                    v.tensor_tensor(wgu[:, 1, m, k, :], wgu_f[:, m, k, :], wgu[:, 0, m, k, :], ALU.subtract) \
                        .then_inc(w_lo, 1)
                elif n_ == 4:
                    dve.wait_ge(w_hi, 5)
                    v.tensor_tensor(wsh[:, 1, :, :], wsh_f, wsh[:, 0, :, :], ALU.subtract).then_inc(w_lo, 1)
                else:
                    dve.wait_ge(w_hi, 7)
                    v.tensor_tensor(wdn[:, 1, 0, :], wdn_f[:, 0, :], wdn[:, 0, 0, :], ALU.subtract).then_inc(w_lo, 1)
                    v.scalar_tensor_tensor(out=wdn[:, 1, 1:3, :], in0=wdn_f[:, 1:3, :], scalar=0.5,
                                           in1=wdn[:, 0, 1:3, :], op0=ALU.mult, op1=ALU.subtract).then_inc(w_lo, 1)

            nl = [0]
            for st_ in range(NU + 13):
                if 1 <= st_ <= NU:
                    u = st_ - 1
                    dve.wait_ge(exp_done, u + 1)
                    if u >= 4:
                        dve.wait_ge(normed, u - 3)
                    v.reciprocal(rinv[:, u % 4:u % 4 + 1], rowsum[:, u % 4:u % 4 + 1]).then_inc(rinv_ready, 1)
                if st_ >= 11 and (st_ - 11) % QPG == 0 and (st_ - 11) // QPG < NGR:
                    G = (st_ - 11) // QPG
                    dve.wait_ge(oT_hi, G + 1)
                    hs = slice((G % NG) * QPG, (G % NG + 1) * QPG)
                    v.tensor_tensor(oT[:, 1, hs, :], psO[:, :].rearrange("p (h n) -> p h n", h=QPG),
                                    oT[:, 0, hs, :], ALU.subtract).then_inc(oT_lo, 1)
                if st_ < NU:
                    u = st_
                    i, h = unit(u)
                    w = (i + 1) * P
                    dve.wait_ge(scores, u + 1)
                    v.tensor_reduce(negmax[:, u % 4:u % 4 + 1], psS[:, 2 * (u % 2):2 * (u % 2) + 2, :]
                                    .rearrange("p a n -> p (a n)")[:, 0:w], AX.X, ALU.max, negate=True) \
                        .then_inc(negmax_ready, 1)
                if LAG <= st_ < NU + LAG:
                    u = st_ - LAG
                    i, h = unit(u)
                    G = u // QPG
                    for c, k in chunks(i):
                        dve.wait_ge(pT_hi, nl[0] + 1)
                        dst = pT[:, G % 2, :, c:c + k, h % QPG, :]
                        v.tensor_tensor(dst[:, 1], psT[:, nl[0] % 2, 0:k * P].rearrange("p (k n) -> p k n", k=k),
                                        dst[:, 0], ALU.subtract).then_inc(pT_lo, 1)
                        nl[0] += 1
                if st_ >= 26 and (st_ - 26) % HQ == 0:
                    xn_later(NT + (st_ - 26) // HQ)
                if st_ >= 25 and (st_ - 25) % HQ == 0:
                    i = (st_ - 25) // HQ
                    residual(NT + i, psM[:, 0:E], 0, 0, wo_done, i + 1)
                if st_ >= 28 and (st_ - 28) % HQ == 0:
                    h_low(NT + (st_ - 28) // HQ)
                if st_ in WSPLIT:
                    weights_low(WSPLIT.index(st_))
            dve.wait_ge(loaded["iota"], 16)

            mx8, neg, zsum, top4, den, rr = (small[:, 20:28], small[:, 28:29], small[:, 29:30],
                                             small[:, 34:35], small[:, 35:36], small[:, 19:20])
            idx = small[:, 52:60]

            def router(t):
                dve.wait_ge(logit_ps, t + 1)
                if t >= 1:
                    dve.wait_ge(e_ready, 2 * t)
                link(v.tensor_copy(logit, psO[:, 0:P]))
                link(v.max(mx8, logit))
                v.tensor_scalar(neg, mx8[:, 0:1], -1.0, None, ALU.mult).then_inc(neg_ready, 1)
                link(v.max_index(small[:, 36:44].bitcast(U32), mx8, logit))
                link(v.tensor_copy(idx, small[:, 36:44].bitcast(U32)))
                link(v.tensor_scalar(onehot, iota, idx[:, 0:1], None, ALU.is_equal))
                for k in range(1, 4):
                    link(v.scalar_tensor_tensor(out=onehot, in0=iota, scalar=idx[:, k:k + 1], in1=onehot,
                                                op0=ALU.is_equal, op1=ALU.add))
                dve.wait_ge(e_ready, 2 * t + 2)
                link(v.tensor_scalar(den, zsum, TOP_EPS, top4, ALU.mult, ALU.add))
                link(v.reciprocal(rr, den))
                v.scalar_tensor_tensor(out=coeff, in0=eexp, scalar=rr, in1=onehot, op0=ALU.mult, op1=ALU.mult) \
                    .then_inc(coeff_ready, 1)
                dve.wait_ge(c_ps, t + 1)
                v.tensor_copy(c_tok[:, t % 2, :], psO[:, 2 * P:2 * P + NB]).then_inc(c_ready, 1)

            router(0)
            dve.wait_ge(c_ready, 1)
            for t in range(NT + 2):
                b = t % 2
                if t < NT:
                    for j in range(2):
                        p = 3 * t + j
                        dve.wait_ge(tanh_ready, p + 1)
                        link(v.scalar_tensor_tensor(out=act0[:, p % 2, :], in0=th0[:, p % 2, :], scalar=1.0,
                                                    in1=psS[:, 2 * (p % 2), :], op0=ALU.add, op1=ALU.mult))
                        if t >= 2 and j == 0:
                            dve.wait_ge(basis_sum, t - 1)
                        for k in range(4):
                            kk = 4 * j + k
                            ins = v.scalar_tensor_tensor(
                                out=basis[:, b, kk, :], in0=act0[:, p % 2, k * P:(k + 1) * P],
                                scalar=c_tok[:, b, kk:kk + 1], in1=psS[:, 2 * (p % 2) + 1, k * P:(k + 1) * P],
                                op0=ALU.mult, op1=ALU.mult)
                        ins.then_inc(pair_used, 1)
                    p = 3 * t + 2
                    dve.wait_ge(tanh_ready, p + 1)
                    link(v.scalar_tensor_tensor(out=act0[:, p % 2, 0:E], in0=th0[:, p % 2, 0:E], scalar=1.0,
                                                in1=psS[:, 2 * (p % 2), 0:E], op0=ALU.add, op1=ALU.mult))
                    if t >= 2:
                        dve.wait_ge(mix_T, t - 1)
                    v.tensor_tensor(mcat[:, b, P:3 * P], act0[:, p % 2, 0:E], psS[:, 2 * (p % 2), E:2 * E],
                                    ALU.mult).then_inc(pair_used, 1)
                if 1 <= t <= NT:
                    bb = (t - 1) % 2
                    dve.wait_ge(mix_hi, t)
                    v.tensor_tensor(mcT[:, bb, 1, :], psT[:, bb, 0:384], mcT[:, bb, 0, :], ALU.subtract) \
                        .then_inc(mix_lo, 1)
                if t + 1 < NT:
                    router(t + 1)
                    dve.wait_ge(c_ready, t + 2)
                if 2 <= t:
                    h_low(2 * NT + t - 2)
                if 1 <= t <= NT:
                    residual(2 * NT + t - 1, psM[:, 0:E], 0, 1, down_ps, t)
                    xn_later(2 * NT + t - 1)
            for k in range(KE):
                dve.wait_ge(w_hi, 8 + k)
                v.tensor_tensor(w1a[:, 1, k, :], w1a_f[:, k, :], w1a[:, 0, k, :], ALU.subtract).then_inc(w_lo, 1)
            dve.wait_ge(loaded["b1a"], 16)
            dve.wait_ge(loaded["rope"], 32)

            def score_products(t):
                b = t % 2
                dve.wait_ge(qkv_ps, t + 1)
                if t >= 2:
                    dve.wait_ge(prod2_ready, t - 1)
                link(v.tensor_tensor(qkb[:, b, :], psS[:, b, :], b1a[:, 0:2 * E], ALU.add))
                v.tensor_tensor(vb[:, b, :], psS[:, 2 + b, 0:E], b1a[:, 2 * E:3 * E], ALU.add).then_inc(qkv_read, 1)
                heads = 2 * H1
                q4 = qkb[:, b, :].rearrange("p (h d c) -> p h d c", h=heads, c=2)
                b4 = ropeB.rearrange("p (h d c) -> p h d c", h=heads, c=2)
                cos = ropeC[:, t, :].unsqueeze(1).to_broadcast([P, heads, D1])
                sin = ropeS[:, t, :].rearrange("p (d c) -> p d c", c=2)
                link(v.tensor_tensor(ropeA.rearrange("p (h d) -> p h d", h=heads),
                                     qkb[:, b, :].rearrange("p (h d) -> p h d", h=heads), cos, ALU.mult))
                for c in range(2):
                    link(v.tensor_tensor(b4[:, :, :, c], q4[:, :, :, 1 - c],
                                         sin[:, :, c].unsqueeze(1).to_broadcast([P, heads, D1 // 2]), ALU.mult))
                v.tensor_tensor(qkr[:, b, :], ropeA, ropeB, ALU.add).then_inc(qkr_ready, 1)
                dve.wait_ge(qkr_ready, t + 1)
                if t >= 2:
                    dve.wait_ge(s_sum, t - 1)
                v.tensor_tensor(prod1[:, b, :].rearrange("p (d h t) -> p d h t", d=D1, h=H1),
                                qkr[:, b, 0:E].rearrange("p (h d) -> p d h", h=H1).unsqueeze(3)
                                .to_broadcast([P, D1, H1, H1]),
                                qkr[:, b, E:2 * E].rearrange("p (t d) -> p d t", t=H1).unsqueeze(2)
                                .to_broadcast([P, D1, H1, H1]), ALU.mult).then_inc(prod1_ready, 1)

            def softmax_in(t):
                dve.wait_ge(s_sum, t + 1)
                ps = psT[:, t % 2, 0:256].rearrange("p (h t) -> p h t", h=H1)
                link(v.tensor_reduce(m1[:, t % 2, :], ps, AX.X, ALU.max))
                if t >= 1:
                    dve.wait_ge(e1_ready, t)
                v.tensor_tensor(ssub.rearrange("p (h t) -> p h t", h=H1), ps,
                                m1[:, t % 2, :].unsqueeze(2).to_broadcast([P, H1, H1]), ALU.subtract) \
                    .then_inc(sub_ready, 1)

            def weighted(t):
                b = t % 2
                dve.wait_ge(e1_ready, t + 1)
                link(v.tensor_reduce(s1, e1[:, b, :].rearrange("p (h t) -> p h t", h=H1), AX.X, ALU.add))
                link(v.reciprocal(r1, s1))
                dve.wait_ge(prod2_ready, t + 1)
                v.tensor_reduce(avr, prod2.rearrange("p (h t) -> p h t", t=H1), AX.X, ALU.add).then_inc(prod2_used, 1)
                dve.wait_ge(prod2_used, t + 1)
                if t >= 2:
                    dve.wait_ge(shuffled[t - 2], 16)
                v.tensor_tensor(av[:, b, :].rearrange("p (h d) -> p h d", h=H1),
                                avr.rearrange("p (h d) -> p h d", h=H1),
                                r1.unsqueeze(2).to_broadcast([P, H1, D1]), ALU.mult).then_inc(av_ready, 1)

            for t in range(NT + 2):
                if t < NT:
                    score_products(t)
                if t >= 2:
                    weighted(t - 2)
                if 1 <= t <= NT:
                    softmax_in(t - 1)
            for t in range(NT + 2):
                if t < NT:
                    dve.wait_ge(a_hi, t + 1)
                    v.tensor_tensor(aT[:, t % 2, 1, :], psT[:, t % 2, 0:E], aT[:, t % 2, 0, :], ALU.subtract) \
                        .then_inc(a_lo, 1)
                    dve.wait_ge(o_ps, t + 1)
                    link(v.tensor_tensor(ytmp, psM[:, 0:E], b1a[:, 3 * E:4 * E], ALU.add))
                    link(v.tensor_tensor(ytmp, ytmp, gates[:, 1, 0, :], ALU.mult))
                    link(v.tensor_tensor(x[:, t, :], x[:, t, :], ytmp, ALU.add))
                    q = 3 * NT + t
                    link(v.bn_stats(st[:, q % 2, :], x[:, t, :]))
                    link(v.bn_aggr(mv2[:, q % 2, :], st[:, q % 2, :]))
                    v.tensor_scalar(ve[:, q % 2:q % 2 + 1], mv2[:, q % 2, 1:2], LN_EPS, None, ALU.add) \
                        .then_inc(var_ready, 1)
                    xn_later(q)
                if 1 <= t <= NT:
                    h_low(3 * NT + t - 1)
            dve.wait_ge(gate_ps, NT)
            dve.wait_ge(loaded["gw"], 48)
            link(v.tensor_copy(g_s, psO[:, 0:NT * NE]))
            v.scalar_tensor_tensor(out=g_a, in0=g_s, scalar=-1.0, in1=g_s, op0=ALU.mult, op1=ALU.max) \
                .then_inc(gabs, 1)
            dve.wait_ge(gexp, 1)
            v.tensor_scalar(g_a, g_b, 1.0, None, ALU.add).then_inc(gabs, 1)
            dve.wait_ge(gabs, 2)
            link(v.tensor_scalar(g_m, g_a, -1.0, None, ALU.add))
            link(v.tensor_scalar(g_x, g_m, 0.0, None, ALU.is_equal))
            link(v.tensor_tensor(g_m, g_m, g_x, ALU.add))
            link(v.reciprocal(g_i, g_m))
            dve.wait_ge(gexp, 2)
            link(v.tensor_tensor(g_c, g_c, g_x, ALU.add))
            link(v.tensor_tensor(g_c, g_c, g_b, ALU.mult))
            link(v.tensor_tensor(g_c, g_c, g_i, ALU.mult))
            v.scalar_tensor_tensor(out=g_c, in0=g_s, scalar=0.0, in1=g_c, op0=ALU.max, op1=ALU.add) \
                .then_inc(sp_ready, 1)
            dve.wait_ge(sq_ready, 1)

            def tiles(a):
                return a.rearrange("p (t e) -> p t e", t=NT)

            link(v.tensor_tensor(tiles(g_x), tiles(g_r), gbB.unsqueeze(1).to_broadcast([P, NT, NE]), ALU.add))
            for t in range(NT):
                e8 = slice(t * NE, (t + 1) * NE)
                link(v.max(g_m[:, e8], g_x[:, e8]))
                link(v.max_index(g_u[:, e8], g_m[:, e8], g_x[:, e8]))
            link(v.tensor_copy(g_i, g_u))
            eq = (tiles(g_a), tiles(g_b))
            for k in range(2):
                link(v.tensor_tensor(eq[k], iota1.unsqueeze(1).to_broadcast([P, NT, NE]),
                                     tiles(g_i)[:, :, k:k + 1].to_broadcast([P, NT, NE]), ALU.is_equal))
            link(v.tensor_tensor(g_a, g_a, g_b, ALU.add))
            link(v.scalar_tensor_tensor(out=cw, in0=tiles(g_r), scalar=0.5, in1=tiles(g_a),
                                        op0=ALU.mult, op1=ALU.mult))
            for t in range(NT + 1):
                b = t % 2
                if t < NT:
                    for j in range(NCH):
                        p = NCH * t + j
                        w = 2 * INTER if j < NCH - 1 else INTER
                        dve.wait_ge(chunk_tanh, p + 1)
                        link(v.scalar_tensor_tensor(out=a1[:, p % 2, 0:w], in0=th1[:, p % 2, 0:w], scalar=1.0,
                                                    in1=psS[:, 2 * (p % 2), 0:w], op0=ALU.add, op1=ALU.mult))
                        if t >= 2 and j == 0:
                            dve.wait_ge(hc_T, 4 * (t - 1))
                        for m in range(w // INTER):
                            e = 2 * j + m
                            lo = m * INTER
                            ins = v.scalar_tensor_tensor(
                                out=hc[:, b, e * INTER:(e + 1) * INTER], in0=a1[:, p % 2, lo:lo + INTER],
                                scalar=cw[:, t, e:e + 1] if e < NE else 0.5,
                                in1=psS[:, 2 * (p % 2) + 1, lo:lo + INTER], op0=ALU.mult, op1=ALU.mult)
                        ins.then_inc(chunk_used, 1)
                if t >= 1:
                    for c in range(4):
                        m = 4 * (t - 1) + c
                        w = 4 if c < 3 else 1
                        rows_ = P if c < 3 else HID - 12 * P
                        dve.wait_ge(hc_hi, m + 1)
                        o = c * 512
                        v.tensor_tensor(hcT[0:rows_, 1 - b, 1, o:o + w * P], psT[0:rows_, m % 2, 0:w * P],
                                        hcT[0:rows_, 1 - b, 0, o:o + w * P], ALU.subtract).then_inc(hc_lo, 1)
                    residual(t - 1, psO[:, 0:E], 1, 1, moe_ps, t, last=True)

        @block.tensor
        def _(pe):
            te = nc.tensor

            def mm(out_, lhsT, rhs, start, stop):
                return te.matmul(out_, lhsT=lhsT, rhs=rhs, start=start, stop=stop)

            def three(out_, a_hi_, a_lo_, b_hi_, b_lo_, first, last):
                mm(out_, a_hi_, b_hi_, first, False)
                mm(out_, a_hi_, b_lo_, False, False)
                return mm(out_, a_lo_, b_hi_, False, last)

            def modulation(j):
                layer, third = MOD[j]
                if j:
                    pe.wait_ge(mod_done, j)
                for k in range(KE):
                    ins = mm(psO[:, :], csB[:, 2 * layer + k, :], wmod[:, layer, k, third * 512:third * 512 + 512],
                             k == 0, k == KE - 1)
                ins.then_inc(mod_ps, 1)
                pe.wait_ge(mod_rows, j + 1)
                for b in range(4 if third == 0 else 2):
                    ins = te.transpose(psM[:, b * P:(b + 1) * P], modrow[:, b * P:(b + 1) * P], ident[:, :])
                ins.then_inc(mod_T, 1)

            def norm_T(q, ps):
                pe.wait_ge(xn_ready, q + 1)
                for k in range(KE):
                    ins = te.transpose(ps[:, k * P:(k + 1) * P], xn[:, q % 2, k * P:(k + 1) * P], ident[:, :])
                ins.then_inc(xn_T, 1)

            def h_out(q):
                return 2 * NT + 4 * (q - NT + 1)

            pe.wait_ge(cond_rows, 1)
            pe.wait_ge(loaded["wmod0a"], 16)
            pe.wait_ge(loaded["ident"], 16)
            modulation(0)
            for i in range(NT):
                if i >= 2:
                    pe.wait_ge(hT_ready, 2 * (i - 1))
                norm_T(i, psT[:, i % 2, :])
            pe.wait_ge(loaded["wkv"], 16)
            for m in range(len(proj)):
                kind, a, b = proj[m]
                if m == NKV:
                    pe.wait_ge(loaded["wq"], 16)
                if m >= 4:
                    if m - 4 < NKV:
                        pe.wait_ge(tmp_ready, m - 3)
                    else:
                        pe.wait_ge(q_ready, m - 3 - NKV)
                if kind == "k":
                    pe.wait_ge(hT_ready, 2 * 4 * (b + 1))
                if kind == "v":
                    pe.wait_ge(hT_ready, 2 * (a + 1))
                for k in range(KE):
                    if kind == "k":
                        lhsT, rhs = wkv[:, k, 2 * a * P:(2 * a + 1) * P], hT[:, k, b * 512:(b + 1) * 512]
                    elif kind == "v":
                        lhsT = hT[:, k, a * P:(a + 1) * P]
                        rhs = wkv[:, k, :].rearrange("p (g c n) -> p g c n", g=NG, c=2)[:, :, 1, :]
                    else:
                        lhsT, rhs = wq[:, k, a * P:(a + 1) * P], hT[:, k, b * 512:(b + 1) * 512]
                    ins = mm(psS[:, m % 4, :], lhsT, rhs, k == 0, k == KE - 1)
                ins.then_inc(proj_done, 1)
            pe.wait_ge(loaded["wmod0b"], 16)
            pe.wait_ge(loaded["wmod1"], 16)
            for j in range(1, 6):
                modulation(j)

            pe.wait_ge(q_ready, 2 * HQ)
            pe.wait_ge(masks_ready, 1)
            pe.wait_ge(mod_done, 6)
            nt = [0]
            for st_ in range(NU + 13):
                if st_ < NU:
                    u = st_
                    i, h = unit(u)
                    if u < NKV:
                        pe.wait_ge(tmp_used, NKV)
                    if u >= 2:
                        pe.wait_ge(exp_done, u - 1)
                    w = (i + 1) * P
                    for c in range(0, w, 512):
                        cw_ = min(512, w - c)
                        bank = psS[:, 2 * (u % 2) + c // 512, :]
                        diag = c + cw_ == w
                        ins = mm(bank[:, 0:cw_], qT[:, i, h, :], kT[:, h // QPG, c:c + cw_], True, not diag)
                        if diag:
                            ins = mm(bank[:, cw_ - P:cw_], ident_b[:, :], mask_b[:, :], False, True)
                    ins.then_inc(scores, 1)
                if LAG <= st_ < NU + LAG:
                    u = st_ - LAG
                    i, h = unit(u)
                    pe.wait_ge(normed, u + 1)
                    for c, k in chunks(i):
                        if nt[0] >= 2:
                            pe.wait_ge(pT_lo, nt[0] - 1)
                        for b in range(k):
                            ins = te.transpose(psT[:, nt[0] % 2, b * P:(b + 1) * P],
                                               probs[:, u % 4, (c + b) * P:(c + b + 1) * P], ident[:, :])
                        ins.then_inc(pT_ps, 1)
                        nt[0] += 1
                G, part = (st_ - 7) // QPG, (st_ - 7) % QPG
                if 0 <= G < NGR:
                    i, g_ = G // NG, G % NG
                    if part == 0:
                        pe.wait_ge(pT_lo, chunk_end[QPG * G + QPG - 1])
                        if G >= 1:
                            pe.wait_ge(oT_lo, G)
                    vs = slice(g_ * P, (g_ + 1) * P)
                    products = [(j, *vp) for j in range(i + 1) for vp in ((0, 0), (0, 1), (1, 0))]
                    n_ = len(products)
                    for m in range(part * n_ // QPG, (part + 1) * n_ // QPG):
                        j, wv, wp = products[m]
                        ins = mm(psO[:, :], v_hl[:, wv, j, vs],
                                 pT[:, G % 2, wp, j, :, :].rearrange("p h n -> p (h n)"), m == 0, m == n_ - 1)
                    if part == QPG - 1:
                        ins.then_inc(pv, 1)
                i, part = (st_ - 21) // HQ, (st_ - 21) % HQ
                if 0 <= i < NT and part < NG:
                    pe.wait_ge(oT_lo, NG * i + part + 1)
                    if part == 0:
                        if i == 0:
                            pe.wait_ge(wo_lo, 4)
                        else:
                            pe.wait_ge(hT_ready, h_out(NT + i - 1))
                    for h in range(part * QPG, (part + 1) * QPG):
                        ins = three(psM[:, 0:E], oT[:, 0, h, :], oT[:, 1, h, :], wo_hl[:, 0, h, :], wo_hl[:, 1, h, :],
                                    h == 0, h == HQ - 1)
                    if part == NG - 1:
                        ins.then_inc(wo_done, 1)
                if st_ >= 27 and (st_ - 27) % HQ == 0:
                    norm_T(NT + (st_ - 27) // HQ, psM[:, 256:512])

            pe.wait_ge(w_lo, 7)
            pe.wait_ge(loaded["wr"], 16)

            def logits(t):
                pe.wait_ge(hT_ready, h_out(NT + t))
                if t >= 1:
                    pe.wait_ge(c_ready, t)
                for k in range(KE):
                    ins = mm(psO[:, 0:P], hT[:, k, t * P:(t + 1) * P], wr[:, k, :], k == 0, k == KE - 1)
                ins.then_inc(logit_ps, 1)

            def basis_weights(t):
                pe.wait_ge(coeff_ready, t + 1)
                te.transpose(psO[:, P:2 * P], coeff, ident[:, :]).then_inc(coT_ps, 1)
                pe.wait_ge(coT_ready, t + 1)
                mm(psO[:, 2 * P:2 * P + NB], coeffT, mixs[:, :], True, True).then_inc(c_ps, 1)

            logits(0)
            basis_weights(0)
            for t in range(NT + 2):
                if t + 1 < NT:
                    logits(t + 1)
                if t < NT:
                    pe.wait_ge(hlo_ready, t + 1)
                    ts_ = slice(t * P, (t + 1) * P)
                    for j in range(3):
                        p = 3 * t + j
                        if p >= 2:
                            pe.wait_ge(pair_used, p - 1)
                        for m in range(2 if j < 2 else 1):
                            for k in range(KE):
                                if j < 2:
                                    wh, wl = (wgu[:, w_, m, k, j * 512:(j + 1) * 512] for w_ in range(2))
                                else:
                                    wh, wl = (wsh[:, w_, k, :] for w_ in range(2))
                                ins = three(psS[:, 2 * (p % 2) + m, :], h_hl[:, 0, k, ts_], h_hl[:, 1, k, ts_],
                                            wh, wl, k == 0, k == KE - 1)
                        ins.then_inc(pair_ps, 1)
                if t >= 2:
                    norm_T(2 * NT + t - 2, psM[:, 256:512])
                if 1 <= t <= NT:
                    b = (t - 1) % 2
                    pe.wait_ge(basis_sum, t)
                    pe.wait_ge(pair_used, 3 * t)
                    if t >= 3:
                        pe.wait_ge(mix_lo, t - 2)
                    for c in range(3):
                        ins = te.transpose(psT[:, b, c * P:(c + 1) * P], mcat[:, b, c * P:(c + 1) * P], ident[:, :])
                    ins.then_inc(mix_T, 1)
                if t + 1 < NT:
                    basis_weights(t + 1)
                if 1 <= t <= NT:
                    pe.wait_ge(mix_lo, t)
                    pe.wait_ge(hT_ready, h_out(NT + NT + t - 2))
                    for c in range(3):
                        cs_ = slice(c * P, (c + 1) * P)
                        ins = three(psM[:, 0:E], mcT[:, b, 0, cs_], mcT[:, b, 1, cs_], wdn[:, 0, c, :], wdn[:, 1, c, :],
                                    c == 0, c == 2)
                    ins.then_inc(down_ps, 1)

            pe.wait_ge(w_lo, 9)

            def qkv(t):
                pe.wait_ge(hlo_ready, NT + t + 1)
                if t >= 2:
                    pe.wait_ge(qkv_read, t - 1)
                ts_ = slice(t * P, (t + 1) * P)
                for bank, c0, c1 in ((t % 2, 0, 2 * E), (2 + t % 2, 2 * E, 3 * E)):
                    for k in range(KE):
                        ins = three(psS[:, bank, 0:c1 - c0], h_hl[:, 0, k, ts_], h_hl[:, 1, k, ts_],
                                    w1a[:, 0, k, c0:c1], w1a[:, 1, k, c0:c1], k == 0, k == KE - 1)
                ins.then_inc(qkv_ps, 1)

            qkv(0)
            for t in range(NT):
                if t + 1 < NT:
                    qkv(t + 1)
                pe.wait_ge(prod1_ready, t + 1)
                if t >= 2:
                    pe.wait_ge(sub_ready, t - 1)
                for k in range(D1):
                    ins = mm(psT[:, t % 2, 0:H1 * H1], ident[:, :], prod1[:, t % 2, k * 256:(k + 1) * 256],
                             k == 0, k == D1 - 1)
                ins.then_inc(s_sum, 1)
            pe.wait_ge(loaded["mixed"], 32)
            pe.wait_ge(loaded["gw"], 48)
            for t in range(NT + 1):
                b = t % 2
                if t < NT:
                    if t >= 2:
                        pe.wait_ge(a_lo, t - 1)
                    for k in range(KE):
                        ins = te.transpose(psT[:, b, k * P:(k + 1) * P], mixed_rows[:, t, k * P:(k + 1) * P],
                                           ident[:, :])
                    ins.then_inc(a_T, 1)
                if t >= 1:
                    norm_T(3 * NT + t - 1, psM[:, 256:512])
                if t < NT:
                    pe.wait_ge(a_lo, t + 1)
                    pe.wait_ge(hT_ready, h_out(3 * NT + t - 1))
                    for k in range(KE):
                        ks = slice(k * P, (k + 1) * P)
                        ins = three(psM[:, 0:E], aT[:, b, 0, ks], aT[:, b, 1, ks], w1a[:, 0, k, 3 * E:4 * E],
                                    w1a[:, 1, k, 3 * E:4 * E], k == 0, k == KE - 1)
                    ins.then_inc(o_ps, 1)
                if t >= 1:
                    pe.wait_ge(hT_ready, h_out(3 * NT + t - 1))
                    for k in range(KE):
                        ins = mm(psO[:, (t - 1) * NE:t * NE], hT[:, k, (t - 1) * P:t * P], gwf[:, k, :],
                                 k == 0, k == KE - 1)
                    ins.then_inc(gate_ps, 1)
            for n_, m in (("w1", 16), ("w3", 16), ("w2", 32)):
                pe.wait_ge(loaded[n_], m)
            for t in range(NT + 1):
                if t < NT:
                    pe.wait_ge(hlo_ready, 2 * NT + t + 1)
                    ts_ = slice(t * P, (t + 1) * P)
                    for j in range(NCH):
                        p = NCH * t + j
                        w = 2 * INTER if j < NCH - 1 else INTER
                        if p >= 2:
                            pe.wait_ge(chunk_used, p - 1)
                        for m, wt in enumerate((w1b, w3b)):
                            for k in range(KE):
                                wcol = wt[:, k, 2 * INTER * j:2 * INTER * j + w]
                                mm(psS[:, 2 * (p % 2) + m, 0:w], h_hl[:, 0, k, ts_], wcol, k == 0, False)
                                ins = mm(psS[:, 2 * (p % 2) + m, 0:w], h_hl[:, 1, k, ts_], wcol, False, k == KE - 1)
                        ins.then_inc(chunk_ps, 1)
                if t >= 1:
                    b = (t - 1) % 2
                    pe.wait_ge(chunk_used, NCH * t)
                    for c in range(4):
                        m = 4 * (t - 1) + c
                        if m >= 2:
                            pe.wait_ge(hc_lo, m - 1)
                        for e in range(4 * c, min(4 * c + 4, KH)):
                            w = min(P, HID - e * P)
                            ins = te.transpose(psT[0:w, m % 2, (e % 4) * P:(e % 4 + 1) * P], hc[:, b, e * P:e * P + w],
                                               ident[:, :])
                        ins.then_inc(hc_T, 1)
                    pe.wait_ge(hc_lo, 4 * t)
                    pe.wait_ge(gabs, 1)
                    if t >= 2:
                        pe.wait_ge(x_out, t - 1)
                    for e in range(KH):
                        w = min(P, HID - e * P)
                        for w_ in range(2):
                            ins = mm(psO[:, 0:E], hcT[0:w, b, w_, e * P:(e + 1) * P], w2b[0:w, e, :],
                                     e == 0 and w_ == 0, e == KH - 1 and w_ == 1)
                    ins.then_inc(moe_ps, 1)


_INS = ["x", "cs", "wmod0", "wmod1", "wq", "bq", "wkv", "bk", "bv", "wo", "peT", "ident", "mask", "iota",
        "wr", "wg", "wu", "wd", "swg", "swu", "swd", "amp", "escale", "w1a", "b1a", "ropeC", "ropeS",
        "gw", "gb", "w1", "w3", "w2"]


def kernel(**inputs):
    import numpy as np
    import concourse.bacc as bacc
    from concourse.bass_utils import run_bass_kernel_spmd

    a = {k: np.asarray(v) for k, v in inputs.items()}
    f32 = np.float32
    S, E, D = 1024, 256, 128
    pos = np.arange(S, dtype=f32)[:, None]
    inv = np.exp(-(np.log(f32(10000.0)) * np.arange(0, D, 2, dtype=f32) / f32(D))).astype(f32)
    ang = (pos * inv).astype(f32)
    pe = np.zeros((S, D), f32)
    pe[:, 0::2], pe[:, 1::2] = np.sin(ang), np.cos(ang)
    inv1 = (f32(1.0) / f32(10000.0) ** (np.arange(0, 16, 2, dtype=f32) / f32(16))).astype(f32)
    fr = (pos * inv1).astype(f32)
    cos = np.repeat(np.cos(fr), 2, axis=1).reshape(8, 128, 16).transpose(1, 0, 2)
    sin = np.stack([-np.sin(fr), np.sin(fr)], -1).reshape(8, 128, 16).transpose(1, 0, 2)
    bkv = a["L0_attn_bkv"].reshape(4, 2, 128)
    d = {
        "x": a["L0_attn_x"].reshape(S, E),
        "cs": np.concatenate([a["L0_c"].reshape(2, 128), a["L1_c"].reshape(2, 128)]).T,
        "wmod0": a["L0_wmod"], "wmod1": a["L1_wmod"],
        "wq": a["L0_attn_wq"], "bq": a["L0_attn_bq"].reshape(16, 128).T,
        "wkv": a["L0_attn_wkv"], "bk": bkv[:, 0].T, "bv": bkv[:, 1].reshape(1, 512),
        "wo": a["L0_attn_wo"], "peT": pe.T, "ident": np.eye(128, dtype=f32),
        "mask": np.triu(np.full((128, 128), -1e30, f32), 1), "iota": np.arange(128, dtype=f32)[None],
        "wr": a["L0_ffn_w_router"], "wg": a["L0_ffn_w_gate"], "wu": a["L0_ffn_w_up"], "wd": a["L0_ffn_w_down"],
        "swg": a["L0_ffn_shared_w_gate"], "swu": a["L0_ffn_shared_w_up"], "swd": a["L0_ffn_shared_w_down"],
        "amp": a["L0_ffn_amplitudes"].reshape(128, 16), "escale": a["L0_ffn_expert_scale"].reshape(128, 1),
        "w1a": np.concatenate([a[f"L1_attn_W{n}"].T for n in "qkvo"], axis=1),
        "b1a": np.concatenate([a[f"L1_attn_b{n}"] for n in "qkvo"])[None],
        "ropeC": cos.reshape(128, 128), "ropeS": sin.reshape(128, 128),
        "gw": a["L1_ffn_gate_w"].T, "gb": a["L1_ffn_gate_b"].reshape(1, 8),
        "w1": np.concatenate([a["L1_ffn_w1"].reshape(1408, 256), a["L1_ffn_sw1"]]).T,
        "w3": np.concatenate([a["L1_ffn_w3"].reshape(1408, 256), a["L1_ffn_sw3"]]).T,
        "w2": np.concatenate([a["L1_ffn_w2"].transpose(0, 2, 1).reshape(1408, 256), a["L1_ffn_sw2"].T]),
    }
    nc = bacc.Bacc("TRN2", target_bir_lowering=False, num_devices=1)
    arrays, aps = {}, {}
    for name in _INS:
        v = np.ascontiguousarray(d[name])
        arrays[f"in_{name}"] = v
        aps[name] = nc.dram_tensor(f"in_{name}", v.shape, mybir.dt.from_np(v.dtype), kind="ExternalInput").ap()
    out = nc.dram_tensor("out", (S, E), F32, kind="ExternalOutput").ap()
    build_program(nc, aps, out)
    r = run_bass_kernel_spmd(nc, [arrays], core_ids=[0])
    return r.results[0]["out"].reshape(1, S, E)
```

```python
from contextlib import ExitStack

import concourse.bass as bass
from concourse import mybir

P = 128
F32 = mybir.dt.float32
BF16 = mybir.dt.bfloat16
U32 = mybir.dt.uint32
ALU = mybir.AluOpType
ACT = mybir.ActivationFunctionType
AX = mybir.AxisListType

LN_EPS = 1e-5
TOP_EPS = 1e-8
GATE_FLOOR = 0.25


def build_program(nc, d, out):
    S, E = d["x"].shape
    NT = S // P
    KE = E // P
    HQ = d["wq"].shape[1] // P
    NG = d["wkv"].shape[1] // (2 * P)
    QPG = HQ // NG
    NU = NT * HQ
    NGR = NT * NG
    NB = 8
    NX = d["wr"].shape[1]
    H1, D1 = 16, E // 16
    INTER, NE = 176, 8
    HID = INTER * (NE + 1)
    KH = -(-HID // P)
    SCALE0 = float(P) ** -0.5
    SCALE1 = float(D1) ** -0.5
    LAG = 3

    with ExitStack() as ctx:
        def sb(name, shape, dt=F32):
            return ctx.enter_context(nc.sbuf_tensor(name, shape, dt))

        def sem(name):
            return ctx.enter_context(nc.semaphore(name))

        x = sb("x", [P, NT, E])
        hT = sb("hT", [P, KE, S])
        wq_region = sb("wq_region", [P, KE * HQ * P])
        wkv_region = sb("wkv_region", [P, KE * 2 * NG * P])
        q_region = sb("q_region", [P, NT * HQ * P])
        k_region = sb("k_region", [P, NG * S])
        v_region = sb("v_region", [P, NT * NG * P])
        pt_region = sb("pt_region", [P, 8192])
        wo_region = sb("wo_region", [P, HQ * E])
        peT = sb("peT", [P, S])
        bvB = sb("bvB", [P, NG * P])
        xn = sb("xn", [P, 2, E])
        tmp = sb("tmp", [P, 2, 512])
        gates = sb("gates", [P, 2, 2, E])
        modcol = sb("modcol", [P, 2, 8])
        ident = sb("ident", [P, P])
        ident_b = sb("ident_b", [P, P], BF16)
        mask_b = sb("mask_b", [P, P], BF16)
        mask_f = sb("mask_f", [P, P])
        csB = sb("csB", [P, 4, P])
        half = sb("half", [P, NT * NE])
        c_tok = sb("c_tok", [P, NT, NB])
        cs = sb("cs", [P, 4])
        cth = sb("cth", [P, 4])
        bq = sb("bq", [P, HQ])
        bk = sb("bk", [P, NG])
        mhalf = sb("mhalf", [P, NT])
        mv = sb("mv", [P, NT, 2])
        st = sb("st", [P, 2, 6])
        mv2 = sb("mv2", [P, 2, 2])
        ve = sb("ve", [P, 2])
        rstd = sb("rstd", [P, 2])
        ve0 = sb("ve0", [P, NT])
        rstd0 = sb("rstd0", [P, NT])
        negmax = sb("negmax", [P, 4])
        rowsum = sb("rowsum", [P, 4])
        rinv = sb("rinv", [P, 4])
        mixs = sb("mixs", [P, NB])
        small = sb("small", [P, 64])

        wq = wq_region[:, :].rearrange("p (k n) -> p k n", k=KE)
        wkv = wkv_region[:, :].rearrange("p (k n) -> p k n", k=KE)
        probs = wq_region[:, :].rearrange("p (r n) -> p r n", r=4)
        oT = wkv_region[:, :].bitcast(BF16).rearrange("p (w h n) -> p w h n", w=2, h=HQ)
        qT = q_region[:, :].rearrange("p (t h n) -> p t h n", t=NT, h=HQ)
        kT = k_region[:, :].rearrange("p (g n) -> p g n", g=NG)
        v_hl = v_region[:, :].bitcast(BF16).rearrange("p (w t n) -> p w t n", w=2, t=NT)
        pT = pt_region[:, :].bitcast(BF16).rearrange("p (b w j h n) -> p b w j h n", b=2, w=2, j=NT, h=QPG)
        wo_hl = wo_region[:, :].bitcast(BF16).rearrange("p (w h n) -> p w h n", w=2, h=HQ)
        wmod = pt_region[:, 0:2 * KE * 6 * E].rearrange("p (l k n) -> p l k n", l=2, k=KE)
        wo_stage = pt_region[:, 2 * KE * 6 * E:8192].rearrange("p (b h n) -> p b h n", b=2, h=4)
        modrow = xn[:, :, :].rearrange("p a n -> p (a n)")

        def slot(a, b):
            w = HQ * P
            return q_region[:, a * w:b * w]

        h_hl = slot(0, 1).bitcast(BF16).rearrange("p (w k n) -> p w k n", w=2, k=KE)
        wgu_f = slot(1, 3).rearrange("p (m k n) -> p m k n", m=2, k=KE)
        wr = peT[:, 0:KE * NX].rearrange("p (k n) -> p k n", k=KE)
        wsh_f = slot(3, 4)[:, 256:256 + 1024].rearrange("p (k n) -> p k n", k=KE)
        wdn_f = slot(3, 4)[:, 1280:1280 + 768].rearrange("p (k n) -> p k n", k=3)
        wgu = slot(4, 6).bitcast(BF16).rearrange("p (w m k n) -> p w m k n", w=2, m=2, k=KE)
        wsh = slot(6, 7)[:, 0:1024].bitcast(BF16).rearrange("p (w k n) -> p w k n", w=2, k=KE)
        wdn = slot(6, 7)[:, 1024:1792].bitcast(BF16).rearrange("p (w k n) -> p w k n", w=2, k=3)
        sc = pt_region
        th0 = sc[:, 0:1024].rearrange("p (b n) -> p b n", b=2)
        act0 = sc[:, 1024:2048].rearrange("p (b n) -> p b n", b=2)
        basis = sc[:, 2048:4096].rearrange("p (b k n) -> p b k n", b=2, k=NB)
        tree = wq_region[:, 0:768]
        mcat = wq_region[:, 768:1536].rearrange("p (b n) -> p b n", b=2)
        mcT = wq_region[:, 1536:2304].bitcast(BF16).rearrange("p (b w n) -> p b w n", b=2, w=2)
        logit, eexp, onehot, coeff = (bvB[:, m * P:(m + 1) * P] for m in range(4))
        iota, coeffT = csB[:, 0, :], csB[:, 1, :]
        w1b = k_region[:, 0:HID].bitcast(BF16).rearrange("p (k n) -> p k n", k=KE)
        w3b = k_region[:, HID:2 * HID].bitcast(BF16).rearrange("p (k n) -> p k n", k=KE)
        w2b = v_region[:, 0:KH * E // 2].bitcast(BF16).rearrange("p (k n) -> p k n", k=KH)
        w1a_f = v_region[:, 1664:1664 + KE * 4 * E].rearrange("p (k n) -> p k n", k=KE)
        w1a = wo_region[:, 0:KE * 4 * E].bitcast(BF16).rearrange("p (w k n) -> p w k n", w=2, k=KE)
        b1a = wo_region[:, 2048:2048 + 4 * E]
        ropeC = wo_region[:, 3072:3072 + NT * D1].rearrange("p (t n) -> p t n", t=NT)
        ropeS = wo_region[:, 3200:3200 + NT * D1].rearrange("p (t n) -> p t n", t=NT)
        gwf = wo_region[:, 3328:3328 + KE * NE].rearrange("p (k n) -> p k n", k=KE)
        gbB = wo_region[:, 3344:3344 + NE]
        iota1 = wo_region[:, 3352:3352 + NE]
        prod1 = slot(1, 5).rearrange("p (b n) -> p b n", b=2)
        prod2 = [wq_region[:, :], pt_region[:, 4096:8192]]
        qkb = slot(5, 6)[:, 0:1024].rearrange("p (b n) -> p b n", b=2)
        vb = slot(5, 6)[:, 1024:1536].rearrange("p (b n) -> p b n", b=2)
        ropeA = slot(6, 7)[:, 0:512]
        ropeB = slot(6, 7)[:, 512:1024]
        qkr = slot(6, 7)[:, 1024:2048].rearrange("p (b n) -> p b n", b=2)
        ssub = slot(7, 8)[:, 0:256]
        e1 = slot(7, 8)[:, 256:768].rearrange("p (b n) -> p b n", b=2)
        av = slot(7, 8)[:, 768:1280].rearrange("p (b n) -> p b n", b=2)
        avr = slot(7, 8)[:, 1280:1280 + 128]
        m1 = slot(7, 8)[:, 1536:1568].rearrange("p (b n) -> p b n", b=2)
        s1 = slot(7, 8)[:, 1568:1584]
        r1 = slot(7, 8)[:, 1584:1600]
        mixed_rows = pt_region[:, 0:NT * E].rearrange("p (t n) -> p t n", t=NT)
        aT = pt_region[:, 2048:2048 + 512].bitcast(BF16).rearrange("p (b w n) -> p b w n", b=2, w=2)
        ytmp = pt_region[:, 2560:2816]
        gbo = pt_region[:, 2816:3072]
        hc = slot(1, 3)[:, 0:2 * HID].rearrange("p (b n) -> p b n", b=2)
        hcT = slot(3, 5)[:, 0:2 * KH * P].bitcast(BF16).rearrange("p (b w n) -> p b w n", b=2, w=2)
        th1 = slot(5, 6)[:, 0:704].rearrange("p (b n) -> p b n", b=2)
        a1 = slot(5, 6)[:, 704:1408].rearrange("p (b n) -> p b n", b=2)
        cw = slot(6, 7)[:, 0:NT * NE].rearrange("p (t n) -> p t n", t=NT)
        g_s = slot(6, 7)[:, 256:320]
        g_a = slot(6, 7)[:, 320:384]
        g_b = slot(6, 7)[:, 384:448]
        g_c = slot(6, 7)[:, 448:512]
        g_m = slot(6, 7)[:, 512:576]
        g_x = slot(6, 7)[:, 576:640]
        g_i = slot(6, 7)[:, 640:704]
        g_u = slot(6, 7)[:, 704:768].bitcast(U32)
        g_r = slot(6, 7)[:, 768:832]

        psS = ctx.enter_context(nc.psum_tensor("psS", [P, 4, 512], F32))
        psT = ctx.enter_context(nc.psum_tensor("psT", [P, 2, 512], F32))
        psO = ctx.enter_context(nc.psum_tensor("psO", [P, 512], F32))
        psM = ctx.enter_context(nc.psum_tensor("psM", [P, 512], F32))
        scratch = nc.dram_tensor("head_shuffle", [H1, S, D1], F32, kind="Internal").ap()

        names_loaded = ["cs", "xa", "xb", "wmod0a", "wmod0b", "wmod1", "wkv", "wq", "peT", "bvB", "ident", "mask",
                        "bq", "bk", "wgu", "wr", "wsh", "wdn", "iota", "amp", "w1", "w3", "w2", "w1a", "b1a",
                        "rope", "gw", "mixed", "escale"]
        loaded = {n: sem("loaded_" + n) for n in names_loaded}
        wo_loaded = [sem(f"wo_loaded{c}") for c in range(4)]
        ve_chain = sem("vector_chain")
        ac_chain = sem("scalar_chain")
        po_chain = sem("pool_chain")
        cond_tanh = sem("cond_tanh")
        cond_rows = sem("cond_rows")
        mod_ps = sem("mod_ps")
        mod_rows = sem("mod_rows")
        mod_T = sem("mod_T")
        mod_done = sem("mod_done")
        var_ready = sem("var_ready")
        rstd_ready = sem("rstd_ready")
        xn_ready = sem("xn_ready")
        xn_T = sem("xn_T")
        hT_ready = sem("hT_ready")
        hlo_ready = sem("hlo_ready")
        proj_done = sem("proj_done")
        tmp_ready = sem("tmp_ready")
        tmp_used = sem("tmp_used")
        q_ready = sem("q_ready")
        vlo_ready = sem("vlo_ready")
        wo_hi = sem("wo_hi")
        wo_lo = sem("wo_lo")
        masks_ready = sem("masks_ready")
        scores = sem("scores")
        negmax_ready = sem("negmax_ready")
        exp_done = sem("exp_done")
        rinv_ready = sem("rinv_ready")
        normed = sem("normed")
        pT_ps = sem("pT_ps")
        pT_hi = sem("pT_hi")
        pT_lo = sem("pT_lo")
        pv = sem("pv")
        oT_hi = sem("oT_hi")
        oT_lo = sem("oT_lo")
        wo_done = sem("wo_done")
        res_read = sem("res_read")
        w_hi = sem("w_hi")
        w_lo = sem("w_lo")
        logit_ps = sem("logit_ps")
        neg_ready = sem("neg_ready")
        e_ready = sem("e_ready")
        coeff_ready = sem("coeff_ready")
        coT_ps = sem("coT_ps")
        coT_ready = sem("coT_ready")
        c_ps = sem("c_ps")
        c_ready = sem("c_ready")
        pair_ps = sem("pair_ps")
        tanh_ready = sem("tanh_ready")
        pair_used = sem("pair_used")
        basis_sum = sem("basis_sum")
        prod2b_ready = sem("prod2b_ready")
        av_ps = sem("av_ps")
        mix_T = sem("mix_T")
        mix_hi = sem("mix_hi")
        mix_lo = sem("mix_lo")
        down_ps = sem("down_ps")
        qkv_ps = sem("qkv_ps")
        qkv_read = sem("qkv_read")
        prod1_ready = sem("prod1_ready")
        s_sum = sem("s_sum")
        sub_ready = sem("sub_ready")
        e1_ready = sem("e1_ready")
        prod2_ready = sem("prod2_ready")
        prod2_used = sem("prod2_used")
        qkr_ready = sem("qkr_ready")
        av_ready = sem("av_ready")
        shuffled = [sem(f"shuffled{t}") for t in range(NT)]
        a_T = sem("a_T")
        a_hi = sem("a_hi")
        a_lo = sem("a_lo")
        o_ps = sem("o_ps")
        gate_ps = sem("gate_ps")
        gate_read = sem("gate_read")
        gexp = sem("gexp")
        gabs = sem("gabs")
        sp_ready = sem("sp_ready")
        sq_ready = sem("sq_ready")
        chunk_ps = sem("chunk_ps")
        chunk_tanh = sem("chunk_tanh")
        chunk_used = sem("chunk_used")
        hc_T = sem("hc_T")
        hc_hi = sem("hc_hi")
        hc_lo = sem("hc_lo")
        moe_ps = sem("moe_ps")
        x_out = sem("x_out")
        stored = sem("stored")

        def unit(u):
            return u // HQ, u % HQ

        def chunks(i):
            return [(c, min(4, i + 1 - c)) for c in range(0, i + 1, 4)]

        chunk_end = []
        for u in range(NU):
            chunk_end.append((chunk_end[-1] if u else 0) + len(chunks(unit(u)[0])))

        proj = [("k", g, n) for n in (0,) for g in range(NG)] + [("v", i, 0) for i in range(NT // 2)]
        proj += [("k", g, 1) for g in range(NG)] + [("v", i, 0) for i in range(NT // 2, NT)]
        NKV = len(proj)
        proj += [("q", h, n) for n in range(2) for h in range(HQ)]

        def expert_steps(st_):
            return [(st_ - NU - 6) // 3] if st_ >= NU + 6 and (st_ - NU - 6) % 3 == 0 else []

        NSTEP = NU + 20
        EXPERTS_LEFT = range(len([1 for n_ in range(NSTEP) if expert_steps(n_)]), NT + 2)

        def at(st_, first):
            i = (st_ - first) // HQ
            return i if st_ >= first and (st_ - first) % HQ == 0 and i < NT else None

        MOD = [(0, 0), (0, 1), (0, 2), (1, 0), (1, 1), (1, 2)]

        WSPLIT = [(NT - 1) * HQ + 1 + 2 * n_ for n_ in range(6)]
        HPE = 8
        HDV = 2
        NCH = NE // 2 + 1

        block = ctx.enter_context(nc.Block())

        @block.sync
        def _(sp):
            sp.dma_start(cs[:, :], d["cs"]).then_inc(loaded["cs"], 16)
            xv = d["x"].rearrange("(t p) n -> p t n", p=P)
            wm = [d[f"wmod{n}"].rearrange("(k p) n -> p k n", p=P) for n in range(2)]
            sp.dma_start(wmod[:, 0, :, 0:2 * E], wm[0][:, :, 0:2 * E]).then_inc(loaded["wmod0a"], 16)
            sp.dma_start(x[:, 0:4, :], xv[:, 0:4, :]).then_inc(loaded["xa"], 16)
            sp.dma_start(ident[:, :], d["ident"]).then_inc(loaded["ident"], 16)
            sp.dma_start(x[:, 4:8, :], xv[:, 4:8, :]).then_inc(loaded["xb"], 16)
            sp.dma_start(wkv, d["wkv"].rearrange("(k p) n -> p k n", p=P)).then_inc(loaded["wkv"], 16)
            sp.dma_start(peT[:, :], d["peT"]).then_inc(loaded["peT"], 16)
            sp.dma_start(bk[:, :], d["bk"]).then_inc(loaded["bk"], 16)
            sp.dma_start(bvB[:, :], d["bv"].partition_broadcast(P)).then_inc(loaded["bvB"], 16)
            sp.dma_start(mask_f[:, :], d["mask"]).then_inc(loaded["mask"], 16)
            sp.dma_start(bq[:, :], d["bq"]).then_inc(loaded["bq"], 16)
            sp.dma_start(wq, d["wq"].rearrange("(k p) n -> p k n", p=P)).then_inc(loaded["wq"], 16)
            sp.dma_start(small[:, 0:16], d["amp"]).then_inc(loaded["amp"], 16)
            sp.dma_start(small[:, 16:17], d["escale"]).then_inc(loaded["escale"], 16)
            sp.dma_start(wmod[:, 0, :, 2 * E:6 * E], wm[0][:, :, 2 * E:6 * E]).then_inc(loaded["wmod0b"], 16)
            sp.dma_start(wmod[:, 1, :, :], wm[1]).then_inc(loaded["wmod1"], 16)
            wov = d["wo"].rearrange("(h p) n -> p h n", p=P)
            for c in range(4):
                if c >= 2:
                    sp.wait_ge(wo_lo, c - 1)
                sp.dma_start(wo_stage[:, c % 2, :, :], wov[:, 4 * c:4 * c + 4, :]).then_inc(wo_loaded[c], 16)
            sp.wait_ge(mod_ps, 6)
            sp.dma_start(iota, d["iota"].partition_broadcast(P)).then_inc(loaded["iota"], 16)
            sp.wait_ge(q_ready, 2 * HQ)
            sp.dma_start(wr, d["wr"].rearrange("(k p) n -> p k n", p=P)).then_inc(loaded["wr"], 16)
            sp.wait_ge(scores, 3 * HQ)
            for m, n in enumerate(("wg", "wu")):
                sp.dma_start(wgu_f[:, m, :, :], d[n].rearrange("(k p) n -> p k n", p=P)).then_inc(loaded["wgu"], 16)
            sp.wait_ge(scores, 4 * HQ)
            for m, n in enumerate(("swg", "swu")):
                sp.dma_start(wsh_f[:, :, m * E:(m + 1) * E],
                             d[n].rearrange("(k p) n -> p k n", p=P)).then_inc(loaded["wsh"], 16)
            sp.dma_start(wdn_f[:, 0:1, :], d["wd"].rearrange("(k p) n -> p k n", p=P)).then_inc(loaded["wdn"], 16)
            sp.dma_start(wdn_f[:, 1:3, :], d["swd"].rearrange("(k p) n -> p k n", p=P)).then_inc(loaded["wdn"], 16)
            sp.wait_ge(scores, NU)
            sp.dma_start(w1b, d["w1"].rearrange("(k p) n -> p k n", p=P)).then_inc(loaded["w1"], 16)
            sp.dma_start(w3b, d["w3"].rearrange("(k p) n -> p k n", p=P)).then_inc(loaded["w3"], 16)
            sp.wait_ge(pv, NGR)
            sp.dma_start(w1a_f, d["w1a"].rearrange("(k p) n -> p k n", p=P)).then_inc(loaded["w1a"], 16)
            full = HID // P
            sp.dma_start(w2b[:, 0:full, :], d["w2"][0:full * P, :].rearrange("(k p) n -> p k n", p=P)) \
                .then_inc(loaded["w2"], 16)
            sp.dma_start(w2b[0:HID - full * P, full, :], d["w2"][full * P:HID, :]).then_inc(loaded["w2"], 16)
            sp.wait_ge(wo_done, NT)
            sp.dma_start(b1a, d["b1a"].partition_broadcast(P)).then_inc(loaded["b1a"], 16)
            sp.dma_start(ropeC, d["ropeC"].rearrange("p (t n) -> p t n", t=NT)).then_inc(loaded["rope"], 16)
            sp.dma_start(ropeS, d["ropeS"].rearrange("p (t n) -> p t n", t=NT)).then_inc(loaded["rope"], 16)
            sp.dma_start(gwf, d["gw"].rearrange("(k p) n -> p k n", p=P)).then_inc(loaded["gw"], 16)
            sp.dma_start(gbB, d["gb"].partition_broadcast(P)).then_inc(loaded["gw"], 16)
            sp.dma_start(iota1, d["iota"][:, 0:NE].partition_broadcast(P)).then_inc(loaded["gw"], 16)
            for t in range(NT):
                sp.wait_ge(av_ready, 2 * (t + 1))
                sp.dma_start(scratch[:, t * P:(t + 1) * P, :].rearrange("h p n -> p h n"),
                             av[:, t % 2, :].rearrange("p (h n) -> p h n", h=H1)).then_inc(shuffled[t], 16)
            for t in range(NT):
                sp.wait_ge(shuffled[t], 16)
            rows = scratch.rearrange("h s n -> (h s n)").rearrange("(t p n) -> p t n", p=P, n=E)
            for j in range(2):
                sp.dma_start(mixed_rows[:, 4 * j:4 * j + 4, :], rows[:, 4 * j:4 * j + 4, :]) \
                    .then_inc(loaded["mixed"], 16)
            ov = out.rearrange("(t p) n -> p t n", p=P)
            for t in range(NT):
                sp.wait_ge(x_out, t + 1)
                sp.dma_start(ov[:, t, :], x[:, t, :]).then_inc(stored, 16)
            sp.wait_ge(stored, 16 * NT)

        @block.gpsimd
        def _(pool):
            g = nc.gpsimd
            n = [0]

            def link(ins):
                n[0] += 1
                ins.then_inc(po_chain, 1)
                pool.wait_ge(po_chain, n[0])

            link(g.memset(mhalf[:, :], -0.5))
            link(g.memset(half[:, :], 0.5))
            pool.wait_ge(var_ready, 1)
            g.tensor_tensor(rstd0[:, :], ve0[:, :], mhalf[:, :], ALU.pow).then_inc(rstd_ready, 1)

            def rstd_of(q):
                pool.wait_ge(var_ready, q - NT + 2)
                g.tensor_tensor(rstd[:, q % 2:q % 2 + 1], ve[:, q % 2:q % 2 + 1], mhalf[:, 0:1], ALU.pow) \
                    .then_inc(rstd_ready, 1)

            for u in range(NU):
                i, h = unit(u)
                w = (i + 1) * P
                pool.wait_ge(rinv_ready, u + 1)
                g.tensor_tensor(probs[:, u % 4, 0:w], probs[:, u % 4, 0:w],
                                rinv[:, u % 4:u % 4 + 1].to_broadcast([P, w]), ALU.mult).then_inc(normed, 1)
                if u >= 24 and (u - 24) % HQ == 0:
                    rstd_of(NT + (u - 24) // HQ)
            rstd_of(2 * NT - 1)

            def tree_sum(t):
                b = t % 2
                pool.wait_ge(pair_used, 3 * t + 2)
                link(g.tensor_tensor(tree[:, 0:512], basis[:, b, 0:4, :], basis[:, b, 4:8, :], ALU.add))
                link(g.tensor_tensor(tree[:, 512:768], tree[:, 0:256], tree[:, 256:512], ALU.add))
                if t >= 2:
                    pool.wait_ge(mix_T, t - 1)
                g.tensor_tensor(mcat[:, b, 0:P], tree[:, 512:640], tree[:, 640:768], ALU.add).then_inc(basis_sum, 1)

            def weigh_values(t):
                pool.wait_ge(e1_ready, t + 1)
                pool.wait_ge(qkv_read, t + 1)
                if t >= 2:
                    pool.wait_ge(av_ps, t - 1)
                    pool.wait_ge(prod2_used, t - 1)
                eb = e1[:, t % 2, :].rearrange("p (h t) -> p h t", h=H1)
                vv = vb[:, t % 2, :].rearrange("p (t d) -> p t d", t=H1)
                g.tensor_tensor(prod2[t % 2][:, 0:2048].rearrange("p (t h d) -> p t h d", t=H1, h=HPE),
                                eb[:, 0:HPE, :].rearrange("p h t -> p t h").unsqueeze(3)
                                .to_broadcast([P, H1, HPE, D1]),
                                vv.unsqueeze(2).to_broadcast([P, H1, HPE, D1]), ALU.mult).then_inc(prod2_ready, 1)
                hm = H1 - HPE - HDV
                g.tensor_tensor(prod2[t % 2][:, 2048:2048 + hm * 256].rearrange("p (h d t) -> p h d t", h=hm, d=D1),
                                eb[:, HPE:H1 - HDV, :].unsqueeze(2).to_broadcast([P, hm, D1, H1]),
                                vv.rearrange("p t d -> p d t").unsqueeze(1).to_broadcast([P, hm, D1, H1]),
                                ALU.mult).then_inc(prod2b_ready, 1)

            for t in range(NT + 2):
                if t == NT + 1:
                    weigh_values(0)
                if t >= 2:
                    rstd_of(2 * NT + t - 2)
                if t < NT:
                    tree_sum(t)
            for t in range(1, NT):
                weigh_values(t)
            for t in range(NT):
                rstd_of(3 * NT + t)
            for b in range(2):
                pool.wait_ge(sp_ready, b + 1)
                bs = slice(32 * b, 32 * b + 32)
                g.tensor_tensor(g_r[:, bs], g_c[:, bs], half[:, bs], ALU.pow).then_inc(sq_ready, 1)

        @block.scalar
        def _(act):
            s = nc.scalar
            act.wait_ge(loaded["cs"], 16)
            s.activation(cth[:, :], cs[:, :], ACT.Tanh, scale=0.5).then_inc(cond_tanh, 1)

            def norm_out(q, ps, layer, which, halves):
                i = q % NT
                act.wait_ge(xn_T, q + 1)
                for k in range(KE):
                    o = which * 4
                    sh = modcol[:, layer, o + k:o + k + 1]
                    sc_ = modcol[:, layer, o + 2 + k:o + 3 + k]
                    src = ps[:, k * P:(k + 1) * P]
                    s.activation(hT[:, k, i * P:(i + 1) * P], src, ACT.Identity, bias=sh, scale=sc_) \
                        .then_inc(hT_ready, 1)
                    if halves:
                        s.activation(h_hl[:, 0, k, i * P:(i + 1) * P], src, ACT.Identity, bias=sh, scale=sc_) \
                            .then_inc(hT_ready, 1)

            act.wait_ge(mod_done, 1)
            for i in range(NT):
                norm_out(i, psT[:, i % 2, :], 0, 0, False)
            for m in range(NKV):
                kind, a, b = proj[m]
                act.wait_ge(tmp_ready, m + 1)
                if kind == "k":
                    s.activation(kT[:, a, b * 512:(b + 1) * 512], tmp[:, m % 2, :], ACT.Copy, scale=SCALE0) \
                        .then_inc(tmp_used, 1)
                else:
                    s.activation(v_hl[:, 0, a, :], tmp[:, m % 2, :], ACT.Copy).then_inc(tmp_used, 1)
            for c in range(4):
                act.wait_ge(wo_loaded[c], 16)
                s.activation(wo_hl[:, 0, 4 * c:4 * c + 4, :], wo_stage[:, c % 2, :, :], ACT.Copy).then_inc(wo_hi, 1)

            def weights_high(n_):
                if n_ < 4:
                    m, k = n_ // 2, n_ % 2
                    act.wait_ge(loaded["wgu"], 32)
                    s.activation(wgu[:, 0, m, k, :], wgu_f[:, m, k, :], ACT.Copy).then_inc(w_hi, 1)
                elif n_ == 4:
                    act.wait_ge(loaded["wsh"], 32)
                    s.activation(wsh[:, 0, :, :], wsh_f, ACT.Copy).then_inc(w_hi, 1)
                else:
                    act.wait_ge(loaded["wdn"], 32)
                    s.activation(wdn[:, 0, 0, :], wdn_f[:, 0, :], ACT.Copy).then_inc(w_hi, 1)
                    s.activation(wdn[:, 0, 1:3, :], wdn_f[:, 1:3, :], ACT.Copy, scale=0.5).then_inc(w_hi, 1)

            nh = [0]

            def attention(st_):
                G = (st_ - 11) // QPG
                if (st_ - 11) % QPG == 0 and 0 <= G < NGR:
                    act.wait_ge(pv, G + 1)
                    if G >= NG:
                        act.wait_ge(wo_done, G // NG)
                    s.activation(oT[:, 0, (G % NG) * QPG:(G % NG + 1) * QPG, :],
                                 psO[:, :].rearrange("p (h n) -> p h n", h=QPG), ACT.Copy).then_inc(oT_hi, 1)
                if LAG <= st_ < NU + LAG:
                    u = st_ - LAG
                    i, h = unit(u)
                    G = u // QPG
                    if G >= 2:
                        act.wait_ge(pv, G - 1)
                    for c, k in chunks(i):
                        act.wait_ge(pT_ps, nh[0] + 1)
                        s.activation(pT[:, G % 2, 0, c:c + k, h % QPG, :],
                                     psT[:, nh[0] % 2, 0:k * P].rearrange("p (k n) -> p k n", k=k),
                                     ACT.Copy).then_inc(pT_hi, 1)
                        nh[0] += 1
                if st_ < NU:
                    u = st_
                    i, h = unit(u)
                    w = (i + 1) * P
                    act.wait_ge(negmax_ready, u + 1)
                    if u >= 4:
                        act.wait_ge(pT_ps, chunk_end[u - 4])
                    s.activation(probs[:, u % 4, 0:w], psS[:, 2 * (u % 2):2 * (u % 2) + 2, :]
                                 .rearrange("p a n -> p (a n)")[:, 0:w], ACT.Exp,
                                 bias=negmax[:, u % 4:u % 4 + 1], accum_out=rowsum[:, u % 4:u % 4 + 1]) \
                        .then_inc(exp_done, 1)
                if (i := at(st_, 27)) is not None:
                    norm_out(NT + i, psM[:, 256:512], 0, 1, True)
                if st_ in WSPLIT:
                    weights_high(WSPLIT.index(st_))
                if (i := at(st_, 31)) is not None:
                    act.wait_ge(neg_ready, i + 1)
                    s.activation(eexp, logit, ACT.Exp, bias=small[:, 28:29], accum_out=small[:, 29:30]) \
                        .then_inc(e_ready, 1)
                    s.activation(small[:, 30:34], small[:, 20:24], ACT.Exp, bias=small[:, 28:29],
                                 accum_out=small[:, 34:35]).then_inc(e_ready, 1)
                if (i := at(st_, 33)) is not None:
                    act.wait_ge(coT_ps, i + 1)
                    s.activation(coeffT, psM[:, P:2 * P], ACT.Copy).then_inc(coT_ready, 1)

            def experts0(t):
                for j in range(3):
                    if j == 2:
                        if t >= 2:
                            norm_out(2 * NT + t - 2, psO[:, 256:512], 1, 0, True)
                        if 1 <= t <= NT:
                            b = (t - 1) % 2
                            act.wait_ge(mix_T, t)
                            s.activation(mcT[:, b, 0, :], psT[:, b, 0:384], ACT.Copy).then_inc(mix_hi, 1)
                    if t < NT:
                        p = 3 * t + j
                        w = 512 if j < 2 else 256
                        act.wait_ge(pair_ps, p + 1)
                        if p >= 2:
                            act.wait_ge(pair_used, p - 1)
                        s.activation(th0[:, p % 2, 0:w], psS[:, 2 * (p % 2), 0:w], ACT.Tanh, scale=0.5) \
                            .then_inc(tanh_ready, 1)
                if 5 <= t < 5 + KE:
                    k = t - 5
                    act.wait_ge(loaded["w1a"], 16)
                    act.wait_ge(wo_done, NT)
                    s.activation(w1a[:, 0, k, :], w1a_f[:, k, :], ACT.Copy).then_inc(w_hi, 1)

            def head_attention(t):
                if 1 <= t <= NT:
                    act.wait_ge(sub_ready, t)
                    if t >= 3:
                        act.wait_ge(prod2b_ready, t - 2)
                    s.activation(e1[:, (t - 1) % 2, :], ssub, ACT.Exp, scale=SCALE1).then_inc(e1_ready, 1)

            for st_ in range(NSTEP):
                attention(st_)
                for t in expert_steps(st_):
                    experts0(t)
            for t in EXPERTS_LEFT:
                if t == NT + 1:
                    head_attention(0)
                    head_attention(1)
                experts0(t)
            for t in range(2, NT + 1):
                head_attention(t)

            def router_exp(b):
                act.wait_ge(gabs, 2 * b + 1)
                bs = slice(32 * b, 32 * b + 32)
                s.activation(g_b[:, bs], g_a[:, bs], ACT.Exp, scale=-1.0).then_inc(gexp, 1)

            def router_ln(b):
                act.wait_ge(gabs, 2 * b + 2)
                bs = slice(32 * b, 32 * b + 32)
                s.activation(g_c[:, bs], g_a[:, bs], ACT.Ln).then_inc(gexp, 1)

            def hidden_high(t, c):
                m = 4 * t + c
                w = 4 if c < 3 else 1
                act.wait_ge(hc_T, m + 1)
                if t >= 2 and c == 0:
                    act.wait_ge(moe_ps, t - 1)
                rows_ = P if c < 3 else HID - 12 * P
                s.activation(hcT[0:rows_, t % 2, 0, c * 512:c * 512 + w * P],
                             psT[0:rows_, m % 2, 0:w * P], ACT.Copy).then_inc(hc_hi, 1)

            for t in range(NT + 5):
                if t < NT:
                    act.wait_ge(a_T, t + 1)
                    s.activation(aT[:, t % 2, 0, :], psT[:, t % 2, 0:E], ACT.Copy).then_inc(a_hi, 1)
                if 3 <= t < NT + 3:
                    norm_out(3 * NT + t - 3, psM[:, 256:512], 1, 1, True)
                if t == NT + 1:
                    router_exp(0)
                if t == NT + 2:
                    router_ln(0)
            for t in range(NT + 1):
                if t == 1:
                    router_exp(1)
                if t == 2:
                    router_ln(1)
                for j in range(NCH):
                    if j >= 2 and t >= 1:
                        hidden_high(t - 1, j - 2)
                    if t < NT:
                        p = NCH * t + j
                        w = 2 * INTER if j < 4 else INTER
                        act.wait_ge(chunk_ps, p + 1)
                        if p >= 2:
                            act.wait_ge(chunk_used, p - 1)
                        s.activation(th1[:, p % 2, 0:w], psS[:, 2 * (p % 2), 0:w], ACT.Tanh, scale=0.5) \
                            .then_inc(chunk_tanh, 1)
                if t >= 1:
                    hidden_high(t - 1, 3)

        @block.vector
        def _(dve):
            v = nc.vector
            n = [0]

            def link(ins):
                n[0] += 1
                ins.then_inc(ve_chain, 1)
                dve.wait_ge(ve_chain, n[0])

            def xn_of(q, mean, rs):
                dve.wait_ge(xn_T, q - 1) if q >= 2 else None
                v.tensor_scalar(xn[:, q % 2, :], x[:, q % NT, :], mean, rs, ALU.subtract, ALU.mult) \
                    .then_inc(xn_ready, 1)

            dve.wait_ge(cond_tanh, 1)
            link(v.scalar_tensor_tensor(out=cth[:, :], in0=cth[:, :], scalar=1.0, in1=cs[:, :],
                                        op0=ALU.add, op1=ALU.mult))
            link(v.tensor_scalar(cth[:, :], cth[:, :], 0.5, None, ALU.mult))
            v.tensor_copy(csB[:, :, :], cth[:, :].unsqueeze(2).to_broadcast([P, 4, P])).then_inc(cond_rows, 1)

            for i in range(NT):
                dve.wait_ge(loaded["xa" if i < 4 else "xb"], 16)
                link(v.bn_stats(st[:, i % 2, :], x[:, i, :]))
                link(v.bn_aggr(mv[:, i, :], st[:, i % 2, :]))
            v.tensor_scalar(ve0[:, :], mv[:, :, 1], LN_EPS, None, ALU.add).then_inc(var_ready, 1)

            def modulation(j):
                layer, third = MOD[j]
                dve.wait_ge(mod_ps, j + 1)
                if third == 0:
                    v.tensor_copy(modrow, psO[:, :]).then_inc(mod_rows, 1)
                else:
                    a = 256 if third == 1 else 0
                    gt = 256 - a
                    v.tensor_copy(modrow[:, 0:256], psO[:, a:a + 256]).then_inc(mod_rows, 1)
                    gdst = gates[:, layer, third - 1, :]
                    gps = psO[:, gt:gt + 256]
                    link(v.tensor_scalar(tmp[:, 0, 0:256], gps, 0.0, 2.0, ALU.is_ge, ALU.mult))
                    link(v.tensor_scalar(tmp[:, 0, 0:256], tmp[:, 0, 0:256], -1.0, None, ALU.add))
                    link(v.tensor_tensor(tmp[:, 0, 256:512], gps, tmp[:, 0, 0:256], ALU.mult))
                    link(v.scalar_tensor_tensor(out=gdst, in0=tmp[:, 0, 256:512], scalar=GATE_FLOOR,
                                                in1=tmp[:, 0, 0:256], op0=ALU.max, op1=ALU.mult))
                dve.wait_ge(mod_T, j + 1)
                cols = psM[:, :].rearrange("p (b n) -> p b n", n=P)[:, :, 0]
                if third == 0:
                    link(v.tensor_copy(modcol[:, layer, 0:2], cols[:, 0:2]))
                    v.tensor_scalar(modcol[:, layer, 2:4], cols[:, 2:4], 1.0, None, ALU.add).then_inc(mod_done, 1)
                elif third == 1:
                    v.tensor_copy(modcol[:, layer, 4:6], cols[:, 0:2]).then_inc(mod_done, 1)
                else:
                    v.tensor_scalar(modcol[:, layer, 6:8], cols[:, 0:2], 1.0, None, ALU.add).then_inc(mod_done, 1)

            modulation(0)
            dve.wait_ge(rstd_ready, 1)
            dve.wait_ge(mod_T, 1)
            for i in range(NT):
                xn_of(i, mv[:, i, 0:1], rstd0[:, i:i + 1])
            dve.wait_ge(loaded["ident"], 16)
            link(v.tensor_copy(ident_b[:, :], ident[:, :]))
            dve.wait_ge(loaded["mask"], 16)
            v.tensor_copy(mask_b[:, :], mask_f[:, :]).then_inc(masks_ready, 1)
            dve.wait_ge(loaded["peT"], 16)
            dve.wait_ge(loaded["bk"], 16)
            dve.wait_ge(loaded["bvB"], 16)
            dve.wait_ge(mod_ps, 1)

            def v_low(m):
                kind, a, b = proj[m]
                if kind == "v":
                    dve.wait_ge(tmp_used, m + 1)
                    link(v.tensor_tensor(v_hl[:, 1, a, :], tmp[:, m % 2, :], v_hl[:, 0, a, :], ALU.subtract))

            for m in range(NKV):
                kind, a, b = proj[m]
                if m >= 1:
                    v_low(m - 1)
                dve.wait_ge(proj_done, m + 1)
                if m >= 2:
                    dve.wait_ge(tmp_used, m - 1)
                bank = psS[:, m % 4, :]
                if kind == "k":
                    v.scalar_tensor_tensor(out=tmp[:, m % 2, :], in0=bank, scalar=bk[:, a:a + 1],
                                           in1=peT[:, b * 512:(b + 1) * 512], op0=ALU.add, op1=ALU.add) \
                        .then_inc(tmp_ready, 1)
                else:
                    v.tensor_tensor(tmp[:, m % 2, :], bank, bvB[:, :], ALU.add).then_inc(tmp_ready, 1)
            v_low(NKV - 1)
            dve.wait_ge(loaded["amp"], 16)
            dve.wait_ge(loaded["escale"], 16)
            link(v.tensor_tensor(small[:, 36:52], small[:, 0:16], small[:, 0:16], ALU.mult))
            link(v.tensor_reduce(mixs[:, :], small[:, 36:52].rearrange("p (k c) -> p k c", c=2), AX.X, ALU.add))
            link(v.tensor_reduce(small[:, 17:18], mixs[:, :], AX.X, ALU.add))
            link(v.tensor_scalar(small[:, 17:18], small[:, 17:18], TOP_EPS, None, ALU.add))
            link(v.reciprocal(small[:, 18:19], small[:, 17:18]))
            link(v.tensor_scalar(mixs[:, :], mixs[:, :], small[:, 18:19], small[:, 16:17], ALU.mult, ALU.mult))
            link(v.tensor_scalar(mixs[:, :], mixs[:, :], 0.5, None, ALU.mult))
            dve.wait_ge(loaded["bq"], 16)
            for m in range(NKV, len(proj)):
                kind, h, nn = proj[m]
                dve.wait_ge(proj_done, m + 1)
                v.scalar_tensor_tensor(out=qT[:, 4 * nn:4 * nn + 4, h, :],
                                       in0=psS[:, m % 4, :].rearrange("p (t n) -> p t n", t=4),
                                       scalar=bq[:, h:h + 1],
                                       in1=peT[:, nn * 512:(nn + 1) * 512].rearrange("p (t n) -> p t n", t=4),
                                       op0=ALU.add, op1=ALU.add).then_inc(q_ready, 1)
                if h % 8 == 7:
                    c = (m - NKV) // 8
                    dve.wait_ge(wo_hi, c + 1)
                    v.tensor_tensor(wo_hl[:, 1, 4 * c:4 * c + 4, :], wo_stage[:, c % 2, :, :],
                                    wo_hl[:, 0, 4 * c:4 * c + 4, :], ALU.subtract).then_inc(wo_lo, 1)
            for j in range(1, 6):
                modulation(j)

            def residual(q, ps, layer, which, ready, value, last=False):
                i = q % NT
                dve.wait_ge(ready, value)
                link(v.tensor_tensor(tmp[:, 0, 0:E], ps, gates[:, layer, which, :], ALU.mult))
                if last:
                    v.tensor_tensor(x[:, i, :], x[:, i, :], tmp[:, 0, 0:E], ALU.add).then_inc(x_out, 1)
                    return
                link(v.tensor_tensor(x[:, i, :], x[:, i, :], tmp[:, 0, 0:E], ALU.add))
                link(v.bn_stats(st[:, q % 2, :], x[:, i, :]))
                link(v.bn_aggr(mv2[:, q % 2, :], st[:, q % 2, :]))
                v.tensor_scalar(ve[:, q % 2:q % 2 + 1], mv2[:, q % 2, 1:2], LN_EPS, None, ALU.add) \
                    .then_inc(var_ready, 1)

            def xn_later(q):
                dve.wait_ge(rstd_ready, q - NT + 2)
                xn_of(q, mv2[:, q % 2, 0:1], rstd[:, q % 2:q % 2 + 1])

            def h_low(q):
                i = q % NT
                dve.wait_ge(hT_ready, 2 * NT + 4 * (q - NT + 1))
                v.tensor_tensor(h_hl[:, 1, :, i * P:(i + 1) * P], hT[:, :, i * P:(i + 1) * P],
                                h_hl[:, 0, :, i * P:(i + 1) * P], ALU.subtract).then_inc(hlo_ready, 1)

            def weights_low(n_):
                if n_ < 4:
                    m, k = n_ // 2, n_ % 2
                    dve.wait_ge(w_hi, n_ + 1)
                    v.tensor_tensor(wgu[:, 1, m, k, :], wgu_f[:, m, k, :], wgu[:, 0, m, k, :], ALU.subtract) \
                        .then_inc(w_lo, 1)
                elif n_ == 4:
                    dve.wait_ge(w_hi, 5)
                    v.tensor_tensor(wsh[:, 1, :, :], wsh_f, wsh[:, 0, :, :], ALU.subtract).then_inc(w_lo, 1)
                else:
                    dve.wait_ge(w_hi, 7)
                    v.tensor_tensor(wdn[:, 1, 0, :], wdn_f[:, 0, :], wdn[:, 0, 0, :], ALU.subtract).then_inc(w_lo, 1)
                    v.scalar_tensor_tensor(out=wdn[:, 1, 1:3, :], in0=wdn_f[:, 1:3, :], scalar=0.5,
                                           in1=wdn[:, 0, 1:3, :], op0=ALU.mult, op1=ALU.subtract).then_inc(w_lo, 1)

            nl = [0]
            mx8, neg, zsum, top4, den, rr = (small[:, 20:28], small[:, 28:29], small[:, 29:30],
                                             small[:, 34:35], small[:, 35:36], small[:, 19:20])
            idx = small[:, 52:60]

            def attention(st_):
                if 1 <= st_ <= NU:
                    u = st_ - 1
                    dve.wait_ge(exp_done, u + 1)
                    if u >= 4:
                        dve.wait_ge(normed, u - 3)
                    v.reciprocal(rinv[:, u % 4:u % 4 + 1], rowsum[:, u % 4:u % 4 + 1]).then_inc(rinv_ready, 1)
                G = (st_ - 11) // QPG
                if (st_ - 11) % QPG == 0 and 0 <= G < NGR:
                    dve.wait_ge(oT_hi, G + 1)
                    hs = slice((G % NG) * QPG, (G % NG + 1) * QPG)
                    v.tensor_tensor(oT[:, 1, hs, :], psO[:, :].rearrange("p (h n) -> p h n", h=QPG),
                                    oT[:, 0, hs, :], ALU.subtract).then_inc(oT_lo, 1)
                if st_ < NU:
                    u = st_
                    i, h = unit(u)
                    w = (i + 1) * P
                    dve.wait_ge(scores, u + 1)
                    v.tensor_reduce(negmax[:, u % 4:u % 4 + 1], psS[:, 2 * (u % 2):2 * (u % 2) + 2, :]
                                    .rearrange("p a n -> p (a n)")[:, 0:w], AX.X, ALU.max, negate=True) \
                        .then_inc(negmax_ready, 1)
                if LAG <= st_ < NU + LAG:
                    u = st_ - LAG
                    i, h = unit(u)
                    G = u // QPG
                    for c, k in chunks(i):
                        dve.wait_ge(pT_hi, nl[0] + 1)
                        dst = pT[:, G % 2, :, c:c + k, h % QPG, :]
                        v.tensor_tensor(dst[:, 1], psT[:, nl[0] % 2, 0:k * P].rearrange("p (k n) -> p k n", k=k),
                                        dst[:, 0], ALU.subtract).then_inc(pT_lo, 1)
                        nl[0] += 1
                if (i := at(st_, 26)) is not None:
                    xn_later(NT + i)
                if (i := at(st_, 25)) is not None:
                    residual(NT + i, psM[:, 0:E], 0, 0, wo_done, i + 1)
                if (i := at(st_, 28)) is not None:
                    h_low(NT + i)
                if st_ in WSPLIT:
                    weights_low(WSPLIT.index(st_))
                if (i := at(st_, 30)) is not None:
                    if i == 0:
                        dve.wait_ge(loaded["iota"], 16)
                    dve.wait_ge(logit_ps, i + 1)
                    link(v.tensor_copy(logit, psM[:, 0:P]))
                    link(v.max(mx8, logit))
                    v.tensor_scalar(neg, mx8[:, 0:1], -1.0, None, ALU.mult).then_inc(neg_ready, 1)
                    link(v.max_index(small[:, 36:44].bitcast(U32), mx8, logit))
                    link(v.tensor_copy(idx, small[:, 36:44].bitcast(U32)))
                if (i := at(st_, 31)) is not None:
                    link(v.tensor_scalar(onehot, iota, idx[:, 0:1], None, ALU.is_equal))
                    for k in range(1, 4):
                        link(v.scalar_tensor_tensor(out=onehot, in0=iota, scalar=idx[:, k:k + 1], in1=onehot,
                                                    op0=ALU.is_equal, op1=ALU.add))
                if (i := at(st_, 32)) is not None:
                    dve.wait_ge(e_ready, 2 * i + 2)
                    link(v.tensor_scalar(den, zsum, TOP_EPS, top4, ALU.mult, ALU.add))
                    link(v.reciprocal(rr, den))
                    v.scalar_tensor_tensor(out=coeff, in0=eexp, scalar=rr, in1=onehot, op0=ALU.mult, op1=ALU.mult) \
                        .then_inc(coeff_ready, 1)
                if (i := at(st_, 35)) is not None:
                    dve.wait_ge(c_ps, i + 1)
                    v.tensor_copy(c_tok[:, i, :], psM[:, 2 * P:2 * P + NB]).then_inc(c_ready, 1)

            def experts0(t):
                b = t % 2
                if t >= 2:
                    residual(2 * NT + t - 2, psO[:, 0:E], 0, 1, down_ps, t - 1)
                for j in range(2):
                    if t < NT:
                        p = 3 * t + j
                        dve.wait_ge(tanh_ready, p + 1)
                        link(v.scalar_tensor_tensor(out=act0[:, p % 2, :], in0=th0[:, p % 2, :], scalar=1.0,
                                                    in1=psS[:, 2 * (p % 2), :], op0=ALU.add, op1=ALU.mult))
                        if j == 0:
                            dve.wait_ge(c_ready, t + 1)
                            if t >= 2:
                                dve.wait_ge(basis_sum, t - 1)
                        for k in range(4):
                            kk = 4 * j + k
                            ins = v.scalar_tensor_tensor(
                                out=basis[:, b, kk, :], in0=act0[:, p % 2, k * P:(k + 1) * P],
                                scalar=c_tok[:, t, kk:kk + 1], in1=psS[:, 2 * (p % 2) + 1, k * P:(k + 1) * P],
                                op0=ALU.mult, op1=ALU.mult)
                        ins.then_inc(pair_used, 1)
                    if j == 0 and t >= 2:
                        xn_later(2 * NT + t - 2)
                if 1 <= t <= NT:
                    dve.wait_ge(mix_hi, t)
                    v.tensor_tensor(mcT[:, 1 - b, 1, :], psT[:, 1 - b, 0:384], mcT[:, 1 - b, 0, :], ALU.subtract) \
                        .then_inc(mix_lo, 1)
                if t < NT:
                    p = 3 * t + 2
                    dve.wait_ge(tanh_ready, p + 1)
                    link(v.scalar_tensor_tensor(out=act0[:, p % 2, 0:E], in0=th0[:, p % 2, 0:E], scalar=1.0,
                                                in1=psS[:, 2 * (p % 2), 0:E], op0=ALU.add, op1=ALU.mult))
                    if t >= 2:
                        dve.wait_ge(mix_T, t - 1)
                    v.tensor_tensor(mcat[:, b, P:3 * P], act0[:, p % 2, 0:E], psS[:, 2 * (p % 2), E:2 * E],
                                    ALU.mult).then_inc(pair_used, 1)
                if t >= 2:
                    h_low(2 * NT + t - 2)
                if 5 <= t < 5 + KE:
                    k = t - 5
                    dve.wait_ge(w_hi, 8 + k)
                    v.tensor_tensor(w1a[:, 1, k, :], w1a_f[:, k, :], w1a[:, 0, k, :], ALU.subtract).then_inc(w_lo, 1)

            def score_products(t):
                b = t % 2
                if t == 0:
                    dve.wait_ge(loaded["b1a"], 16)
                    dve.wait_ge(loaded["rope"], 32)
                dve.wait_ge(qkv_ps, t + 1)
                if t >= 2:
                    dve.wait_ge(prod2b_ready, t - 1)
                v.tensor_tensor(vb[:, b, :], psS[:, 2 + b, 0:E], b1a[:, 2 * E:3 * E], ALU.add).then_inc(ve_chain, 1)
                n[0] += 1
                v.tensor_tensor(qkb[:, b, :], psS[:, b, :], b1a[:, 0:2 * E], ALU.add).then_inc(qkv_read, 1)
                dve.wait_ge(qkv_read, t + 1)
                heads = 2 * H1
                q4 = qkb[:, b, :].rearrange("p (h d c) -> p h d c", h=heads, c=2)
                b4 = ropeB.rearrange("p (h d c) -> p h d c", h=heads, c=2)
                cos = ropeC[:, t, :].unsqueeze(1).to_broadcast([P, heads, D1])
                sin = ropeS[:, t, :].rearrange("p (d c) -> p d c", c=2)
                for c in range(2):
                    v.tensor_tensor(b4[:, :, :, c], q4[:, :, :, 1 - c],
                                    sin[:, :, c].unsqueeze(1).to_broadcast([P, heads, D1 // 2]), ALU.mult) \
                        .then_inc(ve_chain, 1)
                    n[0] += 1
                link(v.tensor_tensor(ropeA.rearrange("p (h d) -> p h d", h=heads),
                                     qkb[:, b, :].rearrange("p (h d) -> p h d", h=heads), cos, ALU.mult))
                link(v.tensor_tensor(qkr[:, b, :], ropeA, ropeB, ALU.add))
                if t >= 2:
                    dve.wait_ge(s_sum, t - 1)
                v.tensor_tensor(prod1[:, b, :].rearrange("p (d h t) -> p d h t", d=D1, h=H1),
                                qkr[:, b, 0:E].rearrange("p (h d) -> p d h", h=H1).unsqueeze(3)
                                .to_broadcast([P, D1, H1, H1]),
                                qkr[:, b, E:2 * E].rearrange("p (t d) -> p d t", t=H1).unsqueeze(2)
                                .to_broadcast([P, D1, H1, H1]), ALU.mult).then_inc(prod1_ready, 1)

            def softmax_in(t):
                dve.wait_ge(s_sum, t + 1)
                ps = psT[:, t % 2, 0:256].rearrange("p (h t) -> p h t", h=H1)
                link(v.tensor_reduce(m1[:, t % 2, :], ps, AX.X, ALU.max))
                if t >= 1:
                    dve.wait_ge(e1_ready, t)
                v.tensor_tensor(ssub.rearrange("p (h t) -> p h t", h=H1), ps,
                                m1[:, t % 2, :].unsqueeze(2).to_broadcast([P, H1, H1]), ALU.subtract) \
                    .then_inc(sub_ready, 1)

            def weigh_last_heads(t):
                b = t % 2
                dve.wait_ge(e1_ready, t + 1)
                eb = e1[:, b, :].rearrange("p (h t) -> p h t", h=H1)
                part2 = prod2[b][:, 2048:4096].rearrange("p (h d t) -> p h d t", h=H1 - HPE, d=D1)
                link(v.tensor_tensor(part2[:, H1 - HPE - HDV:, :, :],
                                     eb[:, H1 - HDV:, :].unsqueeze(2).to_broadcast([P, HDV, D1, H1]),
                                     vb[:, b, :].rearrange("p (t d) -> p d t", t=H1).unsqueeze(1)
                                     .to_broadcast([P, HDV, D1, H1]), ALU.mult))

            def weighted(t):
                b = t % 2
                eb = e1[:, b, :].rearrange("p (h t) -> p h t", h=H1)
                part2 = prod2[b][:, 2048:4096].rearrange("p (h d t) -> p h d t", h=H1 - HPE, d=D1)
                link(v.tensor_reduce(s1, eb, AX.X, ALU.add))
                link(v.reciprocal(r1, s1))
                if t >= 2:
                    dve.wait_ge(shuffled[t - 2], 16)
                out4 = av[:, b, :].rearrange("p (h d) -> p h d", h=H1)
                rb = r1.unsqueeze(2).to_broadcast([P, H1, D1])
                dve.wait_ge(prod2b_ready, t + 1)
                v.tensor_reduce(avr, part2.rearrange("p h d t -> p (h d) t"), AX.X, ALU.add).then_inc(prod2_used, 1)
                dve.wait_ge(av_ps, t + 1)
                v.tensor_tensor(out4[:, 0:HPE, :], (psO if b == 0 else psM)[:, 0:HPE * D1]
                                .rearrange("p (h d) -> p h d", h=HPE), rb[:, 0:HPE, :], ALU.mult).then_inc(av_ready, 1)
                dve.wait_ge(prod2_used, t + 1)
                v.tensor_tensor(out4[:, HPE:, :], avr.rearrange("p (h d) -> p h d", h=H1 - HPE), rb[:, HPE:, :],
                                ALU.mult).then_inc(av_ready, 1)

            def head_attention(t):
                if t >= 2:
                    weigh_last_heads(t - 2)
                if t < NT:
                    score_products(t)
                if 1 <= t <= NT:
                    softmax_in(t - 1)
                if t >= 2:
                    weighted(t - 2)

            for st_ in range(NSTEP):
                attention(st_)
                for t in expert_steps(st_):
                    experts0(t)
            for t in EXPERTS_LEFT:
                if t == NT + 1:
                    head_attention(0)
                    head_attention(1)
                experts0(t)
            for t in range(2, NT + 2):
                head_attention(t)

            def tiles(a, b):
                return a[:, 32 * b:32 * b + 32].rearrange("p (t e) -> p t e", e=NE)

            def router_abs(b):
                bs = slice(32 * b, 32 * b + 32)
                dve.wait_ge(gate_ps, 4 * (b + 1))
                if b == 0:
                    dve.wait_ge(loaded["gw"], 48)
                link(v.tensor_copy(g_s[:, bs], (psS[:, 0, 0:32] if b == 0 else psO[:, 0:32])))
                v.scalar_tensor_tensor(out=g_a[:, bs], in0=g_s[:, bs], scalar=-1.0, in1=g_s[:, bs],
                                       op0=ALU.mult, op1=ALU.max).then_inc(gabs, 1)

            def router_one(b):
                bs = slice(32 * b, 32 * b + 32)
                dve.wait_ge(gexp, 2 * b + 1)
                v.tensor_scalar(g_a[:, bs], g_b[:, bs], 1.0, None, ALU.add).then_inc(gabs, 1)

            def router_softplus(b):
                bs = slice(32 * b, 32 * b + 32)
                ga, gb_, gc, gm, gx, gi = (a[:, bs] for a in (g_a, g_b, g_c, g_m, g_x, g_i))
                dve.wait_ge(gabs, 2 * b + 2)
                link(v.tensor_scalar(gm, ga, -1.0, None, ALU.add))
                link(v.tensor_scalar(gx, gm, 0.0, None, ALU.is_equal))
                link(v.tensor_tensor(gm, gm, gx, ALU.add))
                link(v.reciprocal(gi, gm))
                dve.wait_ge(gexp, 2 * b + 2)
                link(v.tensor_tensor(gc, gc, gx, ALU.add))
                link(v.tensor_tensor(gc, gc, gb_, ALU.mult))
                link(v.tensor_tensor(gc, gc, gi, ALU.mult))
                v.scalar_tensor_tensor(out=gc, in0=g_s[:, bs], scalar=0.0, in1=gc, op0=ALU.max, op1=ALU.add) \
                    .then_inc(sp_ready, 1)

            def router_top2(b):
                bs = slice(32 * b, 32 * b + 32)
                dve.wait_ge(sq_ready, b + 1)
                link(v.tensor_tensor(tiles(g_x, b), tiles(g_r, b), gbB.unsqueeze(1).to_broadcast([P, 4, NE]), ALU.add))
                for t in range(4 * b, 4 * b + 4):
                    e8 = slice(t * NE, (t + 1) * NE)
                    v.max(g_m[:, e8], g_x[:, e8]).then_inc(ve_chain, 1)
                    n[0] += 1
                dve.wait_ge(ve_chain, n[0])
                for t in range(4 * b, 4 * b + 4):
                    e8 = slice(t * NE, (t + 1) * NE)
                    v.max_index(g_u[:, e8], g_m[:, e8], g_x[:, e8]).then_inc(ve_chain, 1)
                    n[0] += 1
                dve.wait_ge(ve_chain, n[0])
                link(v.tensor_copy(g_i[:, bs], g_u[:, bs]))
                for k, dst in enumerate((g_a, g_b)):
                    link(v.tensor_tensor(tiles(dst, b), iota1.unsqueeze(1).to_broadcast([P, 4, NE]),
                                         tiles(g_i, b)[:, :, k:k + 1].to_broadcast([P, 4, NE]), ALU.is_equal))
                link(v.tensor_tensor(g_a[:, bs], g_a[:, bs], g_b[:, bs], ALU.add))
                link(v.scalar_tensor_tensor(out=cw[:, 4 * b:4 * b + 4, :], in0=tiles(g_r, b), scalar=0.5,
                                            in1=tiles(g_a, b), op0=ALU.mult, op1=ALU.mult))

            link(v.tensor_tensor(gbo, b1a[:, 3 * E:4 * E], gates[:, 1, 0, :], ALU.mult))
            for t in range(NT + 5):
                if t < NT:
                    dve.wait_ge(a_hi, t + 1)
                    v.tensor_tensor(aT[:, t % 2, 1, :], psT[:, t % 2, 0:E], aT[:, t % 2, 0, :], ALU.subtract) \
                        .then_inc(a_lo, 1)
                if 2 <= t < NT + 2:
                    i = t - 2
                    link(v.tensor_tensor(x[:, i, :], x[:, i, :], gbo, ALU.add))
                    residual(3 * NT + i, psO[:, 0:E] if i % 2 == 0 else psS[:, 1, 0:E], 1, 0, o_ps, i + 1)
                if 3 <= t < NT + 3:
                    xn_later(3 * NT + t - 3)
                if 4 <= t < NT + 4:
                    h_low(3 * NT + t - 4)
                if t == NT:
                    router_abs(0)
                if t == NT + 2:
                    router_one(0)
                if t == NT + 3:
                    router_softplus(0)
                if t == NT + 4:
                    router_top2(0)
            for t in range(NT + 2):
                b = t % 2
                if t == 0:
                    router_abs(1)
                if t == 2:
                    router_one(1)
                if t == 3:
                    router_softplus(1)
                if t == 4:
                    router_top2(1)
                for j in range(NCH):
                    if t < NT:
                        p = NCH * t + j
                        w = 2 * INTER if j < NCH - 1 else INTER
                        dve.wait_ge(chunk_tanh, p + 1)
                        link(v.scalar_tensor_tensor(out=a1[:, p % 2, 0:w], in0=th1[:, p % 2, 0:w], scalar=1.0,
                                                    in1=psS[:, 2 * (p % 2), 0:w], op0=ALU.add, op1=ALU.mult))
                        if t >= 2 and j == 0:
                            dve.wait_ge(hc_T, 4 * (t - 1))
                        for m in range(w // INTER):
                            e = 2 * j + m
                            lo = m * INTER
                            ins = v.scalar_tensor_tensor(
                                out=hc[:, b, e * INTER:(e + 1) * INTER], in0=a1[:, p % 2, lo:lo + INTER],
                                scalar=cw[:, t, e:e + 1] if e < NE else 0.5,
                                in1=psS[:, 2 * (p % 2) + 1, lo:lo + INTER], op0=ALU.mult, op1=ALU.mult)
                        ins.then_inc(chunk_used, 1)
                    if j == 1 and t >= 2:
                        residual(t - 2, psO[:, 0:E], 1, 1, moe_ps, t - 1, last=True)
                    if j >= 1 and 1 <= t <= NT:
                        c = j - 1
                        m = 4 * (t - 1) + c
                        w = 4 if c < 3 else 1
                        rows_ = P if c < 3 else HID - 12 * P
                        dve.wait_ge(hc_hi, m + 1)
                        o = c * 512
                        v.tensor_tensor(hcT[0:rows_, 1 - b, 1, o:o + w * P], psT[0:rows_, m % 2, 0:w * P],
                                        hcT[0:rows_, 1 - b, 0, o:o + w * P], ALU.subtract).then_inc(hc_lo, 1)

        @block.tensor
        def _(pe):
            te = nc.tensor

            def mm(out_, lhsT, rhs, start, stop):
                return te.matmul(out_, lhsT=lhsT, rhs=rhs, start=start, stop=stop)

            def three(out_, a_hi_, a_lo_, b_hi_, b_lo_, first, last):
                mm(out_, a_hi_, b_hi_, first, False)
                mm(out_, a_hi_, b_lo_, False, False)
                return mm(out_, a_lo_, b_hi_, False, last)

            def modulation(j):
                layer, third = MOD[j]
                if j:
                    pe.wait_ge(mod_done, j)
                for k in range(KE):
                    ins = mm(psO[:, :], csB[:, 2 * layer + k, :], wmod[:, layer, k, third * 512:third * 512 + 512],
                             k == 0, k == KE - 1)
                ins.then_inc(mod_ps, 1)
                pe.wait_ge(mod_rows, j + 1)
                for b in range(4 if third == 0 else 2):
                    ins = te.transpose(psM[:, b * P:(b + 1) * P], modrow[:, b * P:(b + 1) * P], ident[:, :])
                ins.then_inc(mod_T, 1)

            def norm_T(q, ps):
                pe.wait_ge(xn_ready, q + 1)
                for k in range(KE):
                    ins = te.transpose(ps[:, k * P:(k + 1) * P], xn[:, q % 2, k * P:(k + 1) * P], ident[:, :])
                ins.then_inc(xn_T, 1)

            def h_out(q):
                return 2 * NT + 4 * (q - NT + 1)

            pe.wait_ge(cond_rows, 1)
            pe.wait_ge(loaded["wmod0a"], 16)
            pe.wait_ge(loaded["ident"], 16)
            modulation(0)
            for i in range(NT):
                if i >= 2:
                    pe.wait_ge(hT_ready, 2 * (i - 1))
                norm_T(i, psT[:, i % 2, :])
            pe.wait_ge(loaded["wkv"], 16)
            for m in range(len(proj)):
                kind, a, b = proj[m]
                if m == NKV:
                    pe.wait_ge(loaded["wq"], 16)
                if m >= 4:
                    if m - 4 < NKV:
                        pe.wait_ge(tmp_ready, m - 3)
                    else:
                        pe.wait_ge(q_ready, m - 3 - NKV)
                if kind == "k":
                    pe.wait_ge(hT_ready, 2 * 4 * (b + 1))
                if kind == "v":
                    pe.wait_ge(hT_ready, 2 * (a + 1))
                for k in range(KE):
                    if kind == "k":
                        lhsT, rhs = wkv[:, k, 2 * a * P:(2 * a + 1) * P], hT[:, k, b * 512:(b + 1) * 512]
                    elif kind == "v":
                        lhsT = hT[:, k, a * P:(a + 1) * P]
                        rhs = wkv[:, k, :].rearrange("p (g c n) -> p g c n", g=NG, c=2)[:, :, 1, :]
                    else:
                        lhsT, rhs = wq[:, k, a * P:(a + 1) * P], hT[:, k, b * 512:(b + 1) * 512]
                    ins = mm(psS[:, m % 4, :], lhsT, rhs, k == 0, k == KE - 1)
                ins.then_inc(proj_done, 1)
            pe.wait_ge(loaded["wmod0b"], 16)
            pe.wait_ge(loaded["wmod1"], 16)
            for j in range(1, 6):
                modulation(j)

            pe.wait_ge(q_ready, 2 * HQ)
            pe.wait_ge(masks_ready, 1)
            pe.wait_ge(mod_done, 6)
            nt = [0]
            def attention(st_):
                if st_ < NU:
                    u = st_
                    i, h = unit(u)
                    if u < NKV:
                        pe.wait_ge(tmp_used, NKV)
                    if u >= 2:
                        pe.wait_ge(exp_done, u - 1)
                    w = (i + 1) * P
                    for c in range(0, w, 512):
                        cw_ = min(512, w - c)
                        bank = psS[:, 2 * (u % 2) + c // 512, :]
                        diag = c + cw_ == w
                        ins = mm(bank[:, 0:cw_], qT[:, i, h, :], kT[:, h // QPG, c:c + cw_], True, not diag)
                        if diag:
                            ins = mm(bank[:, cw_ - P:cw_], ident_b[:, :], mask_b[:, :], False, True)
                    ins.then_inc(scores, 1)
                if LAG <= st_ < NU + LAG:
                    u = st_ - LAG
                    i, h = unit(u)
                    pe.wait_ge(normed, u + 1)
                    for c, k in chunks(i):
                        if nt[0] >= 2:
                            pe.wait_ge(pT_lo, nt[0] - 1)
                        for b in range(k):
                            ins = te.transpose(psT[:, nt[0] % 2, b * P:(b + 1) * P],
                                               probs[:, u % 4, (c + b) * P:(c + b + 1) * P], ident[:, :])
                        ins.then_inc(pT_ps, 1)
                        nt[0] += 1
                G, part = (st_ - 7) // QPG, (st_ - 7) % QPG
                if 0 <= G < NGR:
                    i, g_ = G // NG, G % NG
                    if part == 0:
                        pe.wait_ge(pT_lo, chunk_end[QPG * G + QPG - 1])
                        if G >= 1:
                            pe.wait_ge(oT_lo, G)
                    vs = slice(g_ * P, (g_ + 1) * P)
                    products = [(j, *vp) for j in range(i + 1) for vp in ((0, 0), (0, 1), (1, 0))]
                    n_ = len(products)
                    for m in range(part * n_ // QPG, (part + 1) * n_ // QPG):
                        j, wv, wp = products[m]
                        ins = mm(psO[:, :], v_hl[:, wv, j, vs],
                                 pT[:, G % 2, wp, j, :, :].rearrange("p h n -> p (h n)"), m == 0, m == n_ - 1)
                    if part == QPG - 1:
                        ins.then_inc(pv, 1)
                i, part = (st_ - 21) // HQ, (st_ - 21) % HQ
                if 0 <= i < NT and part < NG:
                    pe.wait_ge(oT_lo, NG * i + part + 1)
                    if part == 0:
                        if i == 0:
                            pe.wait_ge(wo_lo, 4)
                        else:
                            pe.wait_ge(c_ready, i)
                    for h in range(part * QPG, (part + 1) * QPG):
                        ins = three(psM[:, 0:E], oT[:, 0, h, :], oT[:, 1, h, :], wo_hl[:, 0, h, :], wo_hl[:, 1, h, :],
                                    h == 0, h == HQ - 1)
                    if part == NG - 1:
                        ins.then_inc(wo_done, 1)
                if (i := at(st_, 27)) is not None:
                    norm_T(NT + i, psM[:, 256:512])
                if (i := at(st_, 29)) is not None:
                    if i == 0:
                        pe.wait_ge(loaded["wr"], 16)
                    pe.wait_ge(hT_ready, h_out(NT + i))
                    for k in range(KE):
                        ins = mm(psM[:, 0:P], hT[:, k, i * P:(i + 1) * P], wr[:, k, :], k == 0, k == KE - 1)
                    ins.then_inc(logit_ps, 1)
                if (i := at(st_, 33)) is not None:
                    pe.wait_ge(coeff_ready, i + 1)
                    te.transpose(psM[:, P:2 * P], coeff, ident[:, :]).then_inc(coT_ps, 1)
                if (i := at(st_, 34)) is not None:
                    pe.wait_ge(coT_ready, i + 1)
                    mm(psM[:, 2 * P:2 * P + NB], coeffT, mixs[:, :], True, True).then_inc(c_ps, 1)

            def experts0(t):
                if t == 0:
                    pe.wait_ge(w_lo, 7)
                for j in range(3):
                    if j == 2:
                        if t >= 2:
                            norm_T(2 * NT + t - 2, psO[:, 256:512])
                        if 1 <= t <= NT:
                            b = (t - 1) % 2
                            pe.wait_ge(basis_sum, t)
                            pe.wait_ge(pair_used, 3 * t)
                            if t >= 3:
                                pe.wait_ge(mix_lo, t - 2)
                            for c in range(3):
                                ins = te.transpose(psT[:, b, c * P:(c + 1) * P], mcat[:, b, c * P:(c + 1) * P],
                                                   ident[:, :])
                            ins.then_inc(mix_T, 1)
                    if t < NT:
                        pe.wait_ge(hlo_ready, t + 1)
                        ts_ = slice(t * P, (t + 1) * P)
                        p = 3 * t + j
                        if p >= 2:
                            pe.wait_ge(pair_used, p - 1)
                        for m in range(2 if j < 2 else 1):
                            for k in range(KE):
                                if j < 2:
                                    wh, wl = (wgu[:, w_, m, k, j * 512:(j + 1) * 512] for w_ in range(2))
                                else:
                                    wh, wl = (wsh[:, w_, k, :] for w_ in range(2))
                                ins = three(psS[:, 2 * (p % 2) + m, :], h_hl[:, 0, k, ts_], h_hl[:, 1, k, ts_],
                                            wh, wl, k == 0, k == KE - 1)
                        ins.then_inc(pair_ps, 1)
                if 1 <= t <= NT:
                    pe.wait_ge(mix_lo, t)
                    if t == 1:
                        pe.wait_ge(oT_lo, NGR)
                    else:
                        pe.wait_ge(hT_ready, h_out(2 * NT + t - 2))
                    for c in range(3):
                        cs_ = slice(c * P, (c + 1) * P)
                        ins = three(psO[:, 0:E], mcT[:, b, 0, cs_], mcT[:, b, 1, cs_], wdn[:, 0, c, :], wdn[:, 1, c, :],
                                    c == 0, c == 2)
                    ins.then_inc(down_ps, 1)

            def qkv(t):
                if t == 0:
                    pe.wait_ge(w_lo, 7 + KE)
                    pe.wait_ge(pair_used, 3 * NT)
                pe.wait_ge(hlo_ready, NT + t + 1)
                if t >= 2:
                    pe.wait_ge(qkv_read, t - 1)
                ts_ = slice(t * P, (t + 1) * P)
                for bank, c0, c1 in ((t % 2, 0, 2 * E), (2 + t % 2, 2 * E, 3 * E)):
                    for k in range(KE):
                        ins = three(psS[:, bank, 0:c1 - c0], h_hl[:, 0, k, ts_], h_hl[:, 1, k, ts_],
                                    w1a[:, 0, k, c0:c1], w1a[:, 1, k, c0:c1], k == 0, k == KE - 1)
                ins.then_inc(qkv_ps, 1)

            def identity_sum(ps, src, width):
                for k in range(H1):
                    ins = mm(ps, ident[:, :], src[:, k * width:(k + 1) * width], k == 0, k == H1 - 1)
                return ins

            def head_attention(t):
                if t + 1 < NT:
                    qkv(t + 1)
                if t < NT:
                    pe.wait_ge(prod1_ready, t + 1)
                    if t == 0:
                        pe.wait_ge(mix_lo, NT)
                    if t >= 2:
                        pe.wait_ge(sub_ready, t - 1)
                    identity_sum(psT[:, t % 2, 0:H1 * H1], prod1[:, t % 2, :], H1 * H1).then_inc(s_sum, 1)
                if t >= 1:
                    b = (t - 1) % 2
                    pe.wait_ge(prod2_ready, t)
                    if t == 1:
                        pe.wait_ge(c_ready, NT)
                        pe.wait_ge(hT_ready, h_out(3 * NT - 1))
                    if t >= 3:
                        pe.wait_ge(av_ready, 2 * (t - 2))
                    identity_sum((psO if b == 0 else psM)[:, 0:HPE * D1], prod2[b][:, 0:2048], HPE * D1) \
                        .then_inc(av_ps, 1)

            for st_ in range(NSTEP):
                attention(st_)
                for t in expert_steps(st_):
                    experts0(t)
            for t in EXPERTS_LEFT:
                if t == NT + 1:
                    qkv(0)
                    head_attention(0)
                experts0(t)
            for t in range(1, NT + 1):
                head_attention(t)

            pe.wait_ge(loaded["mixed"], 32)
            pe.wait_ge(loaded["gw"], 48)
            for t in range(NT + 4):
                if t < NT:
                    b = t % 2
                    if t >= 2:
                        pe.wait_ge(a_lo, t - 1)
                    for k in range(KE):
                        ins = te.transpose(psT[:, b, k * P:(k + 1) * P], mixed_rows[:, t, k * P:(k + 1) * P],
                                           ident[:, :])
                    ins.then_inc(a_T, 1)
                if 1 <= t <= NT:
                    i = t - 1
                    pe.wait_ge(a_lo, i + 1)
                    if i >= 2:
                        pe.wait_ge(var_ready, 2 * NT + i)
                    for k in range(KE):
                        ks = slice(k * P, (k + 1) * P)
                        ins = three(psO[:, 0:E] if i % 2 == 0 else psS[:, 1, 0:E], aT[:, i % 2, 0, ks],
                                    aT[:, i % 2, 1, ks], w1a[:, 0, k, 3 * E:4 * E], w1a[:, 1, k, 3 * E:4 * E],
                                    k == 0, k == KE - 1)
                    ins.then_inc(o_ps, 1)
                if 3 <= t < NT + 3:
                    if t >= 4:
                        pe.wait_ge(hT_ready, h_out(3 * NT + t - 4))
                    norm_T(3 * NT + t - 3, psM[:, 256:512])
                if 4 <= t < NT + 4:
                    i = t - 4
                    pe.wait_ge(hT_ready, h_out(3 * NT + i))
                    if i == 4:
                        pe.wait_ge(var_ready, 2 * NT + 2 + 6)
                    for k in range(KE):
                        ins = mm((psS[:, 0, :] if i < 4 else psO)[:, (i % 4) * NE:(i % 4 + 1) * NE],
                                 hT[:, k, i * P:(i + 1) * P], gwf[:, k, :], k == 0, k == KE - 1)
                    ins.then_inc(gate_ps, 1)
            for n_, m in (("w1", 16), ("w3", 16), ("w2", 32)):
                pe.wait_ge(loaded[n_], m)
            pe.wait_ge(gabs, 1)
            pe.wait_ge(var_ready, 3 * NT + 1)
            for t in range(NT + 2):
                for j in range(NCH):
                    if t < NT:
                        pe.wait_ge(hlo_ready, 2 * NT + t + 1)
                        ts_ = slice(t * P, (t + 1) * P)
                        p = NCH * t + j
                        w = 2 * INTER if j < NCH - 1 else INTER
                        if p >= 2:
                            pe.wait_ge(chunk_used, p - 1)
                        for m, wt in enumerate((w1b, w3b)):
                            for k in range(KE):
                                wcol = wt[:, k, 2 * INTER * j:2 * INTER * j + w]
                                mm(psS[:, 2 * (p % 2) + m, 0:w], h_hl[:, 0, k, ts_], wcol, k == 0, False)
                                ins = mm(psS[:, 2 * (p % 2) + m, 0:w], h_hl[:, 1, k, ts_], wcol, False, k == KE - 1)
                        ins.then_inc(chunk_ps, 1)
                    if j == 0 and t >= 2:
                        i = t - 2
                        pe.wait_ge(hc_lo, 4 * (i + 1))
                        pe.wait_ge(gabs, 3)
                        if i >= 1:
                            pe.wait_ge(x_out, i)
                        for e in range(KH):
                            w = min(P, HID - e * P)
                            for w_ in range(2):
                                ins = mm(psO[:, 0:E], hcT[0:w, i % 2, w_, e * P:(e + 1) * P], w2b[0:w, e, :],
                                         e == 0 and w_ == 0, e == KH - 1 and w_ == 1)
                        ins.then_inc(moe_ps, 1)
                    if j >= 1 and 1 <= t <= NT:
                        i, c = t - 1, j - 1
                        m = 4 * i + c
                        pe.wait_ge(chunk_used, NCH * t)
                        if m >= 2:
                            pe.wait_ge(hc_lo, m - 1)
                        for e in range(4 * c, min(4 * c + 4, KH)):
                            w = min(P, HID - e * P)
                            ins = te.transpose(psT[0:w, m % 2, (e % 4) * P:(e % 4 + 1) * P],
                                               hc[:, i % 2, e * P:e * P + w], ident[:, :])
                        ins.then_inc(hc_T, 1)


_INS = ["x", "cs", "wmod0", "wmod1", "wq", "bq", "wkv", "bk", "bv", "wo", "peT", "ident", "mask", "iota",
        "wr", "wg", "wu", "wd", "swg", "swu", "swd", "amp", "escale", "w1a", "b1a", "ropeC", "ropeS",
        "gw", "gb", "w1", "w3", "w2"]


def kernel(**inputs):
    import numpy as np
    import concourse.bacc as bacc
    from concourse.bass_utils import run_bass_kernel_spmd

    a = {k: np.asarray(v) for k, v in inputs.items()}
    f32 = np.float32
    S, E, D = 1024, 256, 128
    pos = np.arange(S, dtype=f32)[:, None]
    inv = np.exp(-(np.log(f32(10000.0)) * np.arange(0, D, 2, dtype=f32) / f32(D))).astype(f32)
    ang = (pos * inv).astype(f32)
    pe = np.zeros((S, D), f32)
    pe[:, 0::2], pe[:, 1::2] = np.sin(ang), np.cos(ang)
    inv1 = (f32(1.0) / f32(10000.0) ** (np.arange(0, 16, 2, dtype=f32) / f32(16))).astype(f32)
    fr = (pos * inv1).astype(f32)
    cos = np.repeat(np.cos(fr), 2, axis=1).reshape(8, 128, 16).transpose(1, 0, 2)
    sin = np.stack([-np.sin(fr), np.sin(fr)], -1).reshape(8, 128, 16).transpose(1, 0, 2)
    bkv = a["L0_attn_bkv"].reshape(4, 2, 128)
    d = {
        "x": a["L0_attn_x"].reshape(S, E),
        "cs": np.concatenate([a["L0_c"].reshape(2, 128), a["L1_c"].reshape(2, 128)]).T,
        "wmod0": a["L0_wmod"], "wmod1": a["L1_wmod"],
        "wq": a["L0_attn_wq"], "bq": a["L0_attn_bq"].reshape(16, 128).T,
        "wkv": a["L0_attn_wkv"], "bk": bkv[:, 0].T, "bv": bkv[:, 1].reshape(1, 512),
        "wo": a["L0_attn_wo"], "peT": pe.T, "ident": np.eye(128, dtype=f32),
        "mask": np.triu(np.full((128, 128), -1e30, f32), 1), "iota": np.arange(128, dtype=f32)[None],
        "wr": a["L0_ffn_w_router"], "wg": a["L0_ffn_w_gate"], "wu": a["L0_ffn_w_up"], "wd": a["L0_ffn_w_down"],
        "swg": a["L0_ffn_shared_w_gate"], "swu": a["L0_ffn_shared_w_up"], "swd": a["L0_ffn_shared_w_down"],
        "amp": a["L0_ffn_amplitudes"].reshape(128, 16), "escale": a["L0_ffn_expert_scale"].reshape(128, 1),
        "w1a": np.concatenate([a[f"L1_attn_W{n}"].T for n in "qkvo"], axis=1),
        "b1a": np.concatenate([a[f"L1_attn_b{n}"] for n in "qkvo"])[None],
        "ropeC": cos.reshape(128, 128), "ropeS": sin.reshape(128, 128),
        "gw": a["L1_ffn_gate_w"].T, "gb": a["L1_ffn_gate_b"].reshape(1, 8),
        "w1": np.concatenate([a["L1_ffn_w1"].reshape(1408, 256), a["L1_ffn_sw1"]]).T,
        "w3": np.concatenate([a["L1_ffn_w3"].reshape(1408, 256), a["L1_ffn_sw3"]]).T,
        "w2": np.concatenate([a["L1_ffn_w2"].transpose(0, 2, 1).reshape(1408, 256), a["L1_ffn_sw2"].T]),
    }
    nc = bacc.Bacc("TRN2", target_bir_lowering=False, num_devices=1)
    arrays, aps = {}, {}
    for name in _INS:
        v = np.ascontiguousarray(d[name])
        arrays[f"in_{name}"] = v
        aps[name] = nc.dram_tensor(f"in_{name}", v.shape, mybir.dt.from_np(v.dtype), kind="ExternalInput").ap()
    out = nc.dram_tensor("out", (S, E), F32, kind="ExternalOutput").ap()
    build_program(nc, aps, out)
    r = run_bass_kernel_spmd(nc, [arrays], core_ids=[0])
    return r.results[0]["out"].reshape(1, S, E)
```

```python
from contextlib import ExitStack

import concourse.bass as bass
from concourse import mybir

P = 128
F32 = mybir.dt.float32
BF16 = mybir.dt.bfloat16
U32 = mybir.dt.uint32
ALU = mybir.AluOpType
ACT = mybir.ActivationFunctionType
AX = mybir.AxisListType

LN_EPS = 1e-5
TOP_EPS = 1e-8
GATE_FLOOR = 0.25


def build_program(nc, d, out):
    S, E = d["x"].shape
    NT = S // P
    KE = E // P
    HQ = d["wq"].shape[1] // P
    NG = d["wkv"].shape[1] // (2 * P)
    QPG = HQ // NG
    NU = NT * HQ
    NGR = NT * NG
    NB = 8
    NX = d["wr"].shape[1]
    H1, D1 = 16, E // 16
    INTER, NE = 176, 8
    HID = INTER * (NE + 1)
    KH = -(-HID // P)
    SCALE0 = float(P) ** -0.5
    SCALE1 = float(D1) ** -0.5
    HPE = 8
    LAG = 3

    with ExitStack() as ctx:
        def sb(name, shape, dt=F32):
            return ctx.enter_context(nc.sbuf_tensor(name, shape, dt))

        def sem(name):
            return ctx.enter_context(nc.semaphore(name))

        x = sb("x", [P, NT, E])
        hT = sb("hT", [P, KE, S])
        wq_region = sb("wq_region", [P, KE * HQ * P])
        wkv_region = sb("wkv_region", [P, KE * 2 * NG * P])
        q_region = sb("q_region", [P, NT * HQ * P])
        k_region = sb("k_region", [P, NG * S])
        v_region = sb("v_region", [P, NT * NG * P])
        pt_region = sb("pt_region", [P, 8192])
        wo_region = sb("wo_region", [P, HQ * E])
        peT = sb("peT", [P, S])
        bvB = sb("bvB", [P, NG * P])
        xn = sb("xn", [P, 2, E])
        tmp = sb("tmp", [P, 2, 512])
        gates = sb("gates", [P, 2, 2, E])
        modcol = sb("modcol", [P, 2, 8])
        ident = sb("ident", [P, P])
        ident_b = sb("ident_b", [P, P], BF16)
        mask_b = sb("mask_b", [P, P], BF16)
        mask_f = sb("mask_f", [P, P])
        csB = sb("csB", [P, 4, P])
        half = sb("half", [P, NT * NE])
        c_tok = sb("c_tok", [P, NT, NB])
        cs = sb("cs", [P, 4])
        cth = sb("cth", [P, 4])
        bq = sb("bq", [P, HQ])
        bk = sb("bk", [P, NG])
        mhalf = sb("mhalf", [P, NT])
        mv = sb("mv", [P, NT, 2])
        st = sb("st", [P, 2, 6])
        mv2 = sb("mv2", [P, 2, 2])
        ve = sb("ve", [P, 2])
        rstd = sb("rstd", [P, 2])
        ve0 = sb("ve0", [P, NT])
        rstd0 = sb("rstd0", [P, NT])
        negmax = sb("negmax", [P, 4])
        rowsum = sb("rowsum", [P, 4])
        rinv = sb("rinv", [P, 4])
        mixs = sb("mixs", [P, NB])
        small = sb("small", [P, 64])

        wq = wq_region[:, :].rearrange("p (k n) -> p k n", k=KE)
        wkv = wkv_region[:, :].rearrange("p (k n) -> p k n", k=KE)
        probs = wq_region[:, :].rearrange("p (r n) -> p r n", r=4)
        oT = wkv_region[:, :].bitcast(BF16).rearrange("p (w h n) -> p w h n", w=2, h=HQ)
        qT = q_region[:, :].rearrange("p (t h n) -> p t h n", t=NT, h=HQ)
        kT = k_region[:, :].rearrange("p (g n) -> p g n", g=NG)
        v_hl = v_region[:, :].bitcast(BF16).rearrange("p (w t n) -> p w t n", w=2, t=NT)
        pT = pt_region[:, :].bitcast(BF16).rearrange("p (b w j h n) -> p b w j h n", b=2, w=2, j=NT, h=QPG)
        wo_hl = wo_region[:, :].bitcast(BF16).rearrange("p (w h n) -> p w h n", w=2, h=HQ)
        wmod = pt_region[:, 0:2 * KE * 6 * E].rearrange("p (l k n) -> p l k n", l=2, k=KE)
        wo_stage = pt_region[:, 2 * KE * 6 * E:8192].rearrange("p (b h n) -> p b h n", b=2, h=4)
        modrow = xn[:, :, :].rearrange("p a n -> p (a n)")

        def slot(a, b):
            w = HQ * P
            return q_region[:, a * w:b * w]

        h_hl = slot(0, 1).bitcast(BF16).rearrange("p (w k n) -> p w k n", w=2, k=KE)
        wgu_f = slot(1, 3).rearrange("p (m k n) -> p m k n", m=2, k=KE)
        wr = peT[:, 0:KE * NX].rearrange("p (k n) -> p k n", k=KE)
        wsh_f = slot(3, 4)[:, 256:256 + 1024].rearrange("p (k n) -> p k n", k=KE)
        wdn_f = slot(3, 4)[:, 1280:1280 + 768].rearrange("p (k n) -> p k n", k=3)
        wgu = slot(4, 6).bitcast(BF16).rearrange("p (w m k n) -> p w m k n", w=2, m=2, k=KE)
        wsh = slot(6, 7)[:, 0:1024].bitcast(BF16).rearrange("p (w k n) -> p w k n", w=2, k=KE)
        wdn = slot(6, 7)[:, 1024:1792].bitcast(BF16).rearrange("p (w k n) -> p w k n", w=2, k=3)
        sc = pt_region
        th0 = sc[:, 0:1024].rearrange("p (b n) -> p b n", b=4)
        act0 = sc[:, 1024:2048].rearrange("p (b n) -> p b n", b=4)
        basis = sc[:, 2048:4096].rearrange("p (b k n) -> p b k n", b=2, k=NB)
        tree = wq_region[:, 0:768]
        mcat = wq_region[:, 768:1536].rearrange("p (b n) -> p b n", b=2)
        mcT = wq_region[:, 1536:2304].bitcast(BF16).rearrange("p (b w n) -> p b w n", b=2, w=2)
        logit, eexp, onehot, coeff = (bvB[:, m * P:(m + 1) * P] for m in range(4))
        iota, coeffT = csB[:, 0, :], csB[:, 1, :]
        w1b = k_region[:, 0:HID].bitcast(BF16).rearrange("p (k n) -> p k n", k=KE)
        w3b = k_region[:, HID:2 * HID].bitcast(BF16).rearrange("p (k n) -> p k n", k=KE)
        w2b = v_region[:, 0:KH * E // 2].bitcast(BF16).rearrange("p (k n) -> p k n", k=KH)
        w1a_f = v_region[:, 1664:1664 + KE * 4 * E].rearrange("p (k n) -> p k n", k=KE)
        w1a = wo_region[:, 0:KE * 4 * E].bitcast(BF16).rearrange("p (w k n) -> p w k n", w=2, k=KE)
        b1a = wo_region[:, 2048:2048 + 4 * E]
        ropeC = wo_region[:, 3072:3072 + NT * D1].rearrange("p (t n) -> p t n", t=NT)
        ropeS = wo_region[:, 3200:3200 + NT * D1].rearrange("p (t n) -> p t n", t=NT)
        gwf = wo_region[:, 3328:3328 + KE * NE].rearrange("p (k n) -> p k n", k=KE)
        gbB = wo_region[:, 3344:3344 + NE]
        iota1 = wo_region[:, 3352:3352 + NE]
        prod1 = slot(1, 5).rearrange("p (b n) -> p b n", b=2)
        prod2 = [wq_region[:, :], pt_region[:, 4096:8192]]
        qkb = slot(5, 6)[:, 0:1024].rearrange("p (b n) -> p b n", b=2)
        vb = slot(5, 6)[:, 1024:1792].rearrange("p (b n) -> p b n", b=3)
        ropeA = slot(6, 7)[:, 0:512]
        ropeB = slot(6, 7)[:, 512:1024]
        qkr = pt_region[:, 0:1024].rearrange("p (b n) -> p b n", b=2)
        ssub = slot(7, 8)[:, 0:256]
        e1 = slot(7, 8)[:, 256:768].rearrange("p (b n) -> p b n", b=2)
        av = slot(7, 8)[:, 768:1280].rearrange("p (b n) -> p b n", b=2)
        avr = slot(7, 8)[:, 1280:1280 + (H1 - HPE) * D1]
        m1 = slot(7, 8)[:, 1536:1568].rearrange("p (b n) -> p b n", b=2)
        r1 = slot(7, 8)[:, 1568:1600].rearrange("p (b n) -> p b n", b=2)
        mixed_rows = pt_region[:, 0:NT * E].rearrange("p (t n) -> p t n", t=NT)
        aT = slot(7, 8).bitcast(BF16).rearrange("p (b w n) -> p b w n", b=NT // 2, w=2)
        gbo = pt_region[:, 2816:3072]
        hc = slot(1, 3)[:, 0:2 * HID].rearrange("p (b n) -> p b n", b=2)
        hcT = slot(3, 5)[:, 0:2 * KH * P].bitcast(BF16).rearrange("p (b w n) -> p b w n", b=2, w=2)
        th1 = slot(5, 6)[:, 0:704].rearrange("p (b n) -> p b n", b=2)
        a1 = slot(5, 6)[:, 704:1408].rearrange("p (b n) -> p b n", b=2)
        cw = slot(6, 7)[:, 0:NT * NE].rearrange("p (t n) -> p t n", t=NT)
        g_s = slot(6, 7)[:, 256:320]
        g_a = slot(6, 7)[:, 320:384]
        g_b = slot(6, 7)[:, 384:448]
        g_c = slot(6, 7)[:, 448:512]
        g_m = slot(6, 7)[:, 512:576]
        g_x = slot(6, 7)[:, 576:640]
        g_i = slot(6, 7)[:, 640:704]
        g_u = slot(6, 7)[:, 704:768].bitcast(U32)
        g_r = slot(6, 7)[:, 768:832]

        psS = ctx.enter_context(nc.psum_tensor("psS", [P, 4, 512], F32))
        psT = ctx.enter_context(nc.psum_tensor("psT", [P, 2, 512], F32))
        psO = ctx.enter_context(nc.psum_tensor("psO", [P, 512], F32))
        psM = ctx.enter_context(nc.psum_tensor("psM", [P, 512], F32))
        scratch = nc.dram_tensor("head_shuffle", [H1, S, D1], F32, kind="Internal").ap()

        names_loaded = ["cs", "xa", "xb", "wmod0a", "wmod0b", "wmod1", "wkv", "wq", "peT", "bvB", "ident", "mask",
                        "bq", "bk", "wgu", "wr", "wsh", "wdn", "iota", "amp", "w1", "w3", "w2", "w1a", "b1a",
                        "rope", "gw", "escale"]
        loaded = {n: sem("loaded_" + n) for n in names_loaded}
        loaded["mixed"] = [sem(f"loaded_mixed{n}") for n in range(2)]
        wo_loaded = [sem(f"wo_loaded{c}") for c in range(4)]
        ve_chain = sem("vector_chain")
        po_chain = sem("pool_chain")
        cond_tanh = sem("cond_tanh")
        cond_rows = sem("cond_rows")
        mod_ps = sem("mod_ps")
        mod_rows = sem("mod_rows")
        mod_T = sem("mod_T")
        mod_done = sem("mod_done")
        var_ready = sem("var_ready")
        rstd_ready = sem("rstd_ready")
        xn_ready = sem("xn_ready")
        xn_T = sem("xn_T")
        hT_ready = sem("hT_ready")
        hlo_ready = sem("hlo_ready")
        hlo1_ready = sem("hlo1_ready")
        proj_done = sem("proj_done")
        tmp_ready = sem("tmp_ready")
        tmp_used = sem("tmp_used")
        q_ready = sem("q_ready")
        wo_hi = sem("wo_hi")
        wo_lo = sem("wo_lo")
        masks_ready = sem("masks_ready")
        scores = sem("scores")
        negmax_ready = sem("negmax_ready")
        exp_done = sem("exp_done")
        rinv_ready = sem("rinv_ready")
        normed = sem("normed")
        pT_ps = sem("pT_ps")
        pT_hi = sem("pT_hi")
        pT_lo = sem("pT_lo")
        pv = sem("pv")
        oT_hi = sem("oT_hi")
        oT_lo = sem("oT_lo")
        wo_done = sem("wo_done")
        w_hi = sem("w_hi")
        w_lo = sem("w_lo")
        logit_ps = sem("logit_ps")
        neg_ready = sem("neg_ready")
        e_ready = sem("e_ready")
        coeff_ready = sem("coeff_ready")
        coT_ps = sem("coT_ps")
        coT_ready = sem("coT_ready")
        c_ps = sem("c_ps")
        c_ready = sem("c_ready")
        pair_ps = sem("pair_ps")
        tanh_ready = sem("tanh_ready")
        pair_used = sem("pair_used")
        basis_sum = sem("basis_sum")
        prod2b_ready = sem("prod2b_ready")
        av_ps = sem("av_ps")
        mix_T = sem("mix_T")
        mix_hi = sem("mix_hi")
        mix_lo = sem("mix_lo")
        down_ps = sem("down_ps")
        down_read = sem("down_read")
        qkv_ps = sem("qkv_ps")
        qkv_read = sem("qkv_read")
        prod1_ready = sem("prod1_ready")
        s_sum = sem("s_sum")
        sub_ready = sem("sub_ready")
        e1_ready = sem("e1_ready")
        prod2_ready = sem("prod2_ready")
        prod2_used = sem("prod2_used")
        av_ready = sem("av_ready")
        shuffled = [sem(f"shuffled{t}") for t in range(NT)]
        a_T = sem("a_T")
        a_hi = sem("a_hi")
        a_lo = sem("a_lo")
        o_ps = sem("o_ps")
        gate_ps = sem("gate_ps")
        o_read = sem("o_read")
        gexp = sem("gexp")
        gabs = sem("gabs")
        sp_ready = sem("sp_ready")
        sq_ready = sem("sq_ready")
        chunk_ps = sem("chunk_ps")
        chunk_tanh = sem("chunk_tanh")
        chunk_used = sem("chunk_used")
        hc_T = sem("hc_T")
        hc_hi = sem("hc_hi")
        hc_lo = sem("hc_lo")
        moe_ps = sem("moe_ps")
        x_out = sem("x_out")
        stored = sem("stored")

        def unit(u):
            return u // HQ, u % HQ

        def chunks(i):
            return [(c, min(4, i + 1 - c)) for c in range(0, i + 1, 4)]

        chunk_end = []
        for u in range(NU):
            chunk_end.append((chunk_end[-1] if u else 0) + len(chunks(unit(u)[0])))

        proj = [("k", g, n) for n in (0,) for g in range(NG)] + [("v", i, 0) for i in range(NT // 2)]
        proj += [("k", g, 1) for g in range(NG)] + [("v", i, 0) for i in range(NT // 2, NT)]
        NKV = len(proj)
        proj += [("q", h, n) for n in range(2) for h in range(HQ)]

        def expert_steps(st_):
            return [(st_ - NU - 6) // 3] if st_ >= NU + 6 and (st_ - NU - 6) % 3 == 0 else []

        NSTEP = NU + 20
        EXPERTS_LEFT = range(len([1 for n_ in range(NSTEP) if expert_steps(n_)]), NT + 3)

        def at(st_, first):
            i = (st_ - first) // HQ
            return i if st_ >= first and (st_ - first) % HQ == 0 and i < NT else None

        MOD = [(0, 0), (0, 1), (0, 2), (1, 0), (1, 1), (1, 2)]

        MOD_AT = [None] + [NKV + 4 + 5 * n_ for n_ in range(5)]
        WSPLIT = [(NT - 1) * HQ + 1 + 2 * n_ for n_ in range(6)]
        VALS = HPE * E

        def heads_dve(t):
            return 2 if t < NT - 1 else H1 - HPE

        NCH = NE // 2 + 1

        NP = NT // 2
        TAIL = [(w, None) for w in range(NP + 3)]
        for n_ in range((NT + 2) * NCH):
            TAIL.append((n_ // NCH, n_ % NCH))
            if n_ == 1:
                TAIL.append((NP + 3, None))
        RB = [(0, 2), (2, NT)]
        TB = [(0, 2), (2, 4), (4, NT)]
        HALFWAY = (0, 3)

        block = ctx.enter_context(nc.Block())

        @block.sync
        def _(sp):
            sp.dma_start(cs[:, :], d["cs"]).then_inc(loaded["cs"], 16)
            xv = d["x"].rearrange("(t p) n -> p t n", p=P)
            wm = [d[f"wmod{n}"].rearrange("(k p) n -> p k n", p=P) for n in range(2)]
            sp.dma_start(wmod[:, 0, :, 0:2 * E], wm[0][:, :, 0:2 * E]).then_inc(loaded["wmod0a"], 16)
            sp.dma_start(x[:, 0:4, :], xv[:, 0:4, :]).then_inc(loaded["xa"], 16)
            sp.dma_start(ident[:, :], d["ident"]).then_inc(loaded["ident"], 16)
            sp.dma_start(x[:, 4:8, :], xv[:, 4:8, :]).then_inc(loaded["xb"], 16)
            sp.dma_start(wkv, d["wkv"].rearrange("(k p) n -> p k n", p=P)).then_inc(loaded["wkv"], 16)
            sp.dma_start(peT[:, :], d["peT"]).then_inc(loaded["peT"], 16)
            sp.dma_start(bk[:, :], d["bk"]).then_inc(loaded["bk"], 16)
            sp.dma_start(bvB[:, :], d["bv"].partition_broadcast(P)).then_inc(loaded["bvB"], 16)
            sp.dma_start(mask_f[:, :], d["mask"]).then_inc(loaded["mask"], 16)
            sp.dma_start(bq[:, :], d["bq"]).then_inc(loaded["bq"], 16)
            sp.dma_start(wq, d["wq"].rearrange("(k p) n -> p k n", p=P)).then_inc(loaded["wq"], 16)
            sp.dma_start(small[:, 0:16], d["amp"]).then_inc(loaded["amp"], 16)
            sp.dma_start(small[:, 16:17], d["escale"]).then_inc(loaded["escale"], 16)
            sp.dma_start(wmod[:, 0, :, 2 * E:6 * E], wm[0][:, :, 2 * E:6 * E]).then_inc(loaded["wmod0b"], 16)
            sp.dma_start(wmod[:, 1, :, :], wm[1]).then_inc(loaded["wmod1"], 16)
            wov = d["wo"].rearrange("(h p) n -> p h n", p=P)
            for c in range(4):
                if c >= 2:
                    sp.wait_ge(wo_lo, c - 1)
                sp.dma_start(wo_stage[:, c % 2, :, :], wov[:, 4 * c:4 * c + 4, :]).then_inc(wo_loaded[c], 16)
            sp.wait_ge(mod_ps, 6)
            sp.dma_start(iota, d["iota"].partition_broadcast(P)).then_inc(loaded["iota"], 16)
            sp.wait_ge(q_ready, 2 * HQ)
            sp.dma_start(wr, d["wr"].rearrange("(k p) n -> p k n", p=P)).then_inc(loaded["wr"], 16)
            sp.wait_ge(scores, 3 * HQ)
            for m, n in enumerate(("wg", "wu")):
                sp.dma_start(wgu_f[:, m, :, :], d[n].rearrange("(k p) n -> p k n", p=P)).then_inc(loaded["wgu"], 16)
            sp.wait_ge(scores, 4 * HQ)
            for m, n in enumerate(("swg", "swu")):
                sp.dma_start(wsh_f[:, :, m * E:(m + 1) * E],
                             d[n].rearrange("(k p) n -> p k n", p=P)).then_inc(loaded["wsh"], 16)
            sp.dma_start(wdn_f[:, 0:1, :], d["wd"].rearrange("(k p) n -> p k n", p=P)).then_inc(loaded["wdn"], 16)
            sp.dma_start(wdn_f[:, 1:3, :], d["swd"].rearrange("(k p) n -> p k n", p=P)).then_inc(loaded["wdn"], 16)
            sp.wait_ge(scores, NU)
            sp.dma_start(w1b, d["w1"].rearrange("(k p) n -> p k n", p=P)).then_inc(loaded["w1"], 16)
            sp.dma_start(w3b, d["w3"].rearrange("(k p) n -> p k n", p=P)).then_inc(loaded["w3"], 16)
            sp.wait_ge(pv, NGR)
            sp.dma_start(w1a_f, d["w1a"].rearrange("(k p) n -> p k n", p=P)).then_inc(loaded["w1a"], 16)
            full = HID // P
            sp.dma_start(w2b[:, 0:full, :], d["w2"][0:full * P, :].rearrange("(k p) n -> p k n", p=P)) \
                .then_inc(loaded["w2"], 16)
            sp.dma_start(w2b[0:HID - full * P, full, :], d["w2"][full * P:HID, :]).then_inc(loaded["w2"], 16)
            sp.wait_ge(wo_done, NT)
            sp.dma_start(b1a, d["b1a"].partition_broadcast(P)).then_inc(loaded["b1a"], 16)
            sp.dma_start(ropeC, d["ropeC"].rearrange("p (t n) -> p t n", t=NT)).then_inc(loaded["rope"], 16)
            sp.dma_start(ropeS, d["ropeS"].rearrange("p (t n) -> p t n", t=NT)).then_inc(loaded["rope"], 16)
            sp.dma_start(gwf, d["gw"].rearrange("(k p) n -> p k n", p=P)).then_inc(loaded["gw"], 16)
            sp.dma_start(gbB, d["gb"].partition_broadcast(P)).then_inc(loaded["gw"], 16)
            sp.dma_start(iota1, d["iota"][:, 0:NE].partition_broadcast(P)).then_inc(loaded["gw"], 16)
            for t in range(NT):
                sp.wait_ge(av_ready, 2 * (t + 1))
                sp.dma_start(scratch[:, t * P:(t + 1) * P, :].rearrange("h p n -> p h n"),
                             av[:, t % 2, :].rearrange("p (h n) -> p h n", h=H1)).then_inc(shuffled[t], 16)
            for t in range(NT):
                sp.wait_ge(shuffled[t], 16)
            rows = scratch.rearrange("h s n -> (h s n)").rearrange("(t p n) -> p t n", p=P, n=E)
            for j in range(2):
                sp.dma_start(mixed_rows[:, 4 * j:4 * j + 4, :], rows[:, 4 * j:4 * j + 4, :]) \
                    .then_inc(loaded["mixed"][j], 16)
            ov = out.rearrange("(t p) n -> p t n", p=P)
            for t in range(NT):
                sp.wait_ge(x_out, t + 1)
                sp.dma_start(ov[:, t, :], x[:, t, :]).then_inc(stored, 16)
            sp.wait_ge(stored, 16 * NT)

        @block.gpsimd
        def _(pool):
            g = nc.gpsimd
            n = [0]

            def link(ins):
                n[0] += 1
                ins.then_inc(po_chain, 1)
                pool.wait_ge(po_chain, n[0])

            link(g.memset(mhalf[:, :], -0.5))
            link(g.memset(half[:, :], 0.5))
            pool.wait_ge(var_ready, 1)
            g.tensor_tensor(rstd0[:, :], ve0[:, :], mhalf[:, :], ALU.pow).then_inc(rstd_ready, 1)

            def rstd_of(q):
                pool.wait_ge(var_ready, q - NT + 2)
                g.tensor_tensor(rstd[:, q % 2:q % 2 + 1], ve[:, q % 2:q % 2 + 1], mhalf[:, 0:1], ALU.pow) \
                    .then_inc(rstd_ready, 1)

            for u in range(NU):
                i, h = unit(u)
                w = (i + 1) * P
                pool.wait_ge(rinv_ready, u + 1)
                g.tensor_tensor(probs[:, u % 4, 0:w], probs[:, u % 4, 0:w],
                                rinv[:, u % 4:u % 4 + 1].to_broadcast([P, w]), ALU.mult).then_inc(normed, 1)
                if u >= 24 and (u - 24) % HQ == 0:
                    rstd_of(NT + (u - 24) // HQ)

            def tree_sum(t):
                b = t % 2
                pool.wait_ge(pair_used, 5 * t + 4)
                link(g.tensor_tensor(tree[:, 0:512], basis[:, b, 0:4, :], basis[:, b, 4:8, :], ALU.add))
                link(g.tensor_tensor(tree[:, 512:768], tree[:, 0:256], tree[:, 256:512], ALU.add))
                if t >= 2:
                    pool.wait_ge(mix_T, t - 1)
                g.tensor_tensor(mcat[:, b, 0:P], tree[:, 512:640], tree[:, 640:768], ALU.add).then_inc(basis_sum, 1)

            tree_sum(0)
            rstd_of(2 * NT - 1)

            def weigh_values(t):
                pool.wait_ge(e1_ready, t + 1)
                pool.wait_ge(qkv_read, t + 1)
                if t >= 2:
                    pool.wait_ge(av_ps, t - 1)
                    pool.wait_ge(prod2_used, t - 1)
                eb = e1[:, t % 2, :].rearrange("p (h t) -> p h t", h=H1)
                vv = vb[:, t % 3, :].rearrange("p (t d) -> p t d", t=H1)
                g.tensor_tensor(prod2[t % 2][:, 0:VALS].rearrange("p (t h d) -> p t h d", t=H1, h=HPE),
                                eb[:, 0:HPE, :].rearrange("p h t -> p t h").unsqueeze(3)
                                .to_broadcast([P, H1, HPE, D1]),
                                vv.unsqueeze(2).to_broadcast([P, H1, HPE, D1]), ALU.mult).then_inc(prod2_ready, 1)
                hm = H1 - HPE - heads_dve(t)
                if hm:
                    g.tensor_tensor(prod2[t % 2][:, VALS:VALS + hm * E].rearrange("p (h d t) -> p h d t", h=hm, d=D1),
                                    eb[:, HPE:HPE + hm, :].unsqueeze(2).to_broadcast([P, hm, D1, H1]),
                                    vv.rearrange("p t d -> p d t").unsqueeze(1).to_broadcast([P, hm, D1, H1]),
                                    ALU.mult).then_inc(prod2b_ready, 1)

            def h_low(q):
                its = slice(q % NT * P, (q % NT + 1) * P)
                pool.wait_ge(hT_ready, 2 * NT + 4 * (q - NT + 1))
                g.tensor_tensor(h_hl[:, 1, :, its], hT[:, :, its], h_hl[:, 0, :, its], ALU.subtract) \
                    .then_inc(hlo1_ready, 1)

            for t in range(NT + 3):
                if 1 <= t < NT:
                    tree_sum(t)
                if 2 <= t < NT + 2:
                    rstd_of(2 * NT + t - 2)
                if t >= 3:
                    h_low(2 * NT + t - 3)
            for t in range(NT):
                weigh_values(t)

            def root(n_):
                pool.wait_ge(sp_ready, 1 if n_ == 0 else 2)
                bs = slice(NE * TB[n_][0], NE * TB[n_][1])
                g.tensor_tensor(g_r[:, bs], g_c[:, bs], half[:, bs], ALU.pow).then_inc(sq_ready, 1)

            for t in range(NP + 4):
                if 2 <= t < NP + 2:
                    pool.wait_ge(var_ready, 2 * NT + t)
                    g.tensor_tensor(rstd[:, :], ve[:, :], mhalf[:, 0:2], ALU.pow).then_inc(rstd_ready, 1)
                if t >= 4:
                    its = slice(2 * (t - 4) * P, 2 * (t - 3) * P)
                    pool.wait_ge(hT_ready, 2 * NT + 8 * NT + 4 * (t - 3))
                    g.tensor_tensor(h_hl[:, 1, :, its], hT[:, :, its], h_hl[:, 0, :, its], ALU.subtract) \
                        .then_inc(hlo1_ready, 1)
                if t == NP + 1:
                    root(0)
            root(1)
            root(2)

        @block.scalar
        def _(act):
            s = nc.scalar
            act.wait_ge(loaded["cs"], 16)
            s.activation(cth[:, :], cs[:, :], ACT.Tanh, scale=0.5).then_inc(cond_tanh, 1)

            def norm_out(q, ps, layer, which, halves):
                i = q % NT
                act.wait_ge(xn_T, q + 1)
                for k in range(KE):
                    o = which * 4
                    sh = modcol[:, layer, o + k:o + k + 1]
                    sc_ = modcol[:, layer, o + 2 + k:o + 3 + k]
                    src = ps[:, k * P:(k + 1) * P]
                    s.activation(hT[:, k, i * P:(i + 1) * P], src, ACT.Identity, bias=sh, scale=sc_) \
                        .then_inc(hT_ready, 1)
                    if halves:
                        s.activation(h_hl[:, 0, k, i * P:(i + 1) * P], src, ACT.Identity, bias=sh, scale=sc_) \
                            .then_inc(hT_ready, 1)

            act.wait_ge(mod_done, 1)
            for i in range(NT):
                norm_out(i, psT[:, i % 2, :], 0, 0, False)
            for m in range(NKV):
                kind, a, b = proj[m]
                act.wait_ge(tmp_ready, m + 1)
                if kind == "k":
                    s.activation(kT[:, a, b * 512:(b + 1) * 512], tmp[:, m % 2, :], ACT.Copy, scale=SCALE0) \
                        .then_inc(tmp_used, 1)
                else:
                    s.activation(v_hl[:, 0, a, :], tmp[:, m % 2, :], ACT.Copy).then_inc(tmp_used, 1)
            for c in range(4):
                act.wait_ge(wo_loaded[c], 16)
                s.activation(wo_hl[:, 0, 4 * c:4 * c + 4, :], wo_stage[:, c % 2, :, :], ACT.Copy).then_inc(wo_hi, 1)

            def weights_high(n_):
                if n_ < 4:
                    m, k = n_ // 2, n_ % 2
                    act.wait_ge(loaded["wgu"], 32)
                    s.activation(wgu[:, 0, m, k, :], wgu_f[:, m, k, :], ACT.Copy).then_inc(w_hi, 1)
                elif n_ == 4:
                    act.wait_ge(loaded["wsh"], 32)
                    s.activation(wsh[:, 0, :, :], wsh_f, ACT.Copy).then_inc(w_hi, 1)
                else:
                    act.wait_ge(loaded["wdn"], 32)
                    s.activation(wdn[:, 0, 0, :], wdn_f[:, 0, :], ACT.Copy).then_inc(w_hi, 1)
                    s.activation(wdn[:, 0, 1:3, :], wdn_f[:, 1:3, :], ACT.Copy, scale=0.5).then_inc(w_hi, 1)

            nh = [0]

            def attention(st_):
                G = (st_ - 11) // QPG
                if (st_ - 11) % QPG == 0 and 0 <= G < NGR:
                    act.wait_ge(pv, G + 1)
                    if G >= NG:
                        act.wait_ge(wo_done, G // NG)
                    s.activation(oT[:, 0, (G % NG) * QPG:(G % NG + 1) * QPG, :],
                                 psO[:, :].rearrange("p (h n) -> p h n", h=QPG), ACT.Copy).then_inc(oT_hi, 1)
                if LAG <= st_ < NU + LAG:
                    u = st_ - LAG
                    i, h = unit(u)
                    G = u // QPG
                    if G >= 2:
                        act.wait_ge(pv, G - 1)
                    for c, k in chunks(i):
                        act.wait_ge(pT_ps, nh[0] + 1)
                        s.activation(pT[:, G % 2, 0, c:c + k, h % QPG, :],
                                     psT[:, nh[0] % 2, 0:k * P].rearrange("p (k n) -> p k n", k=k),
                                     ACT.Copy).then_inc(pT_hi, 1)
                        nh[0] += 1
                if st_ < NU:
                    u = st_
                    i, h = unit(u)
                    w = (i + 1) * P
                    act.wait_ge(negmax_ready, u + 1)
                    if u >= 4:
                        act.wait_ge(pT_ps, chunk_end[u - 4])
                    s.activation(probs[:, u % 4, 0:w], psS[:, 2 * (u % 2):2 * (u % 2) + 2, :]
                                 .rearrange("p a n -> p (a n)")[:, 0:w], ACT.Exp,
                                 bias=negmax[:, u % 4:u % 4 + 1], accum_out=rowsum[:, u % 4:u % 4 + 1]) \
                        .then_inc(exp_done, 1)
                if (i := at(st_, 27)) is not None:
                    norm_out(NT + i, psM[:, 256:512], 0, 1, True)
                if st_ in WSPLIT:
                    weights_high(WSPLIT.index(st_))
                if (i := at(st_, 31)) is not None:
                    act.wait_ge(neg_ready, i + 1)
                    s.activation(eexp, logit, ACT.Exp, bias=small[:, 28:29], accum_out=small[:, 29:30]) \
                        .then_inc(e_ready, 1)
                    s.activation(small[:, 30:34], small[:, 20:24], ACT.Exp, bias=small[:, 28:29],
                                 accum_out=small[:, 34:35]).then_inc(e_ready, 1)
                if (i := at(st_, 33)) is not None:
                    act.wait_ge(coT_ps, i + 1)
                    s.activation(coeffT, psM[:, P:2 * P], ACT.Copy).then_inc(coT_ready, 1)

            def experts0(t):
                for j in range(5):
                    if t < NT:
                        p = 5 * t + j
                        act.wait_ge(pair_ps, p + 1)
                        if p >= 4:
                            act.wait_ge(pair_used, p - 3)
                        s.activation(th0[:, p % 4, :], psS[:, p % 4, 0:256], ACT.Tanh, scale=0.5) \
                            .then_inc(tanh_ready, 1)
                    if j == 1 and 1 <= t <= NT:
                        act.wait_ge(mix_T, t)
                        s.activation(mcT[:, (t - 1) % 2, 0, :], psT[:, 0, 0:384], ACT.Copy).then_inc(mix_hi, 1)
                if t >= 3:
                    norm_out(2 * NT + t - 3, psT[:, 1, 0:E], 1, 0, True)
                if 5 <= t < 5 + KE:
                    k = t - 5
                    act.wait_ge(loaded["w1a"], 16)
                    act.wait_ge(wo_done, NT)
                    s.activation(w1a[:, 0, k, :], w1a_f[:, k, :], ACT.Copy).then_inc(w_hi, 1)

            def head_attention(t):
                if 1 <= t <= NT:
                    act.wait_ge(sub_ready, t)
                    if t >= 3:
                        act.wait_ge(prod2b_ready, t - 2)
                    s.activation(e1[:, (t - 1) % 2, :], ssub, ACT.Exp, scale=SCALE1).then_inc(e1_ready, 1)

            for st_ in range(NSTEP):
                attention(st_)
                for t in expert_steps(st_):
                    experts0(t)
            for t in EXPERTS_LEFT:
                experts0(t)
            for t in range(1, NT + 1):
                head_attention(t)

            def router_exp(b):
                act.wait_ge(gabs, 2 * b + 1)
                bs = slice(NE * RB[b][0], NE * RB[b][1])
                s.activation(g_b[:, bs], g_a[:, bs], ACT.Exp, scale=-1.0).then_inc(gexp, 1)

            def router_ln(b):
                act.wait_ge(gabs, 2 * b + 2)
                bs = slice(NE * RB[b][0], NE * RB[b][1])
                s.activation(g_c[:, bs], g_a[:, bs], ACT.Ln).then_inc(gexp, 1)

            def hidden_high(t, c):
                m = 4 * t + c
                w = 4 if c < 3 else 1
                act.wait_ge(hc_T, m + 1)
                if t >= 2 and c == 0:
                    act.wait_ge(moe_ps, t - 1)
                rows_ = P if c < 3 else HID - 12 * P
                s.activation(hcT[0:rows_, t % 2, 0, c * 512:c * 512 + w * P],
                             psT[0:rows_, m % 2, 0:w * P], ACT.Copy).then_inc(hc_hi, 1)

            for t, j in TAIL:
                if j is None:
                    if t == 5:
                        router_ln(0)
                    if t < NP:
                        act.wait_ge(a_T, t + 1)
                        s.activation(aT[:, t, 0, :], psT[:, t % 2, :], ACT.Copy).then_inc(a_hi, 1)
                    if 3 <= t < NP + 3:
                        act.wait_ge(xn_T, 3 * NT + t - 2)
                        its = slice(2 * (t - 3) * P, 2 * (t - 2) * P)
                        for k in range(KE):
                            for dst in (hT[:, k, its], h_hl[:, 0, k, its]):
                                s.activation(dst, psM[:, 2 * k * P:2 * (k + 1) * P], ACT.Identity,
                                             bias=modcol[:, 1, 4 + k:5 + k], scale=modcol[:, 1, 6 + k:7 + k]) \
                                    .then_inc(hT_ready, 1)
                    if t == 4:
                        router_exp(0)
                    if t == NP + 3:
                        router_exp(1)
                else:
                    if t < NT:
                        p = NCH * t + j
                        w = 2 * INTER if j < NCH - 1 else INTER
                        act.wait_ge(chunk_ps, p + 1)
                        if p >= 2:
                            act.wait_ge(chunk_used, p - 1)
                        s.activation(th1[:, p % 2, 0:w], psS[:, 2 * (p % 2), 0:w], ACT.Tanh, scale=0.5) \
                            .then_inc(chunk_tanh, 1)
                    if j >= 1 and 1 <= t <= NT:
                        hidden_high(t - 1, j - 1)
                    if (t, j) == HALFWAY:
                        router_ln(1)

        @block.vector
        def _(dve):
            v = nc.vector
            n = [0]

            def link(ins):
                n[0] += 1
                ins.then_inc(ve_chain, 1)
                dve.wait_ge(ve_chain, n[0])

            def xn_of(q, mean, rs):
                if q >= 2:
                    dve.wait_ge(xn_T, q - 1)
                v.tensor_scalar(xn[:, q % 2, :], x[:, q % NT, :], mean, rs, ALU.subtract, ALU.mult) \
                    .then_inc(xn_ready, 1)

            dve.wait_ge(cond_tanh, 1)
            link(v.scalar_tensor_tensor(out=cth[:, :], in0=cth[:, :], scalar=1.0, in1=cs[:, :],
                                        op0=ALU.add, op1=ALU.mult))
            link(v.tensor_scalar(cth[:, :], cth[:, :], 0.5, None, ALU.mult))
            v.tensor_copy(csB[:, :, :], cth[:, :].unsqueeze(2).to_broadcast([P, 4, P])).then_inc(cond_rows, 1)

            for i in range(NT):
                dve.wait_ge(loaded["xa" if i < 4 else "xb"], 16)
                link(v.bn_stats(st[:, i % 2, :], x[:, i, :]))
                link(v.bn_aggr(mv[:, i, :], st[:, i % 2, :]))
            v.tensor_scalar(ve0[:, :], mv[:, :, 1], LN_EPS, None, ALU.add).then_inc(var_ready, 1)

            def modulation_rows(j):
                layer, third = MOD[j]
                dve.wait_ge(mod_ps, j + 1)
                if third == 0:
                    v.tensor_copy(modrow, psO[:, :]).then_inc(mod_rows, 1)
                else:
                    a = 256 if third == 1 else 0
                    gt = 256 - a
                    v.tensor_copy(modrow[:, 0:256], psO[:, a:a + 256]).then_inc(mod_rows, 1)
                    gdst = gates[:, layer, third - 1, :]
                    gps = psO[:, gt:gt + 256]
                    link(v.tensor_scalar(tmp[:, 0, 0:256], gps, 0.0, 2.0, ALU.is_ge, ALU.mult))
                    link(v.tensor_scalar(tmp[:, 0, 0:256], tmp[:, 0, 0:256], -1.0, None, ALU.add))
                    link(v.tensor_tensor(tmp[:, 0, 256:512], gps, tmp[:, 0, 0:256], ALU.mult))
                    link(v.scalar_tensor_tensor(out=gdst, in0=tmp[:, 0, 256:512], scalar=GATE_FLOOR,
                                                in1=tmp[:, 0, 0:256], op0=ALU.max, op1=ALU.mult))

            def modulation_columns(j):
                layer, third = MOD[j]
                dve.wait_ge(mod_T, j + 1)
                cols = psM[:, :].rearrange("p (b n) -> p b n", n=P)[:, :, 0]
                if third == 0:
                    link(v.tensor_copy(modcol[:, layer, 0:2], cols[:, 0:2]))
                    v.tensor_scalar(modcol[:, layer, 2:4], cols[:, 2:4], 1.0, None, ALU.add).then_inc(mod_done, 1)
                elif third == 1:
                    v.tensor_copy(modcol[:, layer, 4:6], cols[:, 0:2]).then_inc(mod_done, 1)
                else:
                    v.tensor_scalar(modcol[:, layer, 6:8], cols[:, 0:2], 1.0, None, ALU.add).then_inc(mod_done, 1)

            modulation_rows(0)
            modulation_columns(0)
            dve.wait_ge(rstd_ready, 1)
            dve.wait_ge(mod_T, 1)
            for i in range(NT):
                xn_of(i, mv[:, i, 0:1], rstd0[:, i:i + 1])
            dve.wait_ge(loaded["ident"], 16)
            link(v.tensor_copy(ident_b[:, :], ident[:, :]))
            dve.wait_ge(loaded["mask"], 16)
            v.tensor_copy(mask_b[:, :], mask_f[:, :]).then_inc(masks_ready, 1)
            dve.wait_ge(loaded["peT"], 16)
            dve.wait_ge(loaded["bk"], 16)
            dve.wait_ge(loaded["bvB"], 16)
            dve.wait_ge(mod_ps, 1)

            def v_low(m):
                kind, a, b = proj[m]
                if kind == "v":
                    dve.wait_ge(tmp_used, m + 1)
                    link(v.tensor_tensor(v_hl[:, 1, a, :], tmp[:, m % 2, :], v_hl[:, 0, a, :], ALU.subtract))

            for m in range(NKV):
                kind, a, b = proj[m]
                if m >= 1:
                    v_low(m - 1)
                dve.wait_ge(proj_done, m + 1)
                if m >= 2:
                    dve.wait_ge(tmp_used, m - 1)
                bank = psS[:, m % 4, :]
                if kind == "k":
                    v.scalar_tensor_tensor(out=tmp[:, m % 2, :], in0=bank, scalar=bk[:, a:a + 1],
                                           in1=peT[:, b * 512:(b + 1) * 512], op0=ALU.add, op1=ALU.add) \
                        .then_inc(tmp_ready, 1)
                else:
                    v.tensor_tensor(tmp[:, m % 2, :], bank, bvB[:, :], ALU.add).then_inc(tmp_ready, 1)
            v_low(NKV - 1)
            dve.wait_ge(loaded["amp"], 16)
            dve.wait_ge(loaded["escale"], 16)
            link(v.tensor_tensor(small[:, 36:52], small[:, 0:16], small[:, 0:16], ALU.mult))
            link(v.tensor_reduce(mixs[:, :], small[:, 36:52].rearrange("p (k c) -> p k c", c=2), AX.X, ALU.add))
            link(v.tensor_reduce(small[:, 17:18], mixs[:, :], AX.X, ALU.add))
            link(v.tensor_scalar(small[:, 17:18], small[:, 17:18], TOP_EPS, None, ALU.add))
            link(v.reciprocal(small[:, 18:19], small[:, 17:18]))
            link(v.tensor_scalar(mixs[:, :], mixs[:, :], small[:, 18:19], small[:, 16:17], ALU.mult, ALU.mult))
            link(v.tensor_scalar(mixs[:, :], mixs[:, :], 0.5, None, ALU.mult))
            dve.wait_ge(loaded["bq"], 16)
            for m in range(NKV, len(proj)):
                kind, h, nn = proj[m]
                dve.wait_ge(proj_done, m + 1)
                v.scalar_tensor_tensor(out=qT[:, 4 * nn:4 * nn + 4, h, :],
                                       in0=psS[:, m % 4, :].rearrange("p (t n) -> p t n", t=4),
                                       scalar=bq[:, h:h + 1],
                                       in1=peT[:, nn * 512:(nn + 1) * 512].rearrange("p (t n) -> p t n", t=4),
                                       op0=ALU.add, op1=ALU.add).then_inc(q_ready, 1)
                if m == MOD_AT[1]:
                    dve.wait_ge(tmp_used, NKV)
                if m - 1 in MOD_AT:
                    modulation_rows(MOD_AT.index(m - 1))
                if m - 3 in MOD_AT:
                    modulation_columns(MOD_AT.index(m - 3))
                if h % 8 == 7:
                    c = (m - NKV) // 8
                    dve.wait_ge(wo_hi, c + 1)
                    v.tensor_tensor(wo_hl[:, 1, 4 * c:4 * c + 4, :], wo_stage[:, c % 2, :, :],
                                    wo_hl[:, 0, 4 * c:4 * c + 4, :], ALU.subtract).then_inc(wo_lo, 1)

            def residual(q, ps, layer, which, ready, value, last=False, read=None):
                i = q % NT
                dve.wait_ge(ready, value)
                ins = v.tensor_tensor(tmp[:, q % 2, 0:E], ps, gates[:, layer, which, :], ALU.mult)
                if read is None:
                    link(ins)
                else:
                    ins.then_inc(read, 1)
                    dve.wait_ge(read, value)
                if last:
                    v.tensor_tensor(x[:, i, :], x[:, i, :], tmp[:, q % 2, 0:E], ALU.add).then_inc(x_out, 1)
                    return
                link(v.tensor_tensor(x[:, i, :], x[:, i, :], tmp[:, q % 2, 0:E], ALU.add))
                link(v.bn_stats(st[:, q % 2, :], x[:, i, :]))
                link(v.bn_aggr(mv2[:, q % 2, :], st[:, q % 2, :]))
                v.tensor_scalar(ve[:, q % 2:q % 2 + 1], mv2[:, q % 2, 1:2], LN_EPS, None, ALU.add) \
                    .then_inc(var_ready, 1)

            def xn_later(q):
                dve.wait_ge(rstd_ready, q - NT + 2)
                xn_of(q, mv2[:, q % 2, 0:1], rstd[:, q % 2:q % 2 + 1])

            def h_low(q):
                i = q % NT
                dve.wait_ge(hT_ready, 2 * NT + 4 * (q - NT + 1))
                v.tensor_tensor(h_hl[:, 1, :, i * P:(i + 1) * P], hT[:, :, i * P:(i + 1) * P],
                                h_hl[:, 0, :, i * P:(i + 1) * P], ALU.subtract).then_inc(hlo_ready, 1)

            def weights_low(n_):
                if n_ < 4:
                    m, k = n_ // 2, n_ % 2
                    dve.wait_ge(w_hi, n_ + 1)
                    v.tensor_tensor(wgu[:, 1, m, k, :], wgu_f[:, m, k, :], wgu[:, 0, m, k, :], ALU.subtract) \
                        .then_inc(w_lo, 1)
                elif n_ == 4:
                    dve.wait_ge(w_hi, 5)
                    v.tensor_tensor(wsh[:, 1, :, :], wsh_f, wsh[:, 0, :, :], ALU.subtract).then_inc(w_lo, 1)
                else:
                    dve.wait_ge(w_hi, 7)
                    v.tensor_tensor(wdn[:, 1, 0, :], wdn_f[:, 0, :], wdn[:, 0, 0, :], ALU.subtract).then_inc(w_lo, 1)
                    v.scalar_tensor_tensor(out=wdn[:, 1, 1:3, :], in0=wdn_f[:, 1:3, :], scalar=0.5,
                                           in1=wdn[:, 0, 1:3, :], op0=ALU.mult, op1=ALU.subtract).then_inc(w_lo, 1)

            nl = [0]
            mx8, neg, zsum, top4, den, rr = (small[:, 20:28], small[:, 28:29], small[:, 29:30],
                                             small[:, 34:35], small[:, 35:36], small[:, 19:20])
            idx = small[:, 52:60]

            def attention(st_):
                if 1 <= st_ <= NU:
                    u = st_ - 1
                    dve.wait_ge(exp_done, u + 1)
                    if u >= 4:
                        dve.wait_ge(normed, u - 3)
                    v.reciprocal(rinv[:, u % 4:u % 4 + 1], rowsum[:, u % 4:u % 4 + 1]).then_inc(rinv_ready, 1)
                G = (st_ - 11) // QPG
                if (st_ - 11) % QPG == 0 and 0 <= G < NGR:
                    dve.wait_ge(oT_hi, G + 1)
                    hs = slice((G % NG) * QPG, (G % NG + 1) * QPG)
                    v.tensor_tensor(oT[:, 1, hs, :], psO[:, :].rearrange("p (h n) -> p h n", h=QPG),
                                    oT[:, 0, hs, :], ALU.subtract).then_inc(oT_lo, 1)
                if st_ < NU:
                    u = st_
                    i, h = unit(u)
                    w = (i + 1) * P
                    dve.wait_ge(scores, u + 1)
                    v.tensor_reduce(negmax[:, u % 4:u % 4 + 1], psS[:, 2 * (u % 2):2 * (u % 2) + 2, :]
                                    .rearrange("p a n -> p (a n)")[:, 0:w], AX.X, ALU.max, negate=True) \
                        .then_inc(negmax_ready, 1)
                if LAG <= st_ < NU + LAG:
                    u = st_ - LAG
                    i, h = unit(u)
                    G = u // QPG
                    for c, k in chunks(i):
                        dve.wait_ge(pT_hi, nl[0] + 1)
                        dst = pT[:, G % 2, :, c:c + k, h % QPG, :]
                        v.tensor_tensor(dst[:, 1], psT[:, nl[0] % 2, 0:k * P].rearrange("p (k n) -> p k n", k=k),
                                        dst[:, 0], ALU.subtract).then_inc(pT_lo, 1)
                        nl[0] += 1
                if (i := at(st_, 26)) is not None:
                    xn_later(NT + i)
                if (i := at(st_, 25)) is not None:
                    residual(NT + i, psM[:, 0:E], 0, 0, wo_done, i + 1)
                if (i := at(st_, 28)) is not None:
                    h_low(NT + i)
                if st_ in WSPLIT:
                    weights_low(WSPLIT.index(st_))
                if (i := at(st_, 30)) is not None:
                    if i == 0:
                        dve.wait_ge(loaded["iota"], 16)
                    dve.wait_ge(logit_ps, i + 1)
                    link(v.tensor_copy(logit, psM[:, 0:P]))
                    link(v.max(mx8, logit))
                    v.tensor_scalar(neg, mx8[:, 0:1], -1.0, None, ALU.mult).then_inc(neg_ready, 1)
                    link(v.max_index(small[:, 36:44].bitcast(U32), mx8, logit))
                    link(v.tensor_copy(idx, small[:, 36:44].bitcast(U32)))
                if (i := at(st_, 31)) is not None:
                    link(v.tensor_scalar(onehot, iota, idx[:, 0:1], None, ALU.is_equal))
                    for k in range(1, 4):
                        link(v.scalar_tensor_tensor(out=onehot, in0=iota, scalar=idx[:, k:k + 1], in1=onehot,
                                                    op0=ALU.is_equal, op1=ALU.add))
                if (i := at(st_, 32)) is not None:
                    dve.wait_ge(e_ready, 2 * i + 2)
                    link(v.tensor_scalar(den, zsum, TOP_EPS, top4, ALU.mult, ALU.add))
                    link(v.reciprocal(rr, den))
                    v.scalar_tensor_tensor(out=coeff, in0=eexp, scalar=rr, in1=onehot, op0=ALU.mult, op1=ALU.mult) \
                        .then_inc(coeff_ready, 1)
                if (i := at(st_, 35)) is not None:
                    dve.wait_ge(c_ps, i + 1)
                    v.tensor_copy(c_tok[:, i, :], psM[:, 2 * P:2 * P + NB]).then_inc(c_ready, 1)

            def experts0(t):
                b = t % 2
                for j in range(5):
                    if t < NT:
                        p = 5 * t + j
                        up = psS[:, p % 4, 256:512]
                        dve.wait_ge(tanh_ready, p + 1)
                        link(v.scalar_tensor_tensor(out=act0[:, p % 4, :], in0=th0[:, p % 4, :], scalar=1.0,
                                                    in1=psS[:, p % 4, 0:256], op0=ALU.add, op1=ALU.mult))
                        if j == 0:
                            dve.wait_ge(c_ready, t + 1)
                            if t >= 2:
                                dve.wait_ge(basis_sum, t - 1)
                        if j < 4:
                            for kk in (2 * j, 2 * j + 1):
                                k = slice(kk % 2 * P, (kk % 2 + 1) * P)
                                ins = v.scalar_tensor_tensor(
                                    out=basis[:, b, kk, :], in0=act0[:, p % 4, k], scalar=c_tok[:, t, kk:kk + 1],
                                    in1=up[:, k], op0=ALU.mult, op1=ALU.mult)
                        else:
                            if t >= 2:
                                dve.wait_ge(mix_T, t - 1)
                            ins = v.tensor_tensor(mcat[:, b, P:3 * P], act0[:, p % 4, :], up, ALU.mult)
                        ins.then_inc(pair_used, 1)
                    if j == 1 and t >= 3:
                        xn_later(2 * NT + t - 3)
                if 1 <= t <= NT:
                    dve.wait_ge(mix_hi, t)
                    v.tensor_tensor(mcT[:, 1 - b, 1, :], psT[:, 0, 0:384], mcT[:, 1 - b, 0, :], ALU.subtract) \
                        .then_inc(mix_lo, 1)
                if 2 <= t < NT + 2:
                    residual(2 * NT + t - 2, psO[:, 0:E], 0, 1, down_ps, t - 1, read=down_read)
                if 5 <= t < 5 + KE:
                    k = t - 5
                    dve.wait_ge(w_hi, 8 + k)
                    v.tensor_tensor(w1a[:, 1, k, :], w1a_f[:, k, :], w1a[:, 0, k, :], ALU.subtract).then_inc(w_lo, 1)

            def score_products(t):
                b = t % 2
                if t == 0:
                    dve.wait_ge(loaded["b1a"], 16)
                    dve.wait_ge(loaded["rope"], 32)
                dve.wait_ge(qkv_ps, t + 1)
                if t >= 3:
                    dve.wait_ge(prod2b_ready, t - 2)
                v.tensor_tensor(vb[:, t % 3, :], psS[:, 2 + b, 0:E], b1a[:, 2 * E:3 * E], ALU.add).then_inc(ve_chain, 1)
                n[0] += 1
                v.tensor_tensor(qkb[:, b, :], psS[:, b, :], b1a[:, 0:2 * E], ALU.add).then_inc(qkv_read, 1)
                dve.wait_ge(qkv_read, t + 1)
                heads = 2 * H1
                q4 = qkb[:, b, :].rearrange("p (h d c) -> p h d c", h=heads, c=2)
                b4 = ropeB.rearrange("p (h d c) -> p h d c", h=heads, c=2)
                cos = ropeC[:, t, :].unsqueeze(1).to_broadcast([P, heads, D1])
                sin = ropeS[:, t, :].rearrange("p (d c) -> p d c", c=2)
                for c in range(2):
                    v.tensor_tensor(b4[:, :, :, c], q4[:, :, :, 1 - c],
                                    sin[:, :, c].unsqueeze(1).to_broadcast([P, heads, D1 // 2]), ALU.mult) \
                        .then_inc(ve_chain, 1)
                    n[0] += 1
                link(v.tensor_tensor(ropeA.rearrange("p (h d) -> p h d", h=heads),
                                     qkb[:, b, :].rearrange("p (h d) -> p h d", h=heads), cos, ALU.mult))
                link(v.tensor_tensor(qkr[:, b, :], ropeA, ropeB, ALU.add))
                if t >= 2:
                    dve.wait_ge(s_sum, t - 1)
                v.tensor_tensor(prod1[:, b, :].rearrange("p (d h t) -> p d h t", d=D1, h=H1),
                                qkr[:, b, 0:E].rearrange("p (h d) -> p d h", h=H1).unsqueeze(3)
                                .to_broadcast([P, D1, H1, H1]),
                                qkr[:, b, E:2 * E].rearrange("p (t d) -> p d t", t=H1).unsqueeze(2)
                                .to_broadcast([P, D1, H1, H1]), ALU.mult).then_inc(prod1_ready, 1)

            def softmax_in(t):
                dve.wait_ge(s_sum, t + 1)
                ps = psT[:, t % 2, 0:256].rearrange("p (h t) -> p h t", h=H1)
                link(v.tensor_reduce(m1[:, t % 2, :], ps, AX.X, ALU.max))
                if t >= 1:
                    dve.wait_ge(e1_ready, t)
                v.tensor_tensor(ssub.rearrange("p (h t) -> p h t", h=H1), ps,
                                m1[:, t % 2, :].unsqueeze(2).to_broadcast([P, H1, H1]), ALU.subtract) \
                    .then_inc(sub_ready, 1)

            def weigh_last_heads(t):
                b = t % 2
                dve.wait_ge(e1_ready, t + 1)
                eb = e1[:, b, :].rearrange("p (h t) -> p h t", h=H1)
                part2 = prod2[b][:, VALS:H1 * E].rearrange("p (h d t) -> p h d t", h=H1 - HPE, d=D1)
                link(v.tensor_reduce(r1[:, b, :], eb, AX.X, ALU.add))
                link(v.reciprocal(r1[:, b, :], r1[:, b, :]))
                hd = heads_dve(t)
                link(v.tensor_tensor(part2[:, H1 - HPE - hd:, :, :],
                                     eb[:, H1 - hd:, :].unsqueeze(2).to_broadcast([P, hd, D1, H1]),
                                     vb[:, t % 3, :].rearrange("p (t d) -> p d t", t=H1).unsqueeze(1)
                                     .to_broadcast([P, hd, D1, H1]), ALU.mult))

            def sum_last_heads(t):
                part2 = prod2[t % 2][:, VALS:H1 * E].rearrange("p (h d t) -> p h d t", h=H1 - HPE, d=D1)
                dve.wait_ge(prod2b_ready, min(t + 1, NT - 1))
                if t >= 1:
                    dve.wait_ge(av_ready, 2 * t)
                v.tensor_reduce(avr, part2.rearrange("p h d t -> p (h d) t"), AX.X, ALU.add).then_inc(prod2_used, 1)

            def heads_out(t):
                b = t % 2
                if t >= 2:
                    dve.wait_ge(shuffled[t - 2], 16)
                out4 = av[:, b, :].rearrange("p (h d) -> p h d", h=H1)
                rb = r1[:, b, :].unsqueeze(2).to_broadcast([P, H1, D1])
                dve.wait_ge(prod2_used, t + 1)
                v.tensor_tensor(out4[:, HPE:, :], avr.rearrange("p (h d) -> p h d", h=H1 - HPE), rb[:, HPE:, :],
                                ALU.mult).then_inc(av_ready, 1)
                dve.wait_ge(av_ps, t + 1)
                v.tensor_tensor(out4[:, 0:HPE, :], (psO if b == 0 else psM)[:, 0:HPE * D1]
                                .rearrange("p (h d) -> p h d", h=HPE), rb[:, 0:HPE, :], ALU.mult).then_inc(av_ready, 1)

            def head_attention(t):
                if t >= 3:
                    sum_last_heads(t - 3)
                if 2 <= t < NT + 2:
                    weigh_last_heads(t - 2)
                if t < NT:
                    score_products(t)
                if 1 <= t <= NT:
                    softmax_in(t - 1)
                if t >= 3:
                    heads_out(t - 3)

            for st_ in range(NSTEP):
                attention(st_)
                for t in expert_steps(st_):
                    experts0(t)
            for t in EXPERTS_LEFT:
                if t == NT:
                    head_attention(0)
                experts0(t)
            for t in range(1, NT + 3):
                head_attention(t)

            def tiles(a, t0, t1):
                return a[:, NE * t0:NE * t1].rearrange("p (t e) -> p t e", e=NE)

            def router_abs(b):
                bs = slice(NE * RB[b][0], NE * RB[b][1])
                dve.wait_ge(gate_ps, RB[b][1] // 2)
                if b == 0:
                    dve.wait_ge(loaded["gw"], 48)
                link(v.tensor_copy(g_s[:, bs], psT[:, 1, bs]))
                v.scalar_tensor_tensor(out=g_a[:, bs], in0=g_s[:, bs], scalar=-1.0, in1=g_s[:, bs],
                                       op0=ALU.mult, op1=ALU.max).then_inc(gabs, 1)

            def router_one(b):
                bs = slice(NE * RB[b][0], NE * RB[b][1])
                dve.wait_ge(gexp, 2 * b + 1)
                v.tensor_scalar(g_a[:, bs], g_b[:, bs], 1.0, None, ALU.add).then_inc(gabs, 1)

            def router_softplus(b):
                bs = slice(NE * RB[b][0], NE * RB[b][1])
                ga, gb_, gc, gm, gx, gi = (a[:, bs] for a in (g_a, g_b, g_c, g_m, g_x, g_i))
                dve.wait_ge(gabs, 2 * b + 2)
                link(v.tensor_scalar(gm, ga, -1.0, None, ALU.add))
                link(v.tensor_scalar(gx, gm, 0.0, None, ALU.is_equal))
                link(v.tensor_tensor(gm, gm, gx, ALU.add))
                link(v.reciprocal(gi, gm))
                dve.wait_ge(gexp, 2 * b + 2)
                link(v.tensor_tensor(gc, gc, gx, ALU.add))
                link(v.tensor_tensor(gc, gc, gb_, ALU.mult))
                link(v.tensor_tensor(gc, gc, gi, ALU.mult))
                v.scalar_tensor_tensor(out=gc, in0=g_s[:, bs], scalar=0.0, in1=gc, op0=ALU.max, op1=ALU.add) \
                    .then_inc(sp_ready, 1)

            def router_top2(n_):
                t0, t1 = TB[n_]
                bs = slice(NE * t0, NE * t1)
                dve.wait_ge(sq_ready, n_ + 1)
                link(v.tensor_tensor(tiles(g_x, t0, t1), tiles(g_r, t0, t1),
                                     gbB.unsqueeze(1).to_broadcast([P, t1 - t0, NE]), ALU.add))
                for t in range(t0, t1):
                    e8 = slice(t * NE, (t + 1) * NE)
                    v.max(g_m[:, e8], g_x[:, e8]).then_inc(ve_chain, 1)
                    n[0] += 1
                dve.wait_ge(ve_chain, n[0])
                for t in range(t0, t1):
                    e8 = slice(t * NE, (t + 1) * NE)
                    v.max_index(g_u[:, e8], g_m[:, e8], g_x[:, e8]).then_inc(ve_chain, 1)
                    n[0] += 1
                dve.wait_ge(ve_chain, n[0])
                link(v.tensor_copy(g_i[:, bs], g_u[:, bs]))
                for k, dst in enumerate((g_a, g_b)):
                    link(v.tensor_tensor(tiles(dst, t0, t1), iota1.unsqueeze(1).to_broadcast([P, t1 - t0, NE]),
                                         tiles(g_i, t0, t1)[:, :, k:k + 1].to_broadcast([P, t1 - t0, NE]),
                                         ALU.is_equal))
                link(v.tensor_tensor(g_a[:, bs], g_a[:, bs], g_b[:, bs], ALU.add))
                link(v.scalar_tensor_tensor(out=cw[:, t0:t1, :], in0=tiles(g_r, t0, t1), scalar=0.5,
                                            in1=tiles(g_a, t0, t1), op0=ALU.mult, op1=ALU.mult))

            def projection_step(t):
                if 3 <= t < NP + 3:
                    i = 2 * (t - 3)
                    dve.wait_ge(rstd_ready, 2 * NT + t - 1)
                    dve.wait_ge(xn_T, 3 * NT + t - 3)
                    v.tensor_scalar(xn[:, 0, :], x[:, i, :], mv2[:, 0, 0:1], rstd[:, 0:1], ALU.subtract, ALU.mult)
                    v.tensor_scalar(xn[:, 1, :], x[:, i + 1, :], mv2[:, 1, 0:1], rstd[:, 1:2], ALU.subtract,
                                    ALU.mult).then_inc(xn_ready, 1)
                if t < NP:
                    dve.wait_ge(a_hi, t + 1)
                    v.tensor_tensor(aT[:, t, 1, :], psT[:, t % 2, :], aT[:, t, 0, :], ALU.subtract).then_inc(a_lo, 1)
                if t == 5:
                    router_one(0)
                if 2 <= t < NP + 2:
                    i = 2 * (t - 2)
                    gate = gates[:, 1, 0, :].unsqueeze(1).to_broadcast([P, 2, E])
                    two = tmp[:, 0, :].rearrange("p (t n) -> p t n", t=2)
                    dve.wait_ge(o_ps, t - 1)
                    v.tensor_tensor(two, psO[:, :].rearrange("p (t n) -> p t n", t=2), gate, ALU.mult) \
                        .then_inc(o_read, 1)
                    dve.wait_ge(o_read, t - 1)
                    link(v.tensor_tensor(x[:, i:i + 2, :], x[:, i:i + 2, :], two, ALU.add))
                    for m in range(2):
                        v.bn_stats(st[:, m, :], x[:, i + m, :]).then_inc(ve_chain, 1)
                        n[0] += 1
                    dve.wait_ge(ve_chain, n[0])
                    for m in range(2):
                        v.bn_aggr(mv2[:, m, :], st[:, m, :]).then_inc(ve_chain, 1)
                        n[0] += 1
                    dve.wait_ge(ve_chain, n[0])
                    v.tensor_scalar(ve[:, :], mv2[:, :, 1], LN_EPS, None, ALU.add).then_inc(var_ready, 1)
                if t == 4:
                    router_abs(0)
                if t == 5:
                    router_softplus(0)
                if t == NP + 3:
                    router_abs(1)
                    router_one(1)

            def expert_step(t, j):
                b = t % 2
                if t < NT:
                    p = NCH * t + j
                    w = 2 * INTER if j < NCH - 1 else INTER
                    dve.wait_ge(chunk_tanh, p + 1)
                    link(v.scalar_tensor_tensor(out=a1[:, p % 2, 0:w], in0=th1[:, p % 2, 0:w], scalar=1.0,
                                                in1=psS[:, 2 * (p % 2), 0:w], op0=ALU.add, op1=ALU.mult))
                    if j == 0 and t in [t0 for t0, _ in TB]:
                        router_top2([t0 for t0, _ in TB].index(t))
                    if t >= 2 and j == 0:
                        dve.wait_ge(hc_T, 4 * (t - 1))
                    for m in range(w // INTER):
                        e = 2 * j + m
                        lo = m * INTER
                        ins = v.scalar_tensor_tensor(
                            out=hc[:, b, e * INTER:(e + 1) * INTER], in0=a1[:, p % 2, lo:lo + INTER],
                            scalar=cw[:, t, e:e + 1] if e < NE else 0.5,
                            in1=psS[:, 2 * (p % 2) + 1, lo:lo + INTER], op0=ALU.mult, op1=ALU.mult)
                    ins.then_inc(chunk_used, 1)
                if j == 0 and t >= 3:
                    residual(t - 3, (psO if t % 2 == 1 else psM)[:, 0:E], 1, 1, moe_ps, t - 2, last=True)
                if j >= 1 and 1 <= t <= NT:
                    c = j - 1
                    m = 4 * (t - 1) + c
                    w = 4 if c < 3 else 1
                    rows_ = P if c < 3 else HID - 12 * P
                    dve.wait_ge(hc_hi, m + 1)
                    o = c * 512
                    v.tensor_tensor(hcT[0:rows_, 1 - b, 1, o:o + w * P], psT[0:rows_, m % 2, 0:w * P],
                                    hcT[0:rows_, 1 - b, 0, o:o + w * P], ALU.subtract).then_inc(hc_lo, 1)
                if (t, j) == HALFWAY:
                    router_softplus(1)
                if (t, j) == (NT + 1, NCH - 1):
                    residual(NT - 1, (psO if NT % 2 == 1 else psM)[:, 0:E], 1, 1, moe_ps, NT, last=True)

            link(v.tensor_tensor(gbo, b1a[:, 3 * E:4 * E], gates[:, 1, 0, :], ALU.mult))
            link(v.tensor_tensor(x[:, :, :], x[:, :, :], gbo.unsqueeze(1).to_broadcast([P, NT, E]), ALU.add))
            for t, j in TAIL:
                if j is None:
                    projection_step(t)
                else:
                    expert_step(t, j)

        @block.tensor
        def _(pe):
            te = nc.tensor

            def mm(out_, lhsT, rhs, start, stop):
                return te.matmul(out_, lhsT=lhsT, rhs=rhs, start=start, stop=stop)

            def three(out_, a_hi_, a_lo_, b_hi_, b_lo_, first, last):
                mm(out_, a_hi_, b_hi_, first, False)
                mm(out_, a_hi_, b_lo_, False, False)
                return mm(out_, a_lo_, b_hi_, False, last)

            def modulation_rows(j):
                layer, third = MOD[j]
                if j:
                    pe.wait_ge(mod_done, j)
                for k in range(KE):
                    ins = mm(psO[:, :], csB[:, 2 * layer + k, :], wmod[:, layer, k, third * 512:third * 512 + 512],
                             k == 0, k == KE - 1)
                ins.then_inc(mod_ps, 1)

            def modulation_columns(j):
                layer, third = MOD[j]
                pe.wait_ge(mod_rows, j + 1)
                for b in range(4 if third == 0 else 2):
                    ins = te.transpose(psM[:, b * P:(b + 1) * P], modrow[:, b * P:(b + 1) * P], ident[:, :])
                ins.then_inc(mod_T, 1)

            def norm_T(q, ps):
                pe.wait_ge(xn_ready, q + 1)
                for k in range(KE):
                    ins = te.transpose(ps[:, k * P:(k + 1) * P], xn[:, q % 2, k * P:(k + 1) * P], ident[:, :])
                ins.then_inc(xn_T, 1)

            def h_out(q):
                return 2 * NT + 4 * (q - NT + 1)

            pe.wait_ge(cond_rows, 1)
            pe.wait_ge(loaded["wmod0a"], 16)
            pe.wait_ge(loaded["ident"], 16)
            modulation_rows(0)
            modulation_columns(0)
            for i in range(NT):
                if i >= 2:
                    pe.wait_ge(hT_ready, 2 * (i - 1))
                norm_T(i, psT[:, i % 2, :])
            pe.wait_ge(loaded["wkv"], 16)
            for m in range(len(proj)):
                kind, a, b = proj[m]
                if m == NKV:
                    pe.wait_ge(loaded["wq"], 16)
                if m >= 4:
                    if m - 4 < NKV:
                        pe.wait_ge(tmp_ready, m - 3)
                    else:
                        pe.wait_ge(q_ready, m - 3 - NKV)
                if kind == "k":
                    pe.wait_ge(hT_ready, 2 * 4 * (b + 1))
                if kind == "v":
                    pe.wait_ge(hT_ready, 2 * (a + 1))
                for k in range(KE):
                    if kind == "k":
                        lhsT, rhs = wkv[:, k, 2 * a * P:(2 * a + 1) * P], hT[:, k, b * 512:(b + 1) * 512]
                    elif kind == "v":
                        lhsT = hT[:, k, a * P:(a + 1) * P]
                        rhs = wkv[:, k, :].rearrange("p (g c n) -> p g c n", g=NG, c=2)[:, :, 1, :]
                    else:
                        lhsT, rhs = wq[:, k, a * P:(a + 1) * P], hT[:, k, b * 512:(b + 1) * 512]
                    ins = mm(psS[:, m % 4, :], lhsT, rhs, k == 0, k == KE - 1)
                ins.then_inc(proj_done, 1)
                if m in MOD_AT:
                    j = MOD_AT.index(m)
                    pe.wait_ge(loaded["wmod0b"] if MOD[j][0] == 0 else loaded["wmod1"], 16)
                    modulation_rows(j)
                if m - 2 in MOD_AT:
                    modulation_columns(MOD_AT.index(m - 2))

            pe.wait_ge(q_ready, 2 * HQ)
            pe.wait_ge(masks_ready, 1)
            pe.wait_ge(mod_done, 6)
            nt = [0]
            def attention(st_):
                if st_ < NU:
                    u = st_
                    i, h = unit(u)
                    if u < NKV:
                        pe.wait_ge(tmp_used, NKV)
                    if u >= 2:
                        pe.wait_ge(exp_done, u - 1)
                    w = (i + 1) * P
                    for c in range(0, w, 512):
                        cw_ = min(512, w - c)
                        bank = psS[:, 2 * (u % 2) + c // 512, :]
                        diag = c + cw_ == w
                        ins = mm(bank[:, 0:cw_], qT[:, i, h, :], kT[:, h // QPG, c:c + cw_], True, not diag)
                        if diag:
                            ins = mm(bank[:, cw_ - P:cw_], ident_b[:, :], mask_b[:, :], False, True)
                    ins.then_inc(scores, 1)
                if LAG <= st_ < NU + LAG:
                    u = st_ - LAG
                    i, h = unit(u)
                    pe.wait_ge(normed, u + 1)
                    for c, k in chunks(i):
                        if nt[0] >= 2:
                            pe.wait_ge(pT_lo, nt[0] - 1)
                        for b in range(k):
                            ins = te.transpose(psT[:, nt[0] % 2, b * P:(b + 1) * P],
                                               probs[:, u % 4, (c + b) * P:(c + b + 1) * P], ident[:, :])
                        ins.then_inc(pT_ps, 1)
                        nt[0] += 1
                G, part = (st_ - 7) // QPG, (st_ - 7) % QPG
                if 0 <= G < NGR:
                    i, g_ = G // NG, G % NG
                    if part == 0:
                        pe.wait_ge(pT_lo, chunk_end[QPG * G + QPG - 1])
                        if G >= 1:
                            pe.wait_ge(oT_lo, G)
                    vs = slice(g_ * P, (g_ + 1) * P)
                    products = [(j, *vp) for j in range(i + 1) for vp in ((0, 0), (0, 1), (1, 0))]
                    n_ = len(products)
                    for m in range(part * n_ // QPG, (part + 1) * n_ // QPG):
                        j, wv, wp = products[m]
                        ins = mm(psO[:, :], v_hl[:, wv, j, vs],
                                 pT[:, G % 2, wp, j, :, :].rearrange("p h n -> p (h n)"), m == 0, m == n_ - 1)
                    if part == QPG - 1:
                        ins.then_inc(pv, 1)
                i, part = (st_ - 21) // HQ, (st_ - 21) % HQ
                if 0 <= i < NT and part < NG:
                    pe.wait_ge(oT_lo, NG * i + part + 1)
                    if part == 0:
                        if i == 0:
                            pe.wait_ge(wo_lo, 4)
                        else:
                            pe.wait_ge(c_ready, i)
                    for h in range(part * QPG, (part + 1) * QPG):
                        ins = three(psM[:, 0:E], oT[:, 0, h, :], oT[:, 1, h, :], wo_hl[:, 0, h, :], wo_hl[:, 1, h, :],
                                    h == 0, h == HQ - 1)
                    if part == NG - 1:
                        ins.then_inc(wo_done, 1)
                if (i := at(st_, 27)) is not None:
                    norm_T(NT + i, psM[:, 256:512])
                if (i := at(st_, 29)) is not None:
                    if i == 0:
                        pe.wait_ge(loaded["wr"], 16)
                    pe.wait_ge(hT_ready, h_out(NT + i))
                    for k in range(KE):
                        ins = mm(psM[:, 0:P], hT[:, k, i * P:(i + 1) * P], wr[:, k, :], k == 0, k == KE - 1)
                    ins.then_inc(logit_ps, 1)
                if (i := at(st_, 33)) is not None:
                    pe.wait_ge(coeff_ready, i + 1)
                    te.transpose(psM[:, P:2 * P], coeff, ident[:, :]).then_inc(coT_ps, 1)
                if (i := at(st_, 34)) is not None:
                    pe.wait_ge(coT_ready, i + 1)
                    mm(psM[:, 2 * P:2 * P + NB], coeffT, mixs[:, :], True, True).then_inc(c_ps, 1)

            def experts0(t):
                if t == 0:
                    pe.wait_ge(w_lo, 7)
                for j in range(5):
                    if t < NT:
                        pe.wait_ge(hlo_ready, t + 1)
                        ts_ = slice(t * P, (t + 1) * P)
                        p = 5 * t + j
                        if p >= 4:
                            pe.wait_ge(pair_used, p - 3)
                        for m in range(2):
                            for k in range(KE):
                                if j < 4:
                                    wh, wl = (wgu[:, w_, m, k, j * 256:(j + 1) * 256] for w_ in range(2))
                                else:
                                    wh, wl = (wsh[:, w_, k, m * 256:(m + 1) * 256] for w_ in range(2))
                                ins = three(psS[:, p % 4, m * 256:(m + 1) * 256], h_hl[:, 0, k, ts_], h_hl[:, 1, k, ts_],
                                            wh, wl, k == 0, k == KE - 1)
                        ins.then_inc(pair_ps, 1)
                    if j == 1 and 2 <= t < NT + 2:
                        pe.wait_ge(mix_lo, t - 1)
                        if t == 2:
                            pe.wait_ge(oT_lo, NGR)
                        else:
                            pe.wait_ge(down_read, t - 2)
                        for c in range(3):
                            cs_ = slice(c * P, (c + 1) * P)
                            ins = three(psO[:, 0:E], mcT[:, t % 2, 0, cs_], mcT[:, t % 2, 1, cs_], wdn[:, 0, c, :],
                                        wdn[:, 1, c, :], c == 0, c == 2)
                        ins.then_inc(down_ps, 1)
                    if j == 1 and 1 <= t <= NT:
                        pe.wait_ge(basis_sum, t)
                        pe.wait_ge(pair_used, 5 * t)
                        if t >= 2:
                            pe.wait_ge(mix_lo, t - 1)
                        for c in range(3):
                            ins = te.transpose(psT[:, 0, c * P:(c + 1) * P], mcat[:, (t - 1) % 2, c * P:(c + 1) * P],
                                               ident[:, :])
                        ins.then_inc(mix_T, 1)
                    if j == 3 and t >= 3 and t != NT + 1:
                        for q in range(2 * NT + t - 3 - (t == NT + 2), 2 * NT + t - 2):
                            if q > 2 * NT:
                                pe.wait_ge(hT_ready, h_out(q - 1))
                            norm_T(q, psT[:, 1, 0:E])
            def qkv(t):
                if t == 0:
                    pe.wait_ge(w_lo, 7 + KE)
                    pe.wait_ge(pair_used, 5 * NT)
                pe.wait_ge(hlo1_ready, t + 1)
                if t >= 2:
                    pe.wait_ge(qkv_read, t - 1)
                ts_ = slice(t * P, (t + 1) * P)
                for bank, c0, c1 in ((t % 2, 0, 2 * E), (2 + t % 2, 2 * E, 3 * E)):
                    for k in range(KE):
                        ins = three(psS[:, bank, 0:c1 - c0], h_hl[:, 0, k, ts_], h_hl[:, 1, k, ts_],
                                    w1a[:, 0, k, c0:c1], w1a[:, 1, k, c0:c1], k == 0, k == KE - 1)
                ins.then_inc(qkv_ps, 1)

            def identity_sum(ps, src, width):
                for k in range(H1):
                    ins = mm(ps, ident[:, :], src[:, k * width:(k + 1) * width], k == 0, k == H1 - 1)
                return ins

            def head_attention(t):
                if t < NT:
                    pe.wait_ge(prod1_ready, t + 1)
                    if t == 0:
                        pe.wait_ge(mix_lo, NT)
                    if t == 1:
                        pe.wait_ge(hT_ready, h_out(3 * NT - 1))
                    if t >= 2:
                        pe.wait_ge(sub_ready, t - 1)
                    identity_sum(psT[:, t % 2, 0:H1 * H1], prod1[:, t % 2, :], H1 * H1).then_inc(s_sum, 1)
                if t + 2 < NT:
                    qkv(t + 2)
                if t >= 2:
                    i = t - 2
                    pe.wait_ge(prod2_ready, i + 1)
                    if i == 0:
                        pe.wait_ge(c_ready, NT)
                        pe.wait_ge(hT_ready, h_out(3 * NT - 1))
                    if i >= 2:
                        pe.wait_ge(av_ready, 2 * (i - 1))
                    identity_sum((psO if i % 2 == 0 else psM)[:, 0:HPE * D1], prod2[i % 2][:, 0:VALS], HPE * D1) \
                        .then_inc(av_ps, 1)

            for st_ in range(NSTEP):
                attention(st_)
                for t in expert_steps(st_):
                    experts0(t)
            for t in EXPERTS_LEFT:
                if t == NT:
                    qkv(0)
                    qkv(1)
                experts0(t)
                if t == NT + 1:
                    head_attention(0)
            for t in range(1, NT + 2):
                head_attention(t)

            def projection_step(t):
                if t < NP:
                    if t % 2 == 0:
                        pe.wait_ge(loaded["mixed"][t // 2], 16)
                    if t >= 2:
                        pe.wait_ge(a_lo, t - 1)
                    for k in range(2 * KE):
                        ins = te.transpose(psT[:, t % 2, k * P:(k + 1) * P],
                                           mixed_rows[:, 2 * t + k // KE, (k % KE) * P:(k % KE + 1) * P], ident[:, :])
                    ins.then_inc(a_T, 1)
                if 1 <= t <= NP:
                    pe.wait_ge(a_lo, t)
                    if t >= 2:
                        pe.wait_ge(o_read, t - 1)
                    for m in range(2):
                        for k in range(KE):
                            ks = slice((m * KE + k) * P, (m * KE + k + 1) * P)
                            ins = three(psO[:, m * E:(m + 1) * E], aT[:, t - 1, 0, ks], aT[:, t - 1, 1, ks],
                                        w1a[:, 0, k, 3 * E:4 * E], w1a[:, 1, k, 3 * E:4 * E], k == 0, k == KE - 1)
                    ins.then_inc(o_ps, 1)
                if 4 <= t < NP + 4:
                    pe.wait_ge(hT_ready, 10 * NT + 4 * (t - 3))
                    if t == 4:
                        pe.wait_ge(a_lo, NP)
                    for i in (2 * t - 8, 2 * t - 7):
                        for k in range(KE):
                            ins = mm(psT[:, 1, i * NE:(i + 1) * NE], hT[:, k, i * P:(i + 1) * P], gwf[:, k, :],
                                     k == 0, k == KE - 1)
                    ins.then_inc(gate_ps, 1)
                    if t == 4:
                        pe.wait_ge(gabs, 1)
                if 3 <= t < NP + 3:
                    pe.wait_ge(xn_ready, 3 * NT + t - 2)
                    for k in range(KE):
                        for m in range(2):
                            ins = te.transpose(psM[:, (2 * k + m) * P:(2 * k + m + 1) * P],
                                               xn[:, m, k * P:(k + 1) * P], ident[:, :])
                    ins.then_inc(xn_T, 1)

            def expert_step(t, j):
                if t < NT:
                    if (t, j) == (0, 0):
                        for n_, m in (("w1", 16), ("w3", 16), ("w2", 32)):
                            pe.wait_ge(loaded[n_], m)
                    pe.wait_ge(hlo1_ready, NT + t // 2 + 1)
                    ts_ = slice(t * P, (t + 1) * P)
                    p = NCH * t + j
                    w = 2 * INTER if j < NCH - 1 else INTER
                    if p >= 2:
                        pe.wait_ge(chunk_used, p - 1)
                    for m, wt in enumerate((w1b, w3b)):
                        for k in range(KE):
                            wcol = wt[:, k, 2 * INTER * j:2 * INTER * j + w]
                            mm(psS[:, 2 * (p % 2) + m, 0:w], h_hl[:, 0, k, ts_], wcol, k == 0, False)
                            ins = mm(psS[:, 2 * (p % 2) + m, 0:w], h_hl[:, 1, k, ts_], wcol, False, k == KE - 1)
                    ins.then_inc(chunk_ps, 1)
                if t >= 2:
                    i = t - 2
                    if j == 0:
                        pe.wait_ge(hc_lo, 4 * (i + 1))
                        if i < 2:
                            pe.wait_ge(o_read, NP)
                        else:
                            pe.wait_ge(x_out, i - 1)
                    for e in range(KH * j // NCH, KH * (j + 1) // NCH):
                        w = min(P, HID - e * P)
                        for w_ in range(2):
                            ins = mm((psO if i % 2 == 0 else psM)[:, 0:E], hcT[0:w, i % 2, w_, e * P:(e + 1) * P],
                                     w2b[0:w, e, :], e == 0 and w_ == 0, e == KH - 1 and w_ == 1)
                    if j == NCH - 1:
                        ins.then_inc(moe_ps, 1)
                if j >= 1 and 1 <= t <= NT:
                    i, c = t - 1, j - 1
                    m = 4 * i + c
                    pe.wait_ge(chunk_used, NCH * t)
                    if m == 0:
                        pe.wait_ge(gabs, 3)
                    if m >= 2:
                        pe.wait_ge(hc_lo, m - 1)
                    for e in range(4 * c, min(4 * c + 4, KH)):
                        w = min(P, HID - e * P)
                        ins = te.transpose(psT[0:w, m % 2, (e % 4) * P:(e % 4 + 1) * P],
                                           hc[:, i % 2, e * P:e * P + w], ident[:, :])
                    ins.then_inc(hc_T, 1)

            pe.wait_ge(loaded["gw"], 48)
            for t, j in TAIL:
                if j is None:
                    projection_step(t)
                else:
                    expert_step(t, j)


_INS = ["x", "cs", "wmod0", "wmod1", "wq", "bq", "wkv", "bk", "bv", "wo", "peT", "ident", "mask", "iota",
        "wr", "wg", "wu", "wd", "swg", "swu", "swd", "amp", "escale", "w1a", "b1a", "ropeC", "ropeS",
        "gw", "gb", "w1", "w3", "w2"]


def kernel(**inputs):
    import numpy as np
    import concourse.bacc as bacc
    from concourse.bass_utils import run_bass_kernel_spmd

    a = {k: np.asarray(v) for k, v in inputs.items()}
    f32 = np.float32
    S, E, D = 1024, 256, 128
    pos = np.arange(S, dtype=f32)[:, None]
    inv = np.exp(-(np.log(f32(10000.0)) * np.arange(0, D, 2, dtype=f32) / f32(D))).astype(f32)
    ang = (pos * inv).astype(f32)
    pe = np.zeros((S, D), f32)
    pe[:, 0::2], pe[:, 1::2] = np.sin(ang), np.cos(ang)
    inv1 = (f32(1.0) / f32(10000.0) ** (np.arange(0, 16, 2, dtype=f32) / f32(16))).astype(f32)
    fr = (pos * inv1).astype(f32)
    cos = np.repeat(np.cos(fr), 2, axis=1).reshape(8, 128, 16).transpose(1, 0, 2)
    sin = np.stack([-np.sin(fr), np.sin(fr)], -1).reshape(8, 128, 16).transpose(1, 0, 2)
    bkv = a["L0_attn_bkv"].reshape(4, 2, 128)
    d = {
        "x": a["L0_attn_x"].reshape(S, E),
        "cs": np.concatenate([a["L0_c"].reshape(2, 128), a["L1_c"].reshape(2, 128)]).T,
        "wmod0": a["L0_wmod"], "wmod1": a["L1_wmod"],
        "wq": a["L0_attn_wq"], "bq": a["L0_attn_bq"].reshape(16, 128).T,
        "wkv": a["L0_attn_wkv"], "bk": bkv[:, 0].T, "bv": bkv[:, 1].reshape(1, 512),
        "wo": a["L0_attn_wo"], "peT": pe.T, "ident": np.eye(128, dtype=f32),
        "mask": np.triu(np.full((128, 128), -1e30, f32), 1), "iota": np.arange(128, dtype=f32)[None],
        "wr": a["L0_ffn_w_router"], "wg": a["L0_ffn_w_gate"], "wu": a["L0_ffn_w_up"], "wd": a["L0_ffn_w_down"],
        "swg": a["L0_ffn_shared_w_gate"], "swu": a["L0_ffn_shared_w_up"], "swd": a["L0_ffn_shared_w_down"],
        "amp": a["L0_ffn_amplitudes"].reshape(128, 16), "escale": a["L0_ffn_expert_scale"].reshape(128, 1),
        "w1a": np.concatenate([a[f"L1_attn_W{n}"].T for n in "qkvo"], axis=1),
        "b1a": np.concatenate([a[f"L1_attn_b{n}"] for n in "qkvo"])[None],
        "ropeC": cos.reshape(128, 128), "ropeS": sin.reshape(128, 128),
        "gw": a["L1_ffn_gate_w"].T, "gb": a["L1_ffn_gate_b"].reshape(1, 8),
        "w1": np.concatenate([a["L1_ffn_w1"].reshape(1408, 256), a["L1_ffn_sw1"]]).T,
        "w3": np.concatenate([a["L1_ffn_w3"].reshape(1408, 256), a["L1_ffn_sw3"]]).T,
        "w2": np.concatenate([a["L1_ffn_w2"].transpose(0, 2, 1).reshape(1408, 256), a["L1_ffn_sw2"].T]),
    }
    nc = bacc.Bacc("TRN2", target_bir_lowering=False, num_devices=1)
    arrays, aps = {}, {}
    for name in _INS:
        v = np.ascontiguousarray(d[name])
        arrays[f"in_{name}"] = v
        aps[name] = nc.dram_tensor(f"in_{name}", v.shape, mybir.dt.from_np(v.dtype), kind="ExternalInput").ap()
    out = nc.dram_tensor("out", (S, E), F32, kind="ExternalOutput").ap()
    build_program(nc, aps, out)
    r = run_bass_kernel_spmd(nc, [arrays], core_ids=[0])
    return r.results[0]["out"].reshape(1, S, E)
```
